# Optimizing a Trainium2 kernel written in Bass

```python
import numpy as np
import jax
import jax.numpy as jnp

def _softmax(x, axis=-1):
    return jax.nn.softmax(x, axis=axis)

def _gelu(x):
    return jax.nn.gelu(x, approximate=True)

def _silu(x):
    return jax.nn.silu(x)

def _sigmoid(x):
    return jax.nn.sigmoid(x)

def _layernorm(x, axis=-1, eps=1e-05):
    m = jnp.mean(x, axis=axis, keepdims=True)
    v = jnp.var(x, axis=axis, keepdims=True)
    return (x - m) / jnp.sqrt(v + eps)

def _scatter_add(tgt, idx, src, axis=0):
    return tgt.at[idx].add(src)

def _segment_sum(src, seg, n):
    return jax.ops.segment_sum(src, seg, n)
kernel_name = 'mk_macaron_d1_jaxref_r4_1c845a'

def setup_inputs(seed: int=0):
    np.random.seed(seed)
    _w = jnp.asarray

    def _L0_attn_setup():
        import jax, jax.numpy as jnp
        import numpy as np
        B, T, D = (2, 512, 512)
        H = 8
        KEY_DIM, VAL_DIM = (256, 512)
        HK, HV = (KEY_DIM // H, VAL_DIM // H)
        LOW_RANK = 16
        GATE_NORM = 16.0
        CHUNK = 64
        HIDDEN = (D * 4 * 2 // 3 + 63) // 64 * 64
        EPS = 1e-06

        def rmsnorm(x, w):
            return x * jax.lax.rsqrt(jnp.mean(x * x, axis=-1, keepdims=True) + EPS) * w

        def _gla(h, wq, wk, wv, gk_w1, gk_w2, gk_b, wg, gnorm_w, wo):
            Bb, Tt, _ = h.shape
            nc = Tt // CHUNK

            def split(t, hd):
                t = t.reshape(Bb, nc, CHUNK, H, hd)
                return jnp.transpose(t, (1, 0, 3, 2, 4))
            q = split(h @ wq, HK) * HK ** (-0.5)
            k = split(h @ wk, HK)
            v = split(h @ wv, HV)
            g = split(jax.nn.log_sigmoid(h @ gk_w1 @ gk_w2 + gk_b) / GATE_NORM, HK)
            mask = jnp.tril(jnp.ones((CHUNK, CHUNK), jnp.float32))

            def step(S, inp):
                qc, kc, vc, gc = inp
                b = jnp.cumsum(gc, axis=-2)
                qe = qc * jnp.exp(b)
                A = jnp.einsum('bhik,bhjk->bhij', qe, kc * jnp.exp(-b)) * mask
                o = jnp.einsum('bhck,bhkv->bhcv', qe, S) + jnp.einsum('bhij,bhjv->bhiv', A, vc)
                bl = b[:, :, -1:, :]
                S = jnp.exp(bl[:, :, 0, :])[..., None] * S + jnp.einsum('bhck,bhcv->bhkv', kc * jnp.exp(bl - b), vc)
                return (S, o)
            S0 = jnp.zeros((Bb, H, HK, HV), h.dtype)
            _, o = jax.lax.scan(step, S0, (q, k, v, g))
            o = jnp.transpose(o, (1, 0, 3, 2, 4)).reshape(Bb, Tt, H, HV)
            gate = (h @ wg).reshape(Bb, Tt, H, HV)
            o = rmsnorm(o, gnorm_w) * gate * jax.nn.sigmoid(gate)
            return o.reshape(Bb, Tt, VAL_DIM) @ wo
        key = jax.random.key(seed)
        ks = jax.random.split(key, 12)
        w = lambda k, s: jax.random.normal(k, s, jnp.float32) * 0.02
        return {'x': jax.random.normal(ks[0], (B, T, D), jnp.float32), 'norm1_w': jnp.ones((D,), jnp.float32), 'wq': w(ks[1], (D, KEY_DIM)), 'wk': w(ks[2], (D, KEY_DIM)), 'wv': w(ks[3], (D, VAL_DIM)), 'gk_w1': w(ks[4], (D, LOW_RANK)), 'gk_w2': w(ks[5], (LOW_RANK, KEY_DIM)), 'gk_b': jnp.zeros((KEY_DIM,), jnp.float32), 'wg': w(ks[6], (D, VAL_DIM)), 'gnorm_w': jnp.ones((HV,), jnp.float32), 'wo': w(ks[7], (VAL_DIM, D)), 'ffn_norm_w': jnp.ones((D,), jnp.float32), 'w_gate': w(ks[8], (D, HIDDEN)), 'w_up': w(ks[9], (D, HIDDEN)), 'w_down': w(ks[10], (HIDDEN, D))}
    _L0_attn_in = _L0_attn_setup()

    def _L0_ffn_setup():
        import jax, jax.numpy as jnp
        import numpy as np
        TOP_K = 2
        key = jax.random.key(seed)
        ks = jax.random.split(key, 7)
        B, S, H = (2, 512, 512)
        E, A, NS = (8, 64, 4096)
        x = jax.random.normal(ks[0], (B, S, H), jnp.float32)
        gate_w = jax.random.normal(ks[1], (E, H), jnp.float32) * 0.01
        W = jax.random.normal(ks[2], (H, H), jnp.float32) * 0.02
        atoms = jax.random.normal(ks[3], (A, NS), jnp.float32) * 0.02
        expert_atom_weights = jax.random.normal(ks[4], (E, A), jnp.float32) * 0.1
        importance = jax.random.normal(ks[5], (E, NS), jnp.float32) * 0.1
        mask_idx = jax.random.randint(ks[6], (NS,), 0, H * H, jnp.int32)
        return dict(x=x, gate_w=gate_w, W=W, atoms=atoms, expert_atom_weights=expert_atom_weights, importance=importance, mask_idx=mask_idx)
    _L0_ffn_in = _L0_ffn_setup()
    _d = {'L0_attn_x': _L0_attn_in['x'], 'L0_attn_norm1_w': _L0_attn_in['norm1_w'], 'L0_attn_wq': _L0_attn_in['wq'], 'L0_attn_wk': _L0_attn_in['wk'], 'L0_attn_wv': _L0_attn_in['wv'], 'L0_attn_gk_w1': _L0_attn_in['gk_w1'], 'L0_attn_gk_w2': _L0_attn_in['gk_w2'], 'L0_attn_gk_b': _L0_attn_in['gk_b'], 'L0_attn_wg': _L0_attn_in['wg'], 'L0_attn_gnorm_w': _L0_attn_in['gnorm_w'], 'L0_attn_wo': _L0_attn_in['wo'], 'L0_attn_ffn_norm_w': _L0_attn_in['ffn_norm_w'], 'L0_attn_w_gate': _L0_attn_in['w_gate'], 'L0_attn_w_up': _L0_attn_in['w_up'], 'L0_attn_w_down': _L0_attn_in['w_down'], 'L0_ffn_gate_w': _L0_ffn_in['gate_w'], 'L0_ffn_W': _L0_ffn_in['W'], 'L0_ffn_atoms': _L0_ffn_in['atoms'], 'L0_ffn_expert_atom_weights': _L0_ffn_in['expert_atom_weights'], 'L0_ffn_importance': _L0_ffn_in['importance'], 'L0_ffn_mask_idx': _L0_ffn_in['mask_idx']}
    _x0 = _d['L0_attn_x']
    _d['L0_attn_x'] = jax.random.normal(jax.random.fold_in(jax.random.key(seed), 1), (4, 1024, 512), dtype=_x0.dtype)
    del _x0
    return _d

def reference(L0_attn_x, L0_attn_norm1_w, L0_attn_wq, L0_attn_wk, L0_attn_wv, L0_attn_gk_w1, L0_attn_gk_w2, L0_attn_gk_b, L0_attn_wg, L0_attn_gnorm_w, L0_attn_wo, L0_attn_ffn_norm_w, L0_attn_w_gate, L0_attn_w_up, L0_attn_w_down, L0_ffn_gate_w, L0_ffn_W, L0_ffn_atoms, L0_ffn_expert_atom_weights, L0_ffn_importance, L0_ffn_mask_idx):

    def _L0_attn_ref(x, norm1_w, wq, wk, wv, gk_w1, gk_w2, gk_b, wg, gnorm_w, wo, ffn_norm_w, w_gate, w_up, w_down):
        import jax, jax.numpy as jnp
        import numpy as np
        B, T, D = (2, 512, 512)
        H = 8
        KEY_DIM, VAL_DIM = (256, 512)
        HK, HV = (KEY_DIM // H, VAL_DIM // H)
        LOW_RANK = 16
        GATE_NORM = 16.0
        CHUNK = 64
        HIDDEN = (D * 4 * 2 // 3 + 63) // 64 * 64
        EPS = 1e-06

        def rmsnorm(x, w):
            return x * jax.lax.rsqrt(jnp.mean(x * x, axis=-1, keepdims=True) + EPS) * w

        def _gla(h, wq, wk, wv, gk_w1, gk_w2, gk_b, wg, gnorm_w, wo):
            Bb, Tt, _ = h.shape
            nc = Tt // CHUNK

            def split(t, hd):
                t = t.reshape(Bb, nc, CHUNK, H, hd)
                return jnp.transpose(t, (1, 0, 3, 2, 4))
            q = split(h @ wq, HK) * HK ** (-0.5)
            k = split(h @ wk, HK)
            v = split(h @ wv, HV)
            g = split(jax.nn.log_sigmoid(h @ gk_w1 @ gk_w2 + gk_b) / GATE_NORM, HK)
            mask = jnp.tril(jnp.ones((CHUNK, CHUNK), jnp.float32))

            def step(S, inp):
                qc, kc, vc, gc = inp
                b = jnp.cumsum(gc, axis=-2)
                qe = qc * jnp.exp(b)
                A = jnp.einsum('bhik,bhjk->bhij', qe, kc * jnp.exp(-b)) * mask
                o = jnp.einsum('bhck,bhkv->bhcv', qe, S) + jnp.einsum('bhij,bhjv->bhiv', A, vc)
                bl = b[:, :, -1:, :]
                S = jnp.exp(bl[:, :, 0, :])[..., None] * S + jnp.einsum('bhck,bhcv->bhkv', kc * jnp.exp(bl - b), vc)
                return (S, o)
            S0 = jnp.zeros((Bb, H, HK, HV), h.dtype)
            _, o = jax.lax.scan(step, S0, (q, k, v, g))
            o = jnp.transpose(o, (1, 0, 3, 2, 4)).reshape(Bb, Tt, H, HV)
            gate = (h @ wg).reshape(Bb, Tt, H, HV)
            o = rmsnorm(o, gnorm_w) * gate * jax.nn.sigmoid(gate)
            return o.reshape(Bb, Tt, VAL_DIM) @ wo
        h = rmsnorm(x, norm1_w)
        x = x + _gla(h, wq, wk, wv, gk_w1, gk_w2, gk_b, wg, gnorm_w, wo)
        h2 = rmsnorm(x, ffn_norm_w)
        ffn = jax.nn.silu(h2 @ w_gate) * (h2 @ w_up) @ w_down
        return x + ffn

    def _L0_ffn_ref(x, gate_w, W, atoms, expert_atom_weights, importance, mask_idx):
        import jax, jax.numpy as jnp
        import numpy as np
        TOP_K = 2
        B, S, H = x.shape
        xt = x.reshape(-1, H)
        logits = jnp.clip(xt @ gate_w.T, -50.0, 50.0)
        top_w, top_idx = jax.lax.top_k(logits, TOP_K)
        rw = jax.nn.softmax(top_w, axis=-1)
        deltas = jax.nn.softmax(expert_atom_weights, axis=-1) @ atoms
        weighted = deltas * jax.nn.sigmoid(importance)
        rows = mask_idx // H
        cols = mask_idx % H
        vals = jnp.einsum('tk,tks->ts', rw, weighted[top_idx])
        xg = xt[:, cols]
        contrib = jax.ops.segment_sum((xg * vals).T, rows, num_segments=H)
        out = xt @ W.T + contrib.T
        return out.reshape(B, S, H)
    x = L0_attn_x
    x = x + 0.5 * _L0_ffn_ref(_layernorm(x, axis=-1), L0_ffn_gate_w, L0_ffn_W, L0_ffn_atoms, L0_ffn_expert_atom_weights, L0_ffn_importance, L0_ffn_mask_idx)
    x = x + _L0_attn_ref(_layernorm(x, axis=-1), L0_attn_norm1_w, L0_attn_wq, L0_attn_wk, L0_attn_wv, L0_attn_gk_w1, L0_attn_gk_w2, L0_attn_gk_b, L0_attn_wg, L0_attn_gnorm_w, L0_attn_wo, L0_attn_ffn_norm_w, L0_attn_w_gate, L0_attn_w_up, L0_attn_w_down)
    x = x + 0.5 * _L0_ffn_ref(_layernorm(x, axis=-1), L0_ffn_gate_w, L0_ffn_W, L0_ffn_atoms, L0_ffn_expert_atom_weights, L0_ffn_importance, L0_ffn_mask_idx)
    return x

_drawn_inputs = setup_inputs


def setup_inputs(seed=0):
    import zlib

    import numpy as np

    out = dict(_drawn_inputs(seed))
    spreads = {'L0_attn_norm1_w': (1.0, 0.6),
     'L0_attn_gk_b': (0.0, 2.0),
     'L0_attn_gnorm_w': (1.0, 0.6),
     'L0_attn_ffn_norm_w': (1.0, 0.6)}
    factors = {'L0_attn_gk_w1': 8.0,
     'L0_attn_gk_w2': 8.0,
     'L0_ffn_gate_w': 28.665,
     'L0_ffn_atoms': 8.0,
     'L0_ffn_expert_atom_weights': 25.445,
     'L0_ffn_importance': 56.199}
    for name, (base, spread) in spreads.items():
        noise = np.random.default_rng([zlib.crc32(name.encode()), seed]).standard_normal(out[name].shape)
        drawn = base * np.exp(spread * noise) if base else spread * noise
        out[name] = jnp.asarray(drawn.astype(out[name].dtype))
    for name, factor in factors.items():
        out[name] = (out[name] * factor).astype(out[name].dtype)
    return out
```

```python
from contextlib import ExitStack

import concourse.bass as bass
from concourse import mybir

F32 = mybir.dt.float32
F32R = mybir.dt.float32r
BF16 = mybir.dt.bfloat16
I32 = mybir.dt.int32
ALU = mybir.AluOpType
ACT = mybir.ActivationFunctionType
AX = mybir.AxisListType

P = 128
D = 512
KC = D // P
B, T = 4, 1024
TOK = B * T
NT = TOK // P
E = 8
A = 64
NS = 4096
NB = NS // P
PLACES = D * D
REGION = TOK + P
BLOCKS = (2 * TOK + E * (P - 1)) // P + 1
H, HK, HV = 8, 32, 64
KEY, VAL, LOW = H * HK, H * HV, 16
CHUNK = 64
HID = 1408
NF = HID // P
TILES_B = T // P
LN_EPS, RMS_EPS = 1e-5, 1e-6
assert BLOCKS % 2 == 0


class Phase:

    def __init__(self, nc, name, recycle=False):
        self.nc, self.name, self.recycle, self.sems = nc, name, recycle, []
        self.ctx = ExitStack()

    def __enter__(self):
        self.ctx.__enter__()
        return self

    def __exit__(self, *exc):
        self.ctx.__exit__(*exc)
        if self.recycle and exc[0] is None:
            self.nc.clear_and_free_semaphores(self.sems)
            self.nc.all_engine_barrier()

    def sb(self, name, shape, dt=F32):
        return self.ctx.enter_context(self.nc.sbuf_tensor(f"{self.name}_{name}", shape, dt))

    def ps(self, name, shape, dt=F32):
        return self.ctx.enter_context(self.nc.psum_tensor(f"{self.name}_{name}", shape, dt))

    def sem(self, name):
        self.sems.append(self.nc.alloc_semaphore(f"{self.name}_{name}"))
        return self.sems[-1]


class Steps:

    def __init__(self, eng, sem, base=0):
        self.eng, self.sem, self.base, self.n = eng, sem, base, 0

    def did(self, ins):
        ins.then_inc(self.sem, 1)
        self.n += 1

    def settle(self):
        self.eng.wait_ge(self.sem, self.base + self.n)

    def chain(self, ins):
        self.did(ins)
        self.settle()


def bc(ap, axis, n):
    a = ap.unsqueeze(axis)
    shape = list(a.shape)
    shape[axis] = n
    return a.broadcast_to(shape)


def constants(nc, sb):
    c = {}
    c["ident"] = sb("ident", [P, P])
    c["before"] = sb("before", [P, P])
    c["ones"] = sb("ones", [P, P])
    with Phase(nc, "const") as ph:
        made = ph.sem("made")
        with nc.Block() as block:
            @block.gpsimd
            def _(pool):
                pool.memset(c["ident"][:], 0.0).then_inc(made, 1)
                pool.memset(c["ones"][:], 1.0).then_inc(made, 1)
                pool.wait_ge(made, 2)
                pool.affine_select(out=c["ident"][:], in_=c["ident"][:], compare_op=ALU.not_equal, fill=1.0,
                                   base=0, pattern=[[-1, P]], channel_multiplier=1)
                pool.affine_select(out=c["before"][:], in_=c["ones"][:], compare_op=ALU.is_gt, fill=0.0,
                                   base=0, pattern=[[1, P]], channel_multiplier=-1)
    return c


def sparse_places(nc, cst, atoms, eaw, importance, mask_idx, table):
    W3 = 3 * E
    ZB = NB * W3
    PB = 8
    with Phase(nc, "sp") as ph:
        sb, sem = ph.sb, ph.sem
        eaw_sb = sb("eaw", [E, A])
        atoms_sb = sb("atoms", [A, NS])
        imp = sb("imp", [E, NS])
        idx_row = sb("idx_row", [P, NS], I32)
        idx_col = sb("idx_col", [P, NB], I32)
        row_f = sb("row_f", [P, NS])
        col_f = sb("col_f", [P, NB])
        zero = sb("zero", [P, 4096])
        stat = sb("stat", [E, 4])
        prob = sb("prob", [E, A])
        probT = sb("probT", [A, E])
        impT = sb("impT", [P, NB * E])
        val = sb("val", [P, NB * E])
        val2 = sb("val2", [P, NB * E])
        parts = sb("parts", [P, (NB - 1) * W3 + 2 * (ZB + (NB - 1) * W3)], BF16)
        zb16 = sb("zb16", [P, 512], BF16)
        before = sb("before16", [P, P], BF16)
        ones16 = sb("ones16", [P, 2], BF16)
        eq = [sb(f"eq{u}", [P, NS], BF16) for u in range(2)]
        eqd = [sb(f"eqd{u}", [P, P], BF16) for u in range(2)]
        acc = sb("acc", [P, NB, 2 * W3])
        total = sb("total", [P, NB, E])
        earlier = sb("earlier", [P, NB])
        place_i = sb("place_i", [P, NB], I32)
        place_j = sb("place_j", [P, NB], I32)
        place_f = sb("place_f", [P, NB])
        spare_f = sb("spare_f", [P, NB])
        ps_eq = [ph.ps(f"ps_eq{n}", [P, PB, 2 * W3]) for n in range(NB // PB)]
        ps_imp = ph.ps("ps_imp", [P, 512])
        ps_dl = ph.ps("ps_dl", [P, 512])
        ps_dg = ph.ps("ps_dg", [P, 512])
        ps_p = ph.ps("ps_p", [P, 512])
        loaded, vec, act_s, ten, poo = sem("loaded"), sem("vec"), sem("act"), sem("ten"), sem("pool")
        eq_ready, eq_used, zeroed, stored = sem("eq_ready"), sem("eq_used"), sem("zeroed"), sem("stored")
        final = sem("final")

        with nc.Block() as block:
            @block.sync
            def _(sp):
                sp.dma_start(eaw_sb[:], eaw).then_inc(loaded, 16)
                sp.dma_start(idx_row[:], mask_idx.rearrange("(o s) -> o s", o=1).broadcast_to([P, NS])).then_inc(loaded, 16)
                sp.dma_start(idx_col[:], mask_idx.rearrange("(b p) -> p b", p=P),
                             allow_slow_non_contiguous=True).then_inc(loaded, 16)
                sp.dma_start(imp[:], importance).then_inc(loaded, 16)
                sp.dma_start(atoms_sb[:], atoms).then_inc(loaded, 16)
                sp.wait_ge(vec, 1)
                flat = table[0:PLACES, :].rearrange("(n p k) e -> n p (k e)", n=4, p=P)
                for n in range(4):
                    sp.dma_start(flat[n], zero[:]).then_inc(zeroed, 16)

            @block.gpsimd
            def _(pool):
                st = Steps(pool, poo)
                st.did(pool.iota(spare_f[:], pattern=[[P, NB]], base=PLACES, channel_multiplier=1,
                                 allow_small_or_imprecise_dtypes=True))
                pool.wait_ge(zeroed, 64)
                pool.wait_ge(final, 1)
                for b in range(NB):
                    pool.indirect_dma_start(table, bass.IndirectOffsetOnAxis(ap=place_i[:, b:b + 1], axis=0),
                                            total[:, b, :], None).then_inc(stored, 16)
                pool.wait_ge(stored, 16 * NB)

            @block.scalar
            def _(act):
                act.wait_ge(vec, 5)
                act.activation(prob[:], eaw_sb[:], ACT.Exp, bias=stat[:, 0:1], accum_out=stat[:, 1:2]).then_inc(act_s, 1)
                act.wait_ge(loaded, 80)
                act.activation(imp[:], imp[:], ACT.Sigmoid).then_inc(act_s, 1)

            @block.vector
            def _(dve):
                st = Steps(dve, vec)
                st.did(dve.memset(zero[:], 0.0))
                st.did(dve.memset(parts[:], 0.0))
                st.did(dve.memset(zb16[:], 0.0))
                st.did(dve.memset(ones16[:], 1.0))
                dve.wait_ge(loaded, 80)
                dve.tensor_reduce(stat[:, 0:1], eaw_sb[:], AX.X, ALU.max, negate=True).then_inc(vec, 1)
                st.n += 1
                st.did(dve.tensor_copy(before[:], cst["before"][:]))
                st.settle()
                ones_ramp = parts[:, ZB:ZB + (NB - 1) * W3].rearrange("p (m w) -> p m w", w=W3)
                st.did(dve.memset(ones_ramp[:, :, 0:1], 1.0))
                st.did(dve.tensor_copy(row_f[:], idx_row[:]))
                st.did(dve.tensor_copy(col_f[:], idx_col[:]))
                dve.wait_ge(act_s, 1)
                st.chain(dve.reciprocal(stat[:, 2:3], stat[:, 1:2]))
                st.did(dve.tensor_scalar(prob[:], prob[:], stat[:, 2:3], None, ALU.mult))
                dve.wait_ge(ten, 1)
                st.did(dve.tensor_copy(probT[:], ps_p[0:A, 0:E]))
                dve.wait_ge(ten, 2)
                st.did(dve.tensor_copy(impT[:], ps_imp[:, 0:NB * E]))
                dve.wait_ge(ten, 3)
                st.settle()
                st.chain(dve.tensor_tensor(val[:], ps_dl[:, 0:NB * E], impT[:], ALU.mult))
                pv = parts[:, 0:ZB].rearrange("p (b w) -> p b w", w=W3)
                vv = val[:].rearrange("p (b e) -> p b e", e=E)
                vv2 = val2[:].rearrange("p (b e) -> p b e", e=E)
                st.chain(dve.tensor_copy(pv[:, :, 0:E], vv))
                st.chain(dve.tensor_tensor(vv2, vv, pv[:, :, 0:E], ALU.subtract))
                st.chain(dve.tensor_copy(pv[:, :, E:2 * E], vv2))
                st.chain(dve.tensor_tensor(vv, vv2, pv[:, :, E:2 * E], ALU.subtract))
                st.chain(dve.tensor_copy(pv[:, :, 2 * E:3 * E], vv))
                dve.sem_inc(eq_used, 2)
                with dve.Fori(0, NB // 2) as pair:
                    for u in range(2):
                        dve.wait_ge(eq_used, pair * 2 + u + 1)
                        dve.tensor_scalar(eq[u][:], row_f[:], col_f[:, bass.ds(pair * 2 + u, 1)], None, ALU.is_equal)
                        dve.scalar_tensor_tensor(out=eqd[u][:], in0=row_f[:, bass.ds((pair * 2 + u) * P, P)],
                                                 scalar=col_f[:, bass.ds(pair * 2 + u, 1)], in1=before[:],
                                                 op0=ALU.is_equal, op1=ALU.mult).then_inc(eq_ready, 1)
                st.did(dve.tensor_scalar(place_i[:], idx_col[:], D - 1, 9, ALU.bitwise_and, ALU.logical_shift_left))
                st.chain(dve.tensor_scalar(place_j[:], idx_col[:], 9, None, ALU.logical_shift_right))
                st.chain(dve.tensor_tensor(place_i[:], place_i[:], place_j[:], ALU.bitwise_or))
                st.chain(dve.tensor_copy(place_f[:], place_i[:]))
                dve.wait_ge(poo, 1)
                st.chain(dve.tensor_tensor(place_f[:], place_f[:], spare_f[:], ALU.subtract))
                dve.wait_ge(ten, 4)
                for n in range(NB // PB):
                    st.did(dve.tensor_copy(acc[:, n * PB:(n + 1) * PB, :], ps_eq[n][:]))
                st.did(dve.tensor_copy(earlier[:], ps_dg[:, 0:NB]))
                st.settle()
                st.did(dve.tensor_tensor(earlier[:].unsqueeze(2), earlier[:].unsqueeze(2), acc[:, :, W3:W3 + 1], ALU.add))
                st.chain(dve.tensor_tensor(total[:], acc[:, :, 0:E], acc[:, :, E:2 * E], ALU.add))
                st.did(dve.tensor_tensor(total[:], total[:], acc[:, :, 2 * E:3 * E], ALU.add))
                st.chain(dve.scalar_tensor_tensor(out=place_f[:], in0=earlier[:], scalar=0.5, in1=place_f[:],
                                                  op0=ALU.is_lt, op1=ALU.mult))
                st.chain(dve.tensor_tensor(place_f[:], place_f[:], spare_f[:], ALU.add))
                dve.tensor_copy(place_i[:], place_f[:]).then_inc(final, 1)

            @block.tensor
            def _(pe):
                pe.wait_ge(vec, 11)
                pe.transpose(ps_p[0:A, 0:E], prob[:], cst["ident"][0:E, 0:E]).then_inc(ten, 1)
                pe.wait_ge(act_s, 2)
                for b in range(NB):
                    t = pe.transpose(ps_imp[:, b * E:(b + 1) * E], imp[:, b * P:(b + 1) * P], cst["ident"][0:E, 0:E])
                t.then_inc(ten, 1)
                pe.wait_ge(vec, 12)
                for b in range(NB):
                    m = pe.matmul(ps_dl[:, b * E:(b + 1) * E], atoms_sb[:, b * P:(b + 1) * P], probT[:],
                                  start=True, stop=True)
                m.then_inc(ten, 1)
                for n in range(NB // PB):
                    pe.matmul(ps_eq[n][:], zb16[:, 0:P], zb16[:, 0:PB * 2 * W3], start=True, stop=False,
                              skip_group_check=True)
                with pe.Fori(0, NB // 2) as pair:
                    for u in range(2):
                        pe.wait_ge(eq_ready, pair * 2 + u + 1)
                        for b in range(NB):
                            dist = ZB + (NB - 1 - b) * W3
                            rhs = parts[:, bass.ds((pair * 2 + u) * W3, 2 * dist)].rearrange("p (two d) -> p two d", two=2)
                            pe.matmul(ps_eq[b // PB][:, b % PB, :], eq[u][:, b * P:(b + 1) * P], rhs[:, :, 0:W3],
                                      start=False, stop=False, skip_group_check=True)
                        pe.matmul(ps_dg[:, bass.ds(pair * 2 + u, 1)], eqd[u][:], ones16[:, 0:1],
                                  start=True, stop=True).then_inc(eq_used, 1)
                for n in range(NB // PB):
                    m = pe.matmul(ps_eq[n][:], zb16[:, 0:P], zb16[:, 0:PB * 2 * W3], start=False, stop=True,
                                  skip_group_check=True)
                m.then_inc(ten, 1)


def router(nc, cst, name, x, gate_w, gate, row_of, tile_tab, dispatched):
    JE = NT * E
    with Phase(nc, name) as ph:
        sb, sem = ph.sb, ph.sem
        xn = sb("xn", [P, NT, D])
        cur = [sb(f"cur{u}", [P, D]) for u in range(2)]
        xT = [sb(f"xT{u}", [P, KC, P]) for u in range(2)]
        gw = sb("gw", [E, D])
        gwT = sb("gwT", [P, KC, E])
        bn = sb("bn", [P, NT, 6])
        mv = sb("mv", [P, NT, 2])
        rstd = sb("rstd", [P, NT])
        power = sb("power", [P, NT])
        eps = sb("eps", [P, NT])
        lg = sb("lg", [P, NT, E])
        rev = sb("rev", [P, NT, E])
        cand = sb("cand", [P, NT, E])
        oh = [sb(f"oh{k}", [P, NT, E]) for k in range(2)]
        both = sb("both", [P, NT, E])
        top = [sb(f"top{k}", [P, NT]) for k in range(2)]
        best = sb("best", [P, NT])
        w1 = sb("w1", [P, NT])
        keep = sb("keep", [P, E, NT])
        tot = sb("tot", [P, E, NT])
        upto = sb("upto", [P, E, NT])
        rank = sb("rank", [P, E, NT])
        place = sb("place", [P, E, NT])
        region = sb("region", [P, E, NT])
        prod = sb("prod", [P, E, NT])
        row_f = sb("row_f", [P, NT])
        sent = sb("sent", [P, 2, NT], I32)
        count_i = sb("count_i", [P, E], I32)
        blocks = sb("blocks", [P, E])
        blocks_to = sb("blocks_to", [P, E])
        before_e = sb("before_e", [P, E])
        one_e = sb("one_e", [P, E])
        pad = sb("pad", [P, E])
        pad_off = sb("pad_off", [P, E])
        pad_i = sb("pad_i", [P, E], I32)
        zrow = sb("zrow", [P, D])
        blk = sb("blk", [P, BLOCKS])
        over = sb("over", [P, E - 1, BLOCKS])
        over2 = sb("over2", [P, E - 1, BLOCKS])
        te = sb("te", [P, BLOCKS])
        tb = sb("tb", [P, BLOCKS])
        ps_T = [ph.ps(f"ps_T{u}", [P, KC, P]) for u in range(2)]
        ps_l = ph.ps("ps_l", [P, NT, E])
        ps_in = ph.ps("ps_in", [P, NT, E])
        ps_tot = ph.ps("ps_tot", [P, NT, E])
        G = 4
        loaded = [sem(f"loaded{g}") for g in range(NT // G)]
        stats, mean_in, poo, vec = sem("stats"), sem("mean_in"), sem("pool"), sem("vec")
        normed, turned, copied, scored, gone = sem("normed"), sem("turned"), sem("copied"), sem("scored"), sem("gone")
        gw_in, gw_T, ten, act_s, lnv, final = sem("gw_in"), sem("gw_T"), sem("ten"), sem("act"), sem("lnv"), sem("final")
        cur_free = sem("cur_free")
        with nc.Block() as block:
            @block.sync
            def _(sp):
                src = x.rearrange("(g j p) d -> g p j d", g=NT // G, p=P)
                sp.dma_start(gw[:], gate_w).then_inc(gw_in, 16)
                for g in range(NT // G):
                    sp.dma_start(xn[:, g * G:(g + 1) * G, :], src[g]).then_inc(loaded[g], 16)

            @block.gpsimd
            def _(pool):
                st = Steps(pool, poo)
                st.did(pool.memset(power[:], -0.5))
                st.did(pool.memset(eps[:], LN_EPS))
                st.did(pool.iota(rev[:], pattern=[[0, NT], [-1, E]], base=E, channel_multiplier=0,
                                 allow_small_or_imprecise_dtypes=True))
                st.did(pool.iota(region[:], pattern=[[REGION, E], [0, NT]], base=0, channel_multiplier=0,
                                 allow_small_or_imprecise_dtypes=True))
                st.did(pool.iota(pad_off[:], pattern=[[REGION, E]], base=0, channel_multiplier=1,
                                 allow_small_or_imprecise_dtypes=True))
                st.did(pool.iota(blk[:], pattern=[[1, BLOCKS]], base=0, channel_multiplier=0,
                                 allow_small_or_imprecise_dtypes=True))
                st.did(pool.memset(zrow[:], 0.0))
                pool.wait_ge(stats, NT)
                st.settle()
                st.chain(pool.tensor_tensor(rstd[:], mv[:, :, 1], eps[:], ALU.add))
                st.did(pool.tensor_tensor(rstd[:], rstd[:], power[:], ALU.pow))
                pool.wait_ge(final, 1)
                for j in range(NT):
                    for k in range(2):
                        pool.indirect_dma_start(dispatched, bass.IndirectOffsetOnAxis(ap=sent[:, k, j:j + 1], axis=0),
                                                xn[:, j, :], None).then_inc(gone, 16)
                for e in range(E):
                    pool.indirect_dma_start(dispatched, bass.IndirectOffsetOnAxis(ap=pad_i[:, e:e + 1], axis=0),
                                            zrow[:], None).then_inc(gone, 16)
                pool.wait_ge(gone, 16 * (2 * NT + E))

            @block.vector
            def _(dve):
                for g in range(NT // G):
                    dve.wait_ge(loaded[g], 16)
                    for j in range(g * G, (g + 1) * G):
                        dve.bn_stats(bn[:, j, :], xn[:, j, :]).then_inc(mean_in, 1)
                dve.wait_ge(mean_in, NT)
                for j in range(NT):
                    dve.bn_aggr(mv[:, j, :], bn[:, j, :]).then_inc(stats, 1)
                dve.wait_ge(poo, 9)
                dve.sem_inc(cur_free, 2)
                with dve.Fori(0, NT // 2) as pair:
                    for u in range(2):
                        j = pair * 2 + u
                        for src, dst in ((xn[:, bass.ds(j, 1), :], cur[u][:].unsqueeze(1)),):
                            dve.wait_ge(cur_free, j + 1)
                            dve.tensor_scalar(dst, src, mv[:, bass.ds(j, 1), 0:1], rstd[:, bass.ds(j, 1)],
                                              ALU.subtract, ALU.mult).then_inc(normed, 1)
                            dve.tensor_scalar(src, src, mv[:, bass.ds(j, 1), 0:1], rstd[:, bass.ds(j, 1)],
                                              ALU.subtract, ALU.mult).then_inc(lnv, 1)
                st = Steps(dve, vec)
                dve.wait_ge(scored, NT)
                st.chain(dve.tensor_scalar(lg[:], ps_l[:], 50.0, -50.0, ALU.min, ALU.max))
                for k in range(2):
                    st.chain(dve.tensor_reduce(top[k][:], lg[:], AX.X, ALU.max))
                    st.chain(dve.tensor_tensor(cand[:], lg[:], bc(top[k][:], 2, E), ALU.is_equal))
                    st.chain(dve.tensor_tensor(cand[:], cand[:], rev[:], ALU.mult))
                    st.chain(dve.tensor_reduce(best[:], cand[:], AX.X, ALU.max))
                    st.chain(dve.tensor_tensor(oh[k][:], cand[:], bc(best[:], 2, E), ALU.is_equal))
                    if k == 0:
                        st.chain(dve.scalar_tensor_tensor(out=lg[:], in0=oh[0][:], scalar=-1000.0, in1=lg[:],
                                                          op0=ALU.mult, op1=ALU.add))
                st.did(dve.tensor_tensor(both[:], oh[0][:], oh[1][:], ALU.add))
                assert st.n == 13
                st.did(dve.tensor_tensor(top[1][:], top[1][:], top[0][:], ALU.subtract))
                st.did(dve.memset(keep[:], 1.0))
                st.did(dve.memset(one_e[:], 1.0))
                st.settle()
                st.did(dve.memset(keep[:, :, 0:1], 0.0))
                dve.wait_ge(act_s, 1)
                st.chain(dve.tensor_scalar(w1[:], best[:], 1.0, None, ALU.add))
                st.chain(dve.reciprocal(w1[:], w1[:]))
                st.did(dve.tensor_scalar(gate[:, 0, :], w1[:], 0.5, None, ALU.mult))
                st.chain(dve.tensor_tensor(gate[:, 1, :], w1[:], best[:], ALU.mult))
                st.did(dve.tensor_scalar(gate[:, 1, :], gate[:, 1, :], 0.5, None, ALU.mult))
                dve.wait_ge(ten, 2)
                st.chain(dve.tensor_copy(tot[:].rearrange("p e j -> p j e"), ps_tot[:]))
                flat = lambda t: t[:].rearrange("p e j -> p (e j)")
                st.chain(dve.tensor_tensor_scan(flat(upto), flat(keep), flat(tot), 0.0, ALU.mult, ALU.add))
                st.chain(dve.tensor_tensor(rank[:], upto[:], tot[:], ALU.subtract))
                st.chain(dve.tensor_tensor(rank[:], ps_in[:].rearrange("p j e -> p e j"), rank[:], ALU.add))
                st.did(dve.tensor_tensor(place[:], rank[:], region[:], ALU.add))
                st.chain(dve.tensor_scalar(count_i[:], upto[:, :, NT - 1], float(P - 1), None, ALU.add))
                st.chain(dve.tensor_scalar(count_i[:], count_i[:], 7, None, ALU.logical_shift_right))
                st.did(dve.tensor_tensor(pad[:], upto[:, :, NT - 1], pad_off[:], ALU.add))
                st.chain(dve.tensor_copy(blocks[:], count_i[:]))
                st.did(dve.tensor_copy(pad_i[:], pad[:]))
                st.chain(dve.tensor_tensor_scan(blocks_to[:], one_e[:], blocks[:], 0.0, ALU.mult, ALU.add))
                st.chain(dve.tensor_tensor(before_e[:], blocks_to[:], blocks[:], ALU.subtract))
                for k in range(2):
                    o = oh[k][:].rearrange("p j e -> p e j")
                    st.chain(dve.tensor_tensor(prod[:], place[:], o, ALU.mult))
                    st.chain(dve.tensor_reduce(row_f[:], prod[:].rearrange("p e j -> p j e"), AX.X, ALU.add))
                    st.chain(dve.tensor_copy(sent[:, k, :], row_f[:]))
                dve.nop().then_inc(final, 1)
                st.chain(dve.scalar_tensor_tensor(out=rank[:], in0=bc(before_e[:], 2, NT), scalar=float(P),
                                                  in1=rank[:], op0=ALU.mult, op1=ALU.add))
                for k in range(2):
                    o = oh[k][:].rearrange("p j e -> p e j")
                    st.chain(dve.tensor_tensor(prod[:], rank[:], o, ALU.mult))
                    st.chain(dve.tensor_reduce(row_f[:], prod[:].rearrange("p e j -> p j e"), AX.X, ALU.add))
                    st.chain(dve.tensor_copy(row_of[:, k, :], row_f[:]))
                bb = bc(blk[:], 1, E - 1)
                st.chain(dve.tensor_tensor(over[:], bb, bc(blocks_to[:, 0:E - 1], 2, BLOCKS), ALU.is_ge))
                st.did(dve.tensor_tensor(over2[:], over[:], bc(blocks[:, 0:E - 1], 2, BLOCKS), ALU.mult))
                st.chain(dve.tensor_reduce(te[:], over[:].rearrange("p e j -> p j e"), AX.X, ALU.add))
                st.chain(dve.tensor_reduce(tb[:], over2[:].rearrange("p e j -> p j e"), AX.X, ALU.add))
                st.did(dve.tensor_copy(tile_tab[:, 0, :], te[0:1, :]))
                st.chain(dve.tensor_tensor(tb[:], blk[:], tb[:], ALU.subtract))
                st.chain(dve.scalar_tensor_tensor(out=tb[:], in0=blk[:], scalar=blocks_to[:, E - 1:E], in1=tb[:],
                                                  op0=ALU.is_lt, op1=ALU.mult))
                st.did(dve.tensor_scalar(te[:], te[:], float(REGION), None, ALU.mult))
                st.chain(dve.tensor_scalar(tb[:], tb[:], float(P), None, ALU.mult))
                st.chain(dve.tensor_tensor(tb[:], tb[:], te[:], ALU.add))
                st.chain(dve.tensor_copy(tile_tab[:, 1, :], tb[0:1, :]))

            @block.tensor
            def _(pe):
                pe.wait_ge(gw_in, 16)
                for kc in range(KC):
                    m = pe.transpose(ps_T[0][:, kc, 0:E], gw[:, kc * P:(kc + 1) * P], cst["ident"][0:E, 0:E])
                m.then_inc(gw_T, 1)
                pe.wait_ge(gw_T, 2)
                with pe.Fori(0, NT // 2) as pair:
                    for u in range(2):
                        j = pair * 2 + u
                        pe.wait_ge(normed, j + 1)
                        for kc in range(KC):
                            m = pe.transpose(ps_T[u][:, kc, :], cur[u][:, kc * P:(kc + 1) * P], cst["ident"][:])
                        m.then_inc(turned, 1)
                        pe.wait_ge(copied, j + 1)
                        for kc in range(KC):
                            m = pe.matmul(ps_l[:, bass.ds(j, 1), :], xT[u][:, kc, :], gwT[:, kc, :],
                                          start=(kc == 0), stop=(kc == KC - 1))
                            if kc == 0:
                                m.then_inc(cur_free, 1)
                        m.then_inc(scored, 1)
                pe.wait_ge(vec, 13)
                pe.matmul(ps_in[:], cst["before"][:], both[:], start=True, stop=True).then_inc(ten, 1)
                pe.matmul(ps_tot[:], cst["ones"][:], both[:], start=True, stop=True).then_inc(ten, 1)

            @block.scalar
            def _(act):
                act.wait_ge(gw_T, 1)
                act.copy(gwT[:], ps_T[0][:, :, 0:E]).then_inc(gw_T, 1)
                with act.Fori(0, NT // 2) as pair:
                    for u in range(2):
                        j = pair * 2 + u
                        act.wait_ge(turned, j + 1)
                        act.copy(xT[u][:], ps_T[u][:]).then_inc(copied, 1)
                act.wait_ge(vec, 14)
                act.activation(best[:], top[1][:], ACT.Exp).then_inc(act_s, 1)


def dense_experts(nc, cst, table, W, M, m_store):
    with Phase(nc, "md") as ph:
        sb, sem = ph.sb, ph.sem
        w_sb = sb("w", [P, KC, D])
        tb = [sb(f"tb{u}", [P, D, E]) for u in range(2)]
        ps_w = [ph.ps(f"ps_w{kc}", [P, D]) for kc in range(KC)]
        w_in, turned, added, high, low, stored = (sem("w_in"), sem("turned"), sem("added"), sem("high"), sem("low"),
                                                  sem("stored"))
        tb_in = [sem(f"tb_in{u}") for u in range(2)]
        with nc.Block() as block:
            @block.sync
            def _(sp):
                sp.dma_start(w_sb[:], W.rearrange("(a p) c -> p a c", p=P)).then_inc(w_in, 16)
                for kc in range(KC):
                    if kc >= 2:
                        sp.wait_ge(low, kc - 1)
                    sp.dma_start(tb[kc % 2][:], table[kc * P * D:(kc + 1) * P * D, :]
                                 .rearrange("(p r) e -> p (r e)", p=P)).then_inc(tb_in[kc % 2], 16)
                for kc in range(KC):
                    sp.wait_ge(low, kc + 1)
                    sp.dma_start(m_store[:, kc], M[:, kc].bitcast(F32)).then_inc(stored, 16)
                sp.wait_ge(stored, 16 * KC)

            @block.tensor
            def _(pe):
                pe.wait_ge(w_in, 16)
                for kc in range(KC):
                    for rb in range(KC):
                        m = pe.transpose(ps_w[kc][:, rb * P:(rb + 1) * P], w_sb[:, rb, kc * P:(kc + 1) * P], cst["ident"][:])
                    m.then_inc(turned, 1)

            @block.vector
            def _(dve):
                for kc in range(KC):
                    t = tb[kc % 2][:].rearrange("p r e -> p e r")
                    dve.wait_ge(tb_in[kc % 2], 16 * (kc // 2 + 1))
                    dve.wait_ge(turned, kc + 1)
                    dve.tensor_tensor(t, bc(ps_w[kc][:], 1, E), t, ALU.add).then_inc(added, 1)
                    dve.wait_ge(high, kc + 1)
                    dve.tensor_tensor(M[:, kc, 1], t, M[:, kc, 0].bitcast(F32), ALU.subtract).then_inc(low, 1)

            @block.scalar
            def _(act):
                for kc in range(KC):
                    act.wait_ge(added, kc + 1)
                    act.copy(M[:, kc, 0], tb[kc % 2][:].rearrange("p r e -> p e r")).then_inc(high, 1)


def split_matmul(pe, out, lhs, rhs, first=True, last=True):
    for n, (a, b) in enumerate(((0, 0), (0, 1), (1, 0))):
        m = pe.matmul(out, lhs[a], rhs[b], start=first and n == 0, stop=last and n == 2)
    return m


def experts(nc, cst, name, M, tile_tab, dispatched, routed, m_store=None):
    with Phase(nc, name) as ph:
        sb, sem = ph.sb, ph.sem
        xt = [sb(f"xt{u}", [P, D]) for u in range(2)]
        xT = [[sb(f"xT{u}{h}", [P, KC, P], F32R) for h in range(2)] for u in range(2)]
        yt = [sb(f"yt{u}", [P, D]) for u in range(2)]
        ps_T = [ph.ps(f"ps_T{u}", [P, KC, P]) for u in range(2)]
        ps_y = [ph.ps(f"ps_y{u}", [P, D]) for u in range(2)]
        xt_in = [sem(f"xt_in{u}") for u in range(2)]
        y_out = [sem(f"y_out{u}") for u in range(2)]
        turned, high, low, multiplied, y_ready = (sem("turned"), sem("high"), sem("low"), sem("multiplied"), sem("y_ready"))
        m_in = [sem(f"m_in{kc}") for kc in range(KC)]
        HB = BLOCKS // 2
        with nc.Block() as block:
            @block.sync
            def _(sp):
                for u in range(2):
                    sp.sem_inc(y_out[u], 16)

                def load(u, n):
                    row = sp.snap(sp.value_load(tile_tab[0:1, 1, bass.ds(n, 1)], min_val=0,
                                                max_val=(E - 1) * REGION + TOK))
                    sp.wait_ge(turned, n + 1)
                    sp.dma_start(xt[u][:], dispatched[bass.ds(row, P), :]).then_inc(xt_in[u], 16)

                def store(u, n):
                    row = sp.snap(n * P)
                    sp.wait_ge(y_ready, n + 3)
                    sp.dma_start(routed[bass.ds(row, P), :], yt[u][:]).then_inc(y_out[u], 16)

                for u in range(2):
                    load(u, u)
                for kc in range(KC if m_store is not None else 0):
                    sp.dma_start(M[:, kc].bitcast(F32), m_store[:, kc]).then_inc(m_in[kc], 16)
                with sp.Fori(0, HB - 1) as pair:
                    for u in range(2):
                        load(u, pair * 2 + 2 + u)
                        store(u, pair * 2 + u)
                for u in range(2):
                    store(u, BLOCKS - 2 + u)
                    sp.wait_ge(y_out[u], 16 * (HB + 1))

            def turn(pe, u, n, pair):
                pe.wait_ge(xt_in[u], (pair + 1) * 16)
                pe.wait_ge(low, n + 1)
                for kc in range(KC):
                    m = pe.transpose(ps_T[u][:, kc, :], xt[u][:, kc * P:(kc + 1) * P], cst["ident"][:])
                m.then_inc(turned, 1)

            def multiply(pe, u, n):
                e = pe.value_load(tile_tab[0:1, 0, bass.ds(n, 1)] if not isinstance(n, int)
                                  else tile_tab[0:1, 0, n:n + 1], min_val=0, max_val=E - 1)
                pe.wait_ge(low, n + 3)
                pe.wait_ge(y_ready, n + 1)
                for kc in range(KC):
                    m = split_matmul(pe, ps_y[u][:].unsqueeze(1), [xT[u][h][:, kc, :] for h in range(2)],
                                     [M[:, kc, h, bass.ds(e, 1), :] for h in range(2)], kc == 0, kc == KC - 1)
                m.then_inc(multiplied, 1)

            @block.tensor
            def _(pe):
                pe.sem_inc(turned, 2)
                pe.sem_inc(multiplied, 2)
                turn(pe, 0, 0, 0)
                for kc in range(KC if m_store is not None else 0):
                    pe.wait_ge(m_in[kc], 16)
                with pe.Fori(0, HB - 1) as pair:
                    turn(pe, 1, pair * 2 + 1, pair)
                    multiply(pe, 0, pair * 2)
                    turn(pe, 0, pair * 2 + 2, pair + 1)
                    multiply(pe, 1, pair * 2 + 1)
                turn(pe, 1, BLOCKS - 1, HB - 1)
                multiply(pe, 0, BLOCKS - 2)
                multiply(pe, 1, BLOCKS - 1)

            @block.vector
            def _(dve):
                dve.sem_inc(low, 2)
                with dve.Fori(0, HB) as pair:
                    for u in range(2):
                        n = pair * 2 + u
                        dve.wait_ge(high, n + 1)
                        dve.tensor_tensor(xT[u][1][:], ps_T[u][:], xT[u][0][:].bitcast(F32), ALU.subtract).then_inc(low, 1)

            @block.scalar
            def _(act):
                act.sem_inc(y_ready, 2)
                with act.Fori(0, HB) as pair:
                    for u in range(2):
                        n = pair * 2 + u
                        act.wait_ge(turned, n + 3)
                        act.wait_ge(multiplied, n + 1)
                        act.copy(xT[u][0][:], ps_T[u][:]).then_inc(high, 1)
                    for u in range(2):
                        n = pair * 2 + u
                        act.wait_ge(multiplied, n + 3)
                        act.wait_ge(y_out[u], pair * 16 + 16)
                        act.copy(yt[u][:], ps_y[u][:]).then_inc(y_ready, 1)

            @block.gpsimd
            def _(pool):
                pass


def combine(nc, name, x, routed, gate, row_of, out):
    with Phase(nc, name) as ph:
        sb, sem = ph.sb, ph.sem
        xt = [sb(f"xt{u}", [P, D]) for u in range(2)]
        y = [[sb(f"y{u}{k}", [P, D]) for k in range(2)] for u in range(2)]
        s = [sb(f"s{u}", [P, D]) for u in range(2)]
        res = [sb(f"res{u}", [P, D]) for u in range(2)]
        idx = [sb(f"idx{u}", [P, 2], I32) for u in range(2)]
        x_in = [sem(f"x_in{u}") for u in range(2)]
        y_in = [sem(f"y_in{u}") for u in range(2)]
        out_s = [sem(f"out{u}") for u in range(2)]
        idx_in, used, first, ordered = sem("idx_in"), sem("used"), sem("first"), sem("ordered")
        x_v = x.rearrange("(j p) d -> j p d", p=P)
        out_v = out.rearrange("(j p) d -> j p d", p=P)
        with nc.Block() as block:
            @block.sync
            def _(sp):
                for u in range(2):
                    sp.sem_inc(out_s[u], 16)
                with sp.Fori(0, NT // 2) as pair:
                    for u in range(2):
                        j = pair * 2 + u
                        sp.wait_ge(used, j + 1)
                        sp.dma_start(xt[u][:], x_v[bass.ds(j, 1)].rearrange("a p d -> (a p) d")).then_inc(x_in[u], 16)

            @block.gpsimd
            def _(pool):
                with pool.Fori(0, NT // 2) as pair:
                    for u in range(2):
                        j = pair * 2 + u
                        pool.wait_ge(used, j + 1)
                        pool.tensor_copy(idx[u][:].unsqueeze(2), row_of[:, :, bass.ds(j, 1)]).then_inc(idx_in, 1)
                        pool.wait_ge(idx_in, j + 1)
                        pool.sem_inc(ordered, 1)
                        for k in range(2):
                            pool.indirect_dma_start(y[u][k][:], None, routed,
                                                    bass.IndirectOffsetOnAxis(ap=idx[u][:, k:k + 1], axis=0)).then_inc(y_in[u], 16)

            @block.vector
            def _(dve):
                dve.sem_inc(used, 2)
                with dve.Fori(0, NT // 2) as pair:
                    for u in range(2):
                        j = pair * 2 + u
                        dve.wait_ge(y_in[u], (pair + 1) * 32)
                        dve.wait_ge(x_in[u], (pair + 1) * 16)
                        dve.scalar_tensor_tensor(out=s[u][:].unsqueeze(1), in0=y[u][0][:].unsqueeze(1), scalar=gate[:, 0, bass.ds(j, 1)],
                                                 in1=xt[u][:].unsqueeze(1), op0=ALU.mult, op1=ALU.add).then_inc(first, 1)
                        dve.wait_ge(first, j + 1)
                        dve.wait_ge(out_s[u], (pair + 1) * 16)
                        dve.scalar_tensor_tensor(out=res[u][:], in0=y[u][1][:], scalar=gate[:, 1, bass.ds(j, 1)],
                                                 in1=s[u][:], op0=ALU.mult, op1=ALU.add).then_inc(used, 1)

            @block.scalar
            def _(act):
                with act.Fori(0, NT // 2) as pair:
                    for u in range(2):
                        j = pair * 2 + u
                        act.wait_ge(used, j + 3)
                        act.dma_start(out_v[bass.ds(j, 1)].rearrange("a p d -> (a p) d"), res[u][:]).then_inc(out_s[u], 16)
                for u in range(2):
                    act.wait_ge(out_s[u], 16 * (NT // 2 + 1))


def wait(eng, sem, n):
    if not (isinstance(n, int) and n <= 0):
        eng.wait_ge(sem, n)


def col(ap, t):
    return ap[:, t:t + 1] if isinstance(t, int) else ap[:, bass.ds(t, 1)]


def pipeline(eng, step, lead):
    first, last = 4, NT - 4
    for i in range(lead, first):
        step(i, i % 4, i // 4)
    with eng.Fori(0, (last - first) // 4) as quad:
        for s in range(4):
            step(quad * 4 + (first + s), s, quad + first // 4)
    for i in range(last, NT + 2):
        step(i, i % 4, i // 4)


def inside(t):
    return not isinstance(t, int) or 0 <= t < NT


def attention(nc, cst, x, routed, gate, row_of, w, base, h2T):
    QK, V, G, O = range(4)
    HG = 4
    with Phase(nc, "at", recycle=True) as ph:
        sb, sem = ph.sb, ph.sem
        names = ("ws_scaled w_high w_low w_done consts "
                 "s x1 bn bn_ok mv ve rstd y t1 t2 r2 h hT_t hT_hi hT_lo low low_sb gate_p z ab ez lz ls sig gs bs dec "
                 "eb enb es decay qe ke kd qk_t keT qbd0 qbd1 v v_sb u_p s1 s2 s_tmp a0 a1 am0 am1 qk o osq ss ms8 r8 on og "
                 "og_t ogT_hi ogT_lo wo x2 sq msd rh2 h2 h2_t h2_hi h2_lo base idx_in idx_ok").split()
        S = {n: sem(n) for n in names}
        x_in = [sem(f"x_in{u}") for u in range(2)]
        y_in = [sem(f"y_in{u}") for u in range(2)]
        h_out = [sem(f"h_out{u}") for u in range(2)]
        b_out = [sem(f"b_out{u}") for u in range(2)]
        w_in = [sem(f"w_in{u}") for u in range(2)]
        small_in = sem("small_in")
        wh = [[sb(f"w{n}{h}", [P, KC, D], F32R) for h in range(2)] for n in range(4)]
        w1 = sb("w1f", [P, KC, LOW])
        w1h = [sb(f"w1h{h}", [P, KC, LOW], F32R) for h in range(2)]
        w2b = sb("w2b", [LOW + 1, KEY])
        n1 = sb("n1", [P, KC])
        gn = sb("gn", [P, 1])
        stage = [sb(f"stage{u}", [P, KC, D]) for u in range(2)]
        cum16, suf16, causal = sb("cum16", [P, P]), sb("suf16", [P, P]), sb("causal", [P, P])
        chunk16, hmask, keep = sb("chunk16", [P, 2]), sb("hmask", [P, HG, P]), sb("keep", [P, NT // 4])
        power = sb("power", [P, H])
        two = lambda n, s, dt=F32: [sb(f"{n}{u}", s, dt) for u in range(2)]
        xt, s_, h, v_sb, gs, og, x2, h2, bt = (two(n, [P, D]) for n in
                                               "xt s h v gs og x2 h2 bt".split())
        h2T_sb = two("h2T", [P, 2, KC, P], F32R)
        yk = [two(f"yk{k}_", [P, D]) for k in range(2)]
        x1 = [stage[0][:, r, :] for r in range(4)]
        y = [stage[1][:, r, :] for r in range(4)]
        idx = two("idx", [P, 2], I32)
        bn, mv, ve, t1, t2, rstd, r2 = (two(n, s) for n, s in (("bn", [P, 6]), ("mv", [P, 2]), ("ve", [P, 1]),
                                        ("t1", [P, 1]), ("t2", [P, 1]), ("rstd", [P, 1]), ("r2", [P, 1])))
        hT = [two(f"hT{hf}_", [P, KC, P], F32R) for hf in range(2)]
        ogT = [sb(f"ogT{hf}", [P, KC, P], F32R) for hf in range(2)]
        low = two("low", [LOW + 1, P])
        ab, ez, lz = sb("ab", [P, KEY + D]), sb("ez", [P, KEY + D]), sb("lz", [P, KEY + D])
        ls = two("ls", [P, KEY + D])
        sig = sb("sig", [P, D])
        eb, enb, es = sb("eb", [P, KEY]), sb("enb", [P, KEY]), sb("es", [P, KEY])
        decay = sb("decay", [P, 2, 2])
        qe, ke = sb("qe", [P, KEY]), sb("ke", [P, KEY])
        kd = two("kd", [P, KEY])
        keT, qbd = sb("keT", [P, 2, P]), sb("qbd", [P, 2, HG, P])
        am = sb("am", [P, H, P])
        state = [sb(f"state{n}", [P, 2, HV]) for n in range(4)]
        s_tmp = sb("s_tmp", [P, 2, HV])
        osq, on = sb("osq", [P, D]), sb("on", [P, D])
        ss, ms8, r8 = sb("ss", [P, H]), sb("ms8", [P, H]), sb("r8", [P, H])
        sq, sqs, msd, rh2 = sb("sq", [P, D]), sb("sqs", [P, 1]), sb("msd", [P, 1]), sb("rh2", [P, 1])
        ps_T = ph.ps("ps_T", [P, KC, P])
        ps_qk = ph.ps("ps_qk", [P, D])
        ps_v = ph.ps("ps_v", [P, D])
        ps_zg = ph.ps("ps_zg", [P, 2 * D])
        ps_bs = ph.ps("ps_bs", [P, D])
        ps_a = [ph.ps(f"ps_a{g}", [P, HG, P]) for g in range(2)]
        ps_low, ps_dec = ps_zg[0:LOW, 0:P], ps_a[1][:, 0, 0:4]
        ps_z, ps_g, zg = ps_zg[:, D - KEY:D], ps_zg[:, D:2 * D], ps_zg[:, D - KEY:2 * D]
        ps_u = ps_qk[:, 0:4 * HV].rearrange("p (c g v) -> p c g v", c=2, g=2)

        w_src = [(w["wq"], w["wk"]), (w["wv"],), (w["wg"],), (w["wo"],)]
        x_v = x.rearrange("(j p) d -> j p d", p=P)
        base_v = base.rearrange("(j p) d -> j p d", p=P)

        def tile_of(ap, t):
            return ap[t] if isinstance(t, int) else ap[bass.ds(t, 1)].rearrange("a p d -> (a p) d")

        with nc.Block() as block:
            @block.sync
            def _(sp):
                sp.dma_start(w1[:], w["w1"].rearrange("(kc p) n -> p kc n", p=P)).then_inc(small_in, 16)
                sp.dma_start(w2b[0:LOW, :], w["w2"]).then_inc(small_in, 16)
                sp.dma_start(w2b[LOW:LOW + 1, :], w["gk_b"].rearrange("(o n) -> o n", o=1)).then_inc(small_in, 16)
                sp.dma_start(n1[:], w["norm1_w"].rearrange("(kc p) -> p kc", p=P),
                             allow_slow_non_contiguous=True).then_inc(small_in, 16)
                for c in range(2):
                    sp.dma_start(gn[c * HV:(c + 1) * HV, :], w["gnorm_w"].rearrange("(v o) -> v o", o=1)).then_inc(small_in, 16)
                for n in range(4):
                    if n >= 2:
                        sp.wait_ge(S["w_low"], n - 1)
                    at = 0
                    for src in w_src[n]:
                        cols = src.shape[1]
                        sp.dma_start(stage[n % 2][:, :, at:at + cols],
                                     src.rearrange("(kc p) n -> p kc n", p=P)).then_inc(w_in[n % 2], 16)
                        at += cols

                def step(i, r, q):
                    t = i + 3
                    if inside(t):
                        row = t if isinstance(t, int) else sp.snap(t)
                        wait(sp, S["s"], t - 1)
                        sp.dma_start(xt[(r + 3) % 2][:], tile_of(x_v, row)).then_inc(x_in[(r + 3) % 2], 16)
                    t = i - 2
                    if inside(t):
                        row = t * P if isinstance(t, int) else sp.snap(t * P)
                        dst = h2T[:, :, :, row:row + P] if isinstance(t, int) else h2T[:, :, :, bass.ds(row, P)]
                        wait(sp, S["h2_lo"], t + 1)
                        sp.dma_start(dst, h2T_sb[r % 2][:].bitcast(F32)).then_inc(h_out[r % 2], 16)
                    t = i - 1
                    if inside(t):
                        row = t if isinstance(t, int) else sp.snap(t)
                        wait(sp, S["base"], t + 1)
                        sp.dma_start(tile_of(base_v, row), bt[(r + 1) % 2][:]).then_inc(b_out[(r + 1) % 2], 16)
                pipeline(sp, step, -3)
                for u in range(2):
                    sp.wait_ge(h_out[u], 16 * NT // 2)
                    sp.wait_ge(b_out[u], 16 * NT // 2)

            @block.gpsimd
            def _(pool):
                made = Steps(pool, S["consts"])

                def ms(ap, v):
                    made.chain(pool.memset(ap, v))
                for ap, v in ((cum16, 1 / 16), (suf16, 1 / 16), (causal, 1.0), (chunk16, 0.0), (hmask, 0.0),
                              (keep, 1.0), (power, -0.5), (low[0], 1.0), (low[1], 1.0), (state[0], 0.0), (kd[0], 0.0), (kd[1], 0.0)):
                    ms(ap[:], v)
                for m, sign in ((cum16, 1), (causal, 1), (suf16, -1)):
                    made.chain(pool.affine_select(out=m[:], in_=m[:], compare_op=ALU.is_ge if sign > 0 else ALU.is_gt,
                                                  fill=0.0, base=0, pattern=[[sign, P]], channel_multiplier=-sign))
                ms(cum16[0:CHUNK, CHUNK:P], 0.0)
                ms(causal[0:CHUNK, CHUNK:P], 0.0)
                ms(suf16[CHUNK:P, 0:CHUNK], 0.0)
                for c in range(2):
                    ms(chunk16[c * CHUNK:(c + 1) * CHUNK, c:c + 1], 1 / 16)
                for n in range(HG):
                    ms(hmask[n * HK:(n + 1) * HK, n, :], 1.0)
                ms(keep[:].rearrange("p (a b) -> p a b", b=TILES_B // 4)[:, :, 0:1], 0.0)

                def step(i, r, q):
                    t = i - 1
                    if inside(t):
                        wait(pool, S["ms8"], t + 1)
                        pool.tensor_tensor(r8[:], ms8[:], power[:, 0:H], ALU.pow).then_inc(S["r8"], 1)
                    t = i + 3
                    if inside(t):
                        u = (r + 3) % 2
                        wait(pool, S["x1"], t - 1)
                        src = row_of[:, :, t:t + 1] if isinstance(t, int) else row_of[:, :, bass.ds(t, 1)]
                        pool.tensor_copy(idx[u][:].unsqueeze(2), src).then_inc(S["idx_in"], 1)
                        wait(pool, S["idx_in"], t + 1)
                        pool.sem_inc(S["idx_ok"], 1)
                        for k in range(2):
                            pool.indirect_dma_start(yk[k][u][:], None, routed,
                                                    bass.IndirectOffsetOnAxis(ap=idx[u][:, k:k + 1], axis=0)).then_inc(y_in[u], 16)
                    t = i - 1
                    if inside(t):
                        u = (r + 1) % 2
                        wait(pool, S["x2"], t + 1)
                        wait(pool, b_out[u], (t + (r + 1) % 2 * -1) * 8)
                        pool.tensor_tensor(bt[u][:], x1[(r + 3) % 4], x2[u][:], ALU.add).then_inc(S["base"], 1)
                    t = i + 2
                    if inside(t):
                        u = r % 2
                        wait(pool, S["ve"], t + 1)
                        pool.tensor_tensor(rstd[u][:], ve[u][:], power[:, 0:1], ALU.pow).then_inc(S["rstd"], 1)
                    if inside(i - 1):
                        wait(pool, S["msd"], i)
                        pool.tensor_tensor(rh2[:], msd[:], power[:, 0:1], ALU.pow).then_inc(S["rh2"], 1)
                    if inside(t):
                        wait(pool, S["t2"], t + 1)
                        pool.tensor_tensor(r2[u][:], t2[u][:], power[:, 0:1], ALU.pow).then_inc(S["r2"], 1)
                pipeline(pool, step, -3)

            @block.scalar
            def _(act):
                act.preload_act_table_set("natural_log_exp_and_others")
                for n in range(4):
                    act.wait_ge(S["ws_scaled"], n + 1)
                    act.copy(wh[n][0][:], stage[n % 2][:]).then_inc(S["w_high"], 1)
                act.wait_ge(S["ws_scaled"], 5)
                act.copy(w1h[0][:], w1[:]).then_inc(S["w_high"], 1)

                def step(i, r, q):
                    u, nu = r % 2, (r + 1) % 2
                    if inside(i - 1):
                        wait(act, S["o"], i)
                        wait(act, S["ss"], i - 1)
                        act.activation(osq[:], ps_v[:], ACT.Square).then_inc(S["osq"], 1)
                    n = i + 1
                    if inside(n):
                        wait(act, S["hT_t"], n + 1)
                        wait(act, S["v"], n - 1)
                        wait(act, S["qk"], n - 1)
                        act.copy(hT[0][nu][:], ps_T[:]).then_inc(S["hT_hi"], 1)
                    if inside(i):
                        wait(act, S["bs"], i + 1)
                        wait(act, S["kd"], i)
                        act.activation(eb[:], ps_bs[:, 0:KEY], ACT.Exp).then_inc(S["eb"], 1)
                        act.activation(enb[:], ps_bs[:, 0:KEY], ACT.Exp, scale=-1.0).then_inc(S["enb"], 1)
                        act.activation(es[:], ps_bs[:, KEY:2 * KEY], ACT.Exp).then_inc(S["es"], 1)
                        wait(act, S["dec"], i + 1)
                        wait(act, S["s2"], i)
                        act.activation(decay[:].rearrange("p g c -> p (g c)"), ps_dec, ACT.Exp).then_inc(S["decay"], 1)
                    if inside(n):
                        wait(act, S["low"], n + 1)
                        wait(act, S["z"], n - 1)
                        act.copy(low[nu][0:LOW, :], ps_low).then_inc(S["low_sb"], 1)
                    t = i - 2
                    if inside(t):
                        wait(act, S["h2_t"], t + 1)
                        wait(act, h_out[u], (t - r % 2) * 8)
                        act.copy(h2T_sb[u][:, 0], ps_T[:]).then_inc(S["h2_hi"], 1)
                    if inside(n):
                        wait(act, S["z"], n + 1)
                        wait(act, S["gate_p"], n + 1)
                        wait(act, S["ez"], n)
                        act.activation(ab[:], zg, ACT.Abs).then_inc(S["ab"], 1)
                        wait(act, S["ab"], n + 1)
                        wait(act, S["lz"], n)
                        act.activation(ez[:], ab[:], ACT.Exp, scale=-1.0).then_inc(S["ez"], 1)
                        wait(act, S["ez"], n + 1)
                        wait(act, S["ls"], n)
                        act.activation(lz[:], ez[:], ACT.Ln, bias=1.0).then_inc(S["lz"], 1)
                    if inside(i):
                        wait(act, S["qk_t"], i + 1)
                        wait(act, S["a1"], i)
                        act.copy(keT[:], ps_T[:, 2:4, :]).then_inc(S["keT"], 1)
                    if inside(n):
                        wait(act, S["ls"], n + 1)
                        wait(act, S["gs"], n)
                        act.activation(sig[:], ls[nu][:, KEY:], ACT.Exp).then_inc(S["sig"], 1)
                        wait(act, S["v"], n + 1)
                        wait(act, S["o"], n - 1)
                        act.copy(v_sb[nu][:], ps_v[:]).then_inc(S["v_sb"], 1)
                    if inside(i - 1):
                        wait(act, S["og_t"], i)
                        wait(act, S["wo"], i - 1)
                        act.copy(ogT[0][:], ps_T[:]).then_inc(S["ogT_hi"], 1)
                        wait(act, S["x2"], i)
                        wait(act, S["msd"], i - 1)
                        act.activation(sq[:], x2[nu][:], ACT.Square, accum_out=sqs[:]).then_inc(S["sq"], 1)
                pipeline(act, step, -1)

            @block.vector
            def _(dve):
                dve.wait_ge(small_in, 96)
                for n in range(4):
                    dve.wait_ge(w_in[n % 2], (32, 16, 48, 32)[n])
                    for kc in range(KC):
                        if n == 0:
                            dve.tensor_scalar(stage[0][:, kc, 0:KEY], stage[0][:, kc, 0:KEY], n1[:, kc:kc + 1],
                                              float(HK) ** -0.5, ALU.mult, ALU.mult)
                            m = dve.tensor_scalar(stage[0][:, kc, KEY:], stage[0][:, kc, KEY:], n1[:, kc:kc + 1], None, ALU.mult)
                        else:
                            m = dve.tensor_scalar(stage[n % 2][:, kc, :], stage[n % 2][:, kc, :],
                                                  gn[:, 0:1] if n == 3 else n1[:, kc:kc + 1], None, ALU.mult)
                    m.then_inc(S["ws_scaled"], 1)
                    dve.wait_ge(S["w_high"], n + 1)
                    dve.tensor_tensor(wh[n][1][:], stage[n % 2][:], wh[n][0][:].bitcast(F32), ALU.subtract).then_inc(S["w_low"], 1)
                for kc in range(KC):
                    m = dve.tensor_scalar(w1[:, kc, :], w1[:, kc, :], n1[:, kc:kc + 1], None, ALU.mult)
                m.then_inc(S["ws_scaled"], 1)
                dve.wait_ge(S["w_high"], 5)
                dve.tensor_tensor(w1h[1][:], w1[:], w1h[0][:].bitcast(F32), ALU.subtract).then_inc(S["w_low"], 1)
                dve.wait_ge(S["consts"], 25)

                def step(i, r, q):
                    u, nu = r % 2, (r + 1) % 2
                    n, j, m = i + 1, i - 1, i + 2
                    if inside(n):
                        wait(dve, S["hT_hi"], n + 1)
                        dve.tensor_tensor(hT[1][nu][:], ps_T[:], hT[0][nu][:].bitcast(F32), ALU.subtract).then_inc(S["hT_lo"], 1)
                    if inside(j):
                        wait(dve, S["osq"], j + 1)
                        dve.tensor_reduce(ss[:], osq[:].rearrange("p (h v) -> p h v", h=H), AX.X, ALU.add).then_inc(S["ss"], 1)
                        wait(dve, S["ss"], j + 1)
                        wait(dve, S["r8"], j)
                        dve.tensor_scalar(ms8[:], ss[:], 1.0 / HV, RMS_EPS, ALU.mult, ALU.add).then_inc(S["ms8"], 1)
                    if inside(i):
                        wait(dve, S["qk"], i + 1)
                        wait(dve, S["eb"], i + 1)
                        wait(dve, S["qk_t"], i)
                        dve.tensor_tensor(qe[:], ps_qk[:, 0:KEY], eb[:], ALU.mult).then_inc(S["qe"], 1)
                        wait(dve, S["enb"], i + 1)
                        dve.tensor_tensor(ke[:], ps_qk[:, KEY:], enb[:], ALU.mult).then_inc(S["ke"], 1)
                        wait(dve, S["es"], i + 1)
                        wait(dve, S["u_p"], i)
                        for c in range(2):
                            rows = slice(c * CHUNK, (c + 1) * CHUNK)
                            op = dve.tensor_tensor(kd[c][rows], ps_qk[rows, KEY:], es[rows], ALU.mult)
                        op.then_inc(S["kd"], 1)
                    if inside(j):
                        wait(dve, S["r8"], j + 1)
                        wait(dve, S["og"], j)
                        dve.tensor_tensor(on[:].rearrange("p (h v) -> p h v", h=H), ps_v[:].rearrange("p (h v) -> p h v", h=H),
                                          bc(r8[:], 2, HV), ALU.mult).then_inc(S["on"], 1)
                        wait(dve, S["on"], j + 1)
                        wait(dve, S["og_t"], j - 1)
                        dve.tensor_tensor(og[nu][:], on[:], gs[nu][:], ALU.mult).then_inc(S["og"], 1)
                    if inside(i - 2):
                        wait(dve, S["h2_hi"], i - 1)
                        dve.tensor_tensor(h2T_sb[u][:, 1], ps_T[:], h2T_sb[u][:, 0].bitcast(F32), ALU.subtract).then_inc(S["h2_lo"], 1)
                    if inside(n):
                        wait(dve, S["lz"], n + 1)
                        wait(dve, S["dec"], n - 1)
                        dve.scalar_tensor_tensor(out=ls[nu][:], in0=zg, scalar=0.0, in1=lz[:],
                                                 op0=ALU.min, op1=ALU.subtract).then_inc(S["ls"], 1)
                    if inside(i):
                        wait(dve, S["keT"], i + 1)
                        wait(dve, S["o"], i)
                        for g in range(2):
                            dve.tensor_tensor(qbd[:, g], bc(ps_T[:, g, :], 1, HG), hmask[:], ALU.mult).then_inc(S[f"qbd{g}"], 1)
                    if inside(n):
                        wait(dve, S["sig"], n + 1)
                        wait(dve, S["og"], n - 1)
                        dve.tensor_tensor(gs[nu][:], ps_g, sig[:], ALU.mult).then_inc(S["gs"], 1)
                    if inside(i):
                        wait(dve, S["u_p"], i + 1)
                        wait(dve, S["decay"], i + 1)
                        wait(dve, S["s2"], i)
                        for g in range(2):
                            op = dve.scalar_tensor_tensor(out=state[2 * u + 1][:, g], in0=state[2 * u][:, g],
                                                         scalar=decay[:, g, 0:1], in1=ps_u[:, 0, g],
                                                         op0=ALU.mult, op1=ALU.add)
                        op.then_inc(S["s1"], 1)
                        wait(dve, S["s1"], i + 1)
                        wait(dve, S["o"], i)
                        nxt = state[(2 * u + 2) % 4] if r != 3 else s_tmp
                        for g in range(2):
                            op = dve.scalar_tensor_tensor(out=nxt[:, g], in0=state[2 * u + 1][:, g],
                                                         scalar=decay[:, g, 1:2], in1=ps_u[:, 1, g],
                                                         op0=ALU.mult, op1=ALU.add)
                        if r == 3:
                            op.then_inc(S["s_tmp"], 1)
                            wait(dve, S["s_tmp"], q + 1)
                            if inside(i + 1):
                                op = dve.tensor_scalar(state[0][:], s_tmp[:], col(keep, q + 1), None, ALU.mult)
                        if r != 3 or inside(i + 1):
                            op.then_inc(S["s2"], 1)
                    if inside(j):
                        wait(dve, S["ogT_hi"], j + 1)
                        dve.tensor_tensor(ogT[1][:], ps_T[:], ogT[0][:].bitcast(F32), ALU.subtract).then_inc(S["ogT_lo"], 1)
                    if inside(i):
                        for g in range(2):
                            wait(dve, S[f"a{g}"], i + 1)
                            dve.tensor_tensor(am[:, g * HG:(g + 1) * HG], ps_a[g][:], bc(causal[:], 1, HG),
                                              ALU.mult).then_inc(S[f"am{g}"], 1)
                    if inside(j):
                        wait(dve, S["wo"], j + 1)
                        wait(dve, S["h2"], j - 1)
                        wait(dve, S["base"], j - 1)
                        dve.tensor_tensor(x2[nu][:], ps_bs[:], y[(r + 3) % 4], ALU.add).then_inc(S["x2"], 1)
                    if inside(m):
                        wait(dve, y_in[u], (m - r % 2) * 16 + 32)
                        wait(dve, x_in[u], (m - r % 2) * 8 + 16)
                        dve.scalar_tensor_tensor(out=s_[u][:], in0=yk[0][u][:], scalar=col(gate[:, 0], m), in1=xt[u][:],
                                                 op0=ALU.mult, op1=ALU.add).then_inc(S["s"], 1)
                        wait(dve, S["s"], m + 1)
                        wait(dve, S["base"], m - 3)
                        dve.scalar_tensor_tensor(out=x1[(r + 2) % 4], in0=yk[1][u][:], scalar=col(gate[:, 1], m), in1=s_[u][:],
                                                 op0=ALU.mult, op1=ALU.add).then_inc(S["x1"], 1)
                        wait(dve, S["x1"], m + 1)
                        dve.bn_stats(bn[u][:], x1[(r + 2) % 4]).then_inc(S["bn"], 1)
                        wait(dve, S["bn"], m + 1)
                        dve.sem_inc(S["bn_ok"], 1)
                        dve.bn_aggr(mv[u][:], bn[u][:]).then_inc(S["mv"], 1)
                        wait(dve, S["mv"], m + 1)
                        dve.tensor_scalar(ve[u][:], mv[u][:, 1:2], LN_EPS, None, ALU.add).then_inc(S["ve"], 1)
                    if inside(j):
                        wait(dve, S["sq"], j + 1)
                        wait(dve, S["rh2"], j)
                        dve.tensor_scalar(msd[:], sqs[:], 1.0 / D, RMS_EPS, ALU.mult, ALU.add).then_inc(S["msd"], 1)
                    if inside(m):
                        wait(dve, S["rstd"], m + 1)
                        dve.tensor_scalar(y[(r + 2) % 4], x1[(r + 2) % 4], mv[u][:, 0:1], rstd[u][:],
                                          ALU.subtract, ALU.mult).then_inc(S["y"], 1)
                        dve.tensor_scalar(t1[u][:], mv[u][:, 1:2], rstd[u][:], None, ALU.mult).then_inc(S["t1"], 1)
                        wait(dve, S["t1"], m + 1)
                        dve.tensor_scalar(t2[u][:], t1[u][:], rstd[u][:], RMS_EPS, ALU.mult, ALU.add).then_inc(S["t2"], 1)
                    if inside(j):
                        wait(dve, S["rh2"], j + 1)
                        wait(dve, S["h2_t"], j - 1)
                        dve.tensor_scalar(h2[nu][:], x2[nu][:], rh2[:], None, ALU.mult).then_inc(S["h2"], 1)
                    if inside(m):
                        wait(dve, S["r2"], m + 1)
                        wait(dve, S["hT_t"], m - 1)
                        dve.tensor_scalar(h[u][:], y[(r + 2) % 4], r2[u][:], None, ALU.mult).then_inc(S["h"], 1)
                pipeline(dve, step, -2)

            @block.tensor
            def _(pe):
                pe.wait_ge(S["w_low"], 5)
                pe.wait_ge(S["consts"], 25)

                def turn(src, blocks, at=0):
                    for kc in range(blocks):
                        op = pe.transpose(ps_T[:, at + kc, :], src[:, kc * P:(kc + 1) * P], cst["ident"][:])
                    return op

                def project(out, u, wt):
                    for kc in range(KC):
                        op = split_matmul(pe, out, [hT[hf][u][:, kc, :] for hf in range(2)],
                                         [wt[hf][:, kc, :] for hf in range(2)], kc == 0, kc == KC - 1)
                    return op

                def step(i, r, q):
                    u, nu = r % 2, (r + 1) % 2
                    n, j, t = i + 1, i - 1, i - 2
                    if inside(n):
                        wait(pe, S["h"], n + 1)
                        wait(pe, S["ogT_lo"], n - 2)
                        turn(h[nu], KC).then_inc(S["hT_t"], 1)
                    if inside(i):
                        wait(pe, S["ls"], i + 1)
                        wait(pe, S["x2"], i - 1)
                        pe.matmul(ps_bs[:, 0:KEY], cum16[:], ls[u][:, 0:KEY], start=True, stop=True)
                        pe.matmul(ps_bs[:, KEY:], suf16[:], ls[u][:, 0:KEY], start=True, stop=True).then_inc(S["bs"], 1)
                        wait(pe, S["am1"], i)
                        for g in range(2):
                            op = pe.matmul(ps_dec[:, 2 * g:2 * g + 2], ls[u][:, g * P:(g + 1) * P], chunk16[:],
                                          start=True, stop=True)
                        op.then_inc(S["dec"], 1)
                    if inside(n):
                        wait(pe, S["hT_lo"], n + 1)
                        wait(pe, S["low_sb"], n)
                        for kc in range(KC):
                            op = split_matmul(pe, ps_low, [w1h[hf][:, kc, :] for hf in range(2)],
                                             [hT[hf][nu][:, kc, :] for hf in range(2)], kc == 0, kc == KC - 1)
                        op.then_inc(S["low"], 1)
                        wait(pe, S["gs"], n)
                        project(ps_g, nu, wh[G]).then_inc(S["gate_p"], 1)
                    if inside(t):
                        wait(pe, S["h2"], t + 1)
                        turn(h2[u], KC).then_inc(S["h2_t"], 1)
                    if inside(n):
                        wait(pe, S["low_sb"], n + 1)
                        pe.matmul(ps_z, low[nu][:], w2b[:], start=True, stop=True).then_inc(S["z"], 1)
                    if inside(i):
                        wait(pe, S["ke"], i + 1)
                        wait(pe, S["h2_lo"], i - 1)
                        turn(qe, 2)
                        turn(ke, 2, 2).then_inc(S["qk_t"], 1)
                    if inside(n):
                        wait(pe, S["on"], n - 1)
                        project(ps_v[:], nu, wh[V]).then_inc(S["v"], 1)
                    if inside(i):
                        wait(pe, S["kd"], i + 1)
                        wait(pe, S["v_sb"], i + 1)
                        for c in range(2):
                            for hd in range(H):
                                g, hh = divmod(hd, HG)
                                op = pe.matmul(ps_u[hh * HK:(hh + 1) * HK, c, g], kd[c][:, hd * HK:(hd + 1) * HK],
                                               v_sb[u][:, hd * HV:(hd + 1) * HV], start=True, stop=True)
                        op.then_inc(S["u_p"], 1)
                    if inside(j):
                        wait(pe, S["og"], j + 1)
                        wait(pe, S["keT"], min(j + 2, NT) if isinstance(j, int) else j + 2)
                        wait(pe, S["qbd1"], min(j + 2, NT) if isinstance(j, int) else j + 2)
                        if isinstance(j, int) and j == NT - 1:
                            wait(pe, S["h2_lo"], NT - 1)
                        turn(og[nu], KC).then_inc(S["og_t"], 1)
                    if inside(i):
                        wait(pe, S["keT"], i + 1)
                        for g in range(2):
                            wait(pe, S[f"qbd{g}"], i + 1)
                            wait(pe, S["decay"], i + 1)
                            pe.matmul(ps_a[g][:], keT[:, g], qbd[:, g], start=True, stop=True).then_inc(S[f"a{g}"], 1)
                    if inside(n):
                        wait(pe, S["s2"], n)
                        project(ps_qk[:], nu, wh[QK]).then_inc(S["qk"], 1)
                    if inside(j):
                        wait(pe, S["ogT_lo"], j + 1)
                        wait(pe, S["es"], min(j + 2, NT) if isinstance(j, int) else j + 2)
                        for kc in range(KC):
                            op = split_matmul(pe, ps_bs[:], [ogT[hf][:, kc, :] for hf in range(2)],
                                             [wh[O][hf][:, kc, :] for hf in range(2)], kc == 0, kc == KC - 1)
                        op.then_inc(S["wo"], 1)
                    if inside(i):
                        wait(pe, S["v_sb"], min(i + 2, NT) if isinstance(i, int) else i + 2)
                        wait(pe, S["s1"], i + 1)
                        for g in range(2):
                            wait(pe, S[f"am{g}"], i + 1)
                            for hh in range(HG):
                                hd = g * HG + hh
                                pe.matmul(ps_v[:, hd * HV:(hd + 1) * HV], am[:, hd], v_sb[u][:, hd * HV:(hd + 1) * HV],
                                          start=(hd == 0), stop=False, skip_group_check=True)
                                for c in range(2):
                                    op = pe.matmul(ps_v[c * CHUNK:(c + 1) * CHUNK, hd * HV:(hd + 1) * HV],
                                                  qbd[:, g, hh, c * CHUNK:(c + 1) * CHUNK], state[2 * u + c][:, g],
                                                  start=False, stop=(hd == H - 1), skip_group_check=True)
                        op.then_inc(S["o"], 1)
                pipeline(pe, step, -1)


def swiglu(nc, h2T, norm_w, w_gate, w_up, w_down, base, out):
    SPAN = 512
    NSP = TOK // SPAN
    TS = SPAN // P
    with Phase(nc, "ff") as ph:
        sb, sem = ph.sb, ph.sem
        wgu = [[sb(f"w{m}{hf}", [P, NF, KC, P], F32R) for hf in range(2)] for m in range(2)]
        wd = [sb(f"wd{hf}", [P, NF, D], F32R) for hf in range(2)]
        nw = sb("nw", [P, KC])
        hh = [sb(f"hh{u}", [P, 2, KC, SPAN], F32R) for u in range(2)]
        bt = [sb(f"bt{u}", [P, TS, D]) for u in range(2)]
        sg = [sb(f"sg{u}", [P, SPAN]) for u in range(2)]
        act_f = [sb(f"act{u}", [P, SPAN]) for u in range(2)]
        aT = [[sb(f"aT{u}{hf}", [P, SPAN], F32R) for hf in range(2)] for u in range(2)]
        ps_g = [ph.ps(f"ps_g{u}", [P, SPAN]) for u in range(2)]
        ps_u = [ph.ps(f"ps_u{u}", [P, SPAN]) for u in range(2)]
        acc = [ph.ps(f"acc{t}", [P, D]) for t in range(TS)]
        nw_in, w_scaled, w_high, w_low = sem("nw_in"), sem("w_scaled"), sem("w_high"), sem("w_low")
        w_in = [sem(f"w_in{u}") for u in range(2)]
        h_in = [sem(f"h_in{u}") for u in range(2)]
        b_in = [sem(f"b_in{u}") for u in range(2)]
        x_out = [sem(f"x_out{u}") for u in range(2)]
        gate_s, up_s, silu_s, act_s, high, low, down_s, added = (
            sem(n) for n in ("gate", "up", "silu", "act", "high", "low", "down", "added"))
        base_v = base.rearrange("(s t p) d -> s p t d", p=P, t=TS)
        out_v = out.rearrange("(s t p) d -> s p t d", p=P, t=TS)

        def spans(eng, body):
            for s in range(2):
                body(s, s)
            with eng.Fori(0, NSP // 2 - 1) as pair:
                for s in range(2):
                    body(pair * 2 + (s + 2), s)

        def of(v, s):
            return v[s] if isinstance(s, int) else v[bass.ds(s, 1)].rearrange("a p t d -> (a p) t d")

        with nc.Block() as block:
            @block.sync
            def _(sp):
                def load_h(s, u):
                    at = s * SPAN if isinstance(s, int) else sp.snap(s * SPAN)
                    src = h2T[:, :, :, at:at + SPAN] if isinstance(s, int) else h2T[:, :, :, bass.ds(at, SPAN)]
                    wait(sp, up_s, (s - 1) * NF)
                    sp.dma_start(hh[u][:].bitcast(F32), src).then_inc(h_in[u], 16)

                sp.dma_start(nw[:], norm_w.rearrange("(kc p) -> p kc", p=P), allow_slow_non_contiguous=True).then_inc(nw_in, 16)
                load_h(0, 0)
                for f in range(NF):
                    wait(sp, w_low, f - 1)
                    st = bt[f % 2]
                    cols = slice(f * P, (f + 1) * P)
                    for m, wm in enumerate((w_gate, w_up)):
                        sp.dma_start(st[:, m].rearrange("p (kc n) -> p kc n", kc=KC),
                                     wm[:, cols].rearrange("(kc p) n -> p kc n", p=P)).then_inc(w_in[f % 2], 16)
                    sp.dma_start(st[:, 2], w_down[f * P:(f + 1) * P, :]).then_inc(w_in[f % 2], 16)
                load_h(1, 1)
                sp.wait_ge(w_low, NF)

                def body(s, u, h_next):
                    row = s if isinstance(s, int) else sp.snap(s)
                    wait(sp, x_out[u], (s - u) * 8)
                    sp.dma_start(bt[u][:], of(base_v, row)).then_inc(b_in[u], 16)
                    if isinstance(s, int) and s == 0:
                        return
                    row = s - 1 if isinstance(s, int) else sp.snap(s - 1)
                    wait(sp, added, s)
                    sp.dma_start(of(out_v, row), bt[1 - u][:]).then_inc(x_out[1 - u], 16)
                    if h_next:
                        load_h(s + 1, 1 - u)
                for s in range(NSP):
                    body(s, s % 2, s < NSP - 1)
                sp.wait_ge(added, NSP)
                sp.dma_start(out_v[NSP - 1], bt[1][:]).then_inc(x_out[1], 16)
                for u in range(2):
                    sp.wait_ge(x_out[u], 16 * NSP // 2)

            @block.scalar
            def _(act):
                def body(s, u):
                    for f in range(NF):
                        b = f % 2
                        g = s * NF + f
                        if isinstance(s, int) and s == 0:
                            act.wait_ge(w_scaled, f + 1)
                            for m in range(2):
                                act.copy(wgu[m][0][:, f], bt[b][:, m].rearrange("p (kc n) -> p kc n", kc=KC))
                            act.copy(wd[0][:, f], bt[b][:, 2]).then_inc(w_high, 1)
                        wait(act, gate_s, g + 1)
                        wait(act, act_s, g if f == 0 else g - 1)
                        act.activation(sg[b][:], ps_g[b][:], ACT.Silu).then_inc(silu_s, 1)
                        wait(act, act_s, g + 1)
                        wait(act, down_s, g if f == 0 else g - 1)
                        act.copy(aT[b][0][:], act_f[b][:]).then_inc(high, 1)
                spans(act, body)

            @block.vector
            def _(dve):
                dve.wait_ge(nw_in, 16)

                def finish(s, u):
                    wait(dve, down_s, (s + 1) * NF)
                    wait(dve, b_in[u], (s - u) * 8 + 16)
                    for t in range(TS):
                        op = dve.tensor_tensor(bt[u][:, t], acc[t][:], bt[u][:, t], ALU.add)
                    op.then_inc(added, 1)

                def body(s, u):
                    for f in range(NF):
                        b = f % 2
                        g = s * NF + f
                        if isinstance(s, int) and s == 0:
                            dve.wait_ge(w_in[b], 48 * (f // 2 + 1))
                            for m in range(2):
                                for kc in range(KC):
                                    piece = bt[b][:, m, kc * P:(kc + 1) * P]
                                    op = dve.tensor_scalar(piece, piece, nw[:, kc:kc + 1], None, ALU.mult)
                            op.then_inc(w_scaled, 1)
                            dve.wait_ge(w_high, f + 1)
                            for m in range(2):
                                dve.tensor_tensor(wgu[m][1][:, f], bt[b][:, m].rearrange("p (kc n) -> p kc n", kc=KC),
                                                  wgu[m][0][:, f].bitcast(F32), ALU.subtract)
                            dve.tensor_tensor(wd[1][:, f], bt[b][:, 2], wd[0][:, f].bitcast(F32),
                                              ALU.subtract).then_inc(w_low, 1)
                        wait(dve, silu_s, g + 1)
                        wait(dve, up_s, g + 1)
                        wait(dve, low, g if f == 0 else g - 1)
                        dve.tensor_tensor(act_f[b][:], ps_u[b][:], sg[b][:], ALU.mult).then_inc(act_s, 1)
                        wait(dve, high, g + 1)
                        dve.tensor_tensor(aT[b][1][:], act_f[b][:], aT[b][0][:].bitcast(F32), ALU.subtract).then_inc(low, 1)
                        if f == 0 and not (isinstance(s, int) and s == 0):
                            finish(s - 1, 1 - u)
                spans(dve, body)
                finish(NSP - 1, 1)

            @block.tensor
            def _(pe):
                def down(g, f, first, last):
                    wait(pe, low, g + 1)
                    for t in range(TS):
                        cols = slice(t * P, (t + 1) * P)
                        op = split_matmul(pe, acc[t][:], [aT[f % 2][hf][:, cols] for hf in range(2)],
                                          [wd[hf][:, f] for hf in range(2)], first, last)
                    op.then_inc(down_s, 1)

                def body(s, u):
                    wait(pe, h_in[u], (s - u) * 8 + 16)
                    for f in range(NF):
                        b = f % 2
                        g = s * NF + f
                        if isinstance(s, int) and s == 0:
                            pe.wait_ge(w_low, f + 1)
                        wait(pe, silu_s, g if f == 0 else g - 1)
                        for kc in range(KC):
                            op = split_matmul(pe, ps_g[b][:], [wgu[0][hf][:, f, kc] for hf in range(2)],
                                              [hh[u][:, hf, kc] for hf in range(2)], kc == 0, kc == KC - 1)
                        op.then_inc(gate_s, 1)
                        wait(pe, act_s, g if f == 0 else g - 1)
                        for kc in range(KC):
                            op = split_matmul(pe, ps_u[b][:], [wgu[1][hf][:, f, kc] for hf in range(2)],
                                              [hh[u][:, hf, kc] for hf in range(2)], kc == 0, kc == KC - 1)
                        op.then_inc(up_s, 1)
                        if f > 0:
                            if f == 1:
                                wait(pe, added, s)
                            down(g - 1, f - 1, f == 1, False)
                        elif not (isinstance(s, int) and s == 0):
                            down(g - 1, NF - 1, False, True)
                spans(pe, body)
                down(NSP * NF - 1, NF - 1, False, True)


def macaron(nc, x, norm1_w, wq, wk, wv, w1, w2, gk_b, wg, gnorm_w, wo, ffn_norm_w, w_gate, w_up, w_down,
            gate_w, W, atoms, eaw, importance, mask_idx, out):
    x = x.rearrange("b t d -> (b t) d")
    out = out.rearrange("b t d -> (b t) d")

    def dram(name, shape):
        return nc.dram_tensor(name, shape, F32).ap()

    table = dram("table", (PLACES + NS, E))
    m_store = dram("m_store", (P, KC, 2, E, D))
    dispatched = dram("dispatched", (E * REGION, D))
    routed = dram("routed", (BLOCKS * P, D))
    base = dram("base", (TOK, D))
    h2T = dram("h2T", (P, 2, KC, TOK))
    x3 = dram("x3", (TOK, D))
    with ExitStack() as ctx:
        def sb(name, shape, dt=F32):
            return ctx.enter_context(nc.sbuf_tensor(name, shape, dt))

        cst = constants(nc, sb)
        gate = sb("gate", [P, 2, NT])
        row_of = sb("row_of", [P, 2, NT], I32)
        tile_tab = sb("tile_tab", [1, 2, BLOCKS], I32)
        sparse_places(nc, cst, atoms, eaw, importance, mask_idx, table)
        router(nc, cst, "r1", x, gate_w, gate, row_of, tile_tab, dispatched)
        with nc.sbuf_tensor("M1", [P, KC, 2, E, D], F32R) as M:
            dense_experts(nc, cst, table, W, M, m_store)
            experts(nc, cst, "e1", M, tile_tab, dispatched, routed)
        w = dict(norm1_w=norm1_w, wq=wq, wk=wk, wv=wv, w1=w1, w2=w2, gk_b=gk_b, wg=wg, gnorm_w=gnorm_w, wo=wo)
        attention(nc, cst, x, routed, gate, row_of, w, base, h2T)
        swiglu(nc, h2T, ffn_norm_w, w_gate, w_up, w_down, base, x3)
        router(nc, cst, "r2", x3, gate_w, gate, row_of, tile_tab, dispatched)
        with nc.sbuf_tensor("M2", [P, KC, 2, E, D], F32R) as M:
            experts(nc, cst, "e2", M, tile_tab, dispatched, routed, m_store)
        combine(nc, "c2", x3, routed, gate, row_of, out)


_INS = ['L0_attn_x', 'L0_attn_norm1_w', 'L0_attn_wq', 'L0_attn_wk', 'L0_attn_wv', 'L0_attn_gk_w1', 'L0_attn_gk_w2',
        'L0_attn_gk_b', 'L0_attn_wg', 'L0_attn_gnorm_w', 'L0_attn_wo', 'L0_attn_ffn_norm_w', 'L0_attn_w_gate',
        'L0_attn_w_up', 'L0_attn_w_down', 'L0_ffn_gate_w', 'L0_ffn_W', 'L0_ffn_atoms', 'L0_ffn_expert_atom_weights',
        'L0_ffn_importance', 'L0_ffn_mask_idx']


def kernel(**inputs):
    import numpy as _np
    import concourse.bacc as _bacc
    from concourse.bass_utils import run_bass_kernel_spmd as _run

    nc = _bacc.Bacc("TRN2", target_bir_lowering=False, num_devices=1)
    arrays, args = {}, []
    for name in _INS:
        a = _np.ascontiguousarray(inputs[name])
        arrays[f"in_{name}_dram"] = a
        args.append(nc.dram_tensor(f"in_{name}_dram", a.shape, mybir.dt.from_np(a.dtype), kind="ExternalInput").ap())
    args.append(nc.dram_tensor("out_0_dram", (B, T, D), F32, kind="ExternalOutput").ap())
    macaron(nc, *args)
    r = _run(nc, [arrays], core_ids=[0])
    return r.results[0]["out_0_dram"]
```

```python
from contextlib import ExitStack

import concourse.bass as bass
from concourse import mybir

F32 = mybir.dt.float32
F32R = mybir.dt.float32r
BF16 = mybir.dt.bfloat16
I32 = mybir.dt.int32
ALU = mybir.AluOpType
ACT = mybir.ActivationFunctionType
AX = mybir.AxisListType

P = 128
D = 512
KC = D // P
B, T = 4, 1024
TOK = B * T
NT = TOK // P
E = 8
A = 64
NS = 4096
NB = NS // P
PLACES = D * D
REGION = TOK + P
BLOCKS = (2 * TOK + E * (P - 1)) // P + 1
H, HK, HV = 8, 32, 64
KEY, VAL, LOW = H * HK, H * HV, 16
CHUNK = 64
HID = 1408
NF = HID // P
TILES_B = T // P
LN_EPS, RMS_EPS = 1e-5, 1e-6
assert BLOCKS % 4 == 0


class Phase:

    def __init__(self, nc, name, recycle=False):
        self.nc, self.name, self.recycle, self.sems = nc, name, recycle, []
        self.ctx = ExitStack()

    def __enter__(self):
        self.ctx.__enter__()
        return self

    def __exit__(self, *exc):
        self.ctx.__exit__(*exc)
        if self.recycle and exc[0] is None:
            self.nc.clear_and_free_semaphores(self.sems)
            self.nc.all_engine_barrier()

    def sb(self, name, shape, dt=F32):
        return self.ctx.enter_context(self.nc.sbuf_tensor(f"{self.name}_{name}", shape, dt))

    def ps(self, name, shape, dt=F32):
        return self.ctx.enter_context(self.nc.psum_tensor(f"{self.name}_{name}", shape, dt))

    def sem(self, name):
        self.sems.append(self.nc.alloc_semaphore(f"{self.name}_{name}"))
        return self.sems[-1]


class Steps:

    def __init__(self, eng, sem, base=0):
        self.eng, self.sem, self.base, self.n = eng, sem, base, 0

    def did(self, ins):
        ins.then_inc(self.sem, 1)
        self.n += 1

    def settle(self):
        self.eng.wait_ge(self.sem, self.base + self.n)

    def chain(self, ins):
        self.did(ins)
        self.settle()


def bc(ap, axis, n):
    a = ap.unsqueeze(axis)
    shape = list(a.shape)
    shape[axis] = n
    return a.broadcast_to(shape)


def constants(nc, sb):
    c = {}
    c["ident"] = sb("ident", [P, P])
    c["before"] = sb("before", [P, P])
    c["ones"] = sb("ones", [P, P])
    with Phase(nc, "const") as ph:
        made = ph.sem("made")
        with nc.Block() as block:
            @block.gpsimd
            def _(pool):
                pool.memset(c["ident"][:], 0.0).then_inc(made, 1)
                pool.memset(c["ones"][:], 1.0).then_inc(made, 1)
                pool.wait_ge(made, 2)
                pool.affine_select(out=c["ident"][:], in_=c["ident"][:], compare_op=ALU.not_equal, fill=1.0,
                                   base=0, pattern=[[-1, P]], channel_multiplier=1)
                pool.affine_select(out=c["before"][:], in_=c["ones"][:], compare_op=ALU.is_gt, fill=0.0,
                                   base=0, pattern=[[1, P]], channel_multiplier=-1)
    return c


def sparse_places(nc, cst, atoms, eaw, importance, mask_idx, table, place_i, total):
    W3 = 3 * E
    ZB = NB * W3
    PB = 8
    with Phase(nc, "sp") as ph:
        sb, sem = ph.sb, ph.sem
        eaw_sb = sb("eaw", [E, A])
        atoms_sb = sb("atoms", [A, NS])
        imp = sb("imp", [E, NS])
        idx_row = sb("idx_row", [P, NS], I32)
        idx_col = sb("idx_col", [P, NB], I32)
        row_f = sb("row_f", [P, NS])
        col_f = sb("col_f", [P, NB])
        zero = sb("zero", [P, 4096])
        stat = sb("stat", [E, 4])
        prob = sb("prob", [E, A])
        probT = sb("probT", [A, E])
        impT = sb("impT", [P, NB * E])
        val = sb("val", [P, NB * E])
        val2 = sb("val2", [P, NB * E])
        parts = sb("parts", [P, (NB - 1) * W3 + 2 * (ZB + (NB - 1) * W3)], BF16)
        zb16 = sb("zb16", [P, 512], BF16)
        before = sb("before16", [P, P], BF16)
        ones16 = sb("ones16", [P, 2], BF16)
        eq = [sb(f"eq{u}", [P, NS], BF16) for u in range(2)]
        eqd = [sb(f"eqd{u}", [P, P], BF16) for u in range(2)]
        acc = sb("acc", [P, NB, 2 * W3])
        earlier = sb("earlier", [P, NB])
        place_j = sb("place_j", [P, NB], I32)
        place_f = sb("place_f", [P, NB])
        spare_f = sb("spare_f", [P, NB])
        ps_eq = [ph.ps(f"ps_eq{n}", [P, PB, 2 * W3]) for n in range(NB // PB)]
        ps_imp = ph.ps("ps_imp", [P, 512])
        ps_dl = ph.ps("ps_dl", [P, 512])
        ps_dg = ph.ps("ps_dg", [P, 512])
        ps_p = ph.ps("ps_p", [P, 512])
        loaded, vec, act_s, ten, poo = sem("loaded"), sem("vec"), sem("act"), sem("ten"), sem("pool")
        eq_ready, eq_used, zeroed = sem("eq_ready"), sem("eq_used"), sem("zeroed")

        with nc.Block() as block:
            @block.sync
            def _(sp):
                sp.dma_start(eaw_sb[:], eaw).then_inc(loaded, 16)
                sp.dma_start(idx_row[:], mask_idx.rearrange("(o s) -> o s", o=1).broadcast_to([P, NS])).then_inc(loaded, 16)
                sp.dma_start(idx_col[:], mask_idx.rearrange("(b p) -> p b", p=P),
                             allow_slow_non_contiguous=True).then_inc(loaded, 16)
                sp.dma_start(imp[:], importance).then_inc(loaded, 16)
                sp.dma_start(atoms_sb[:], atoms).then_inc(loaded, 16)
                sp.wait_ge(vec, 1)
                flat = table[0:PLACES, :].rearrange("(n p k) e -> n p (k e)", n=4, p=P)
                for n in range(4):
                    sp.dma_start(flat[n], zero[:]).then_inc(zeroed, 16)

            @block.gpsimd
            def _(pool):
                st = Steps(pool, poo)
                st.did(pool.iota(spare_f[:], pattern=[[P, NB]], base=PLACES, channel_multiplier=1,
                                 allow_small_or_imprecise_dtypes=True))
                pool.wait_ge(zeroed, 64)

            @block.scalar
            def _(act):
                act.wait_ge(vec, 5)
                act.activation(prob[:], eaw_sb[:], ACT.Exp, bias=stat[:, 0:1], accum_out=stat[:, 1:2]).then_inc(act_s, 1)
                act.wait_ge(loaded, 80)
                act.activation(imp[:], imp[:], ACT.Sigmoid).then_inc(act_s, 1)

            @block.vector
            def _(dve):
                st = Steps(dve, vec)
                st.did(dve.memset(zero[:], 0.0))
                st.did(dve.memset(parts[:], 0.0))
                st.did(dve.memset(zb16[:], 0.0))
                st.did(dve.memset(ones16[:], 1.0))
                dve.wait_ge(loaded, 80)
                dve.tensor_reduce(stat[:, 0:1], eaw_sb[:], AX.X, ALU.max, negate=True).then_inc(vec, 1)
                st.n += 1
                st.did(dve.tensor_copy(before[:], cst["before"][:]))
                st.settle()
                ones_ramp = parts[:, ZB:ZB + (NB - 1) * W3].rearrange("p (m w) -> p m w", w=W3)
                st.did(dve.memset(ones_ramp[:, :, 0:1], 1.0))
                st.did(dve.tensor_copy(row_f[:], idx_row[:]))
                st.did(dve.tensor_copy(col_f[:], idx_col[:]))
                dve.wait_ge(act_s, 1)
                st.chain(dve.reciprocal(stat[:, 2:3], stat[:, 1:2]))
                st.did(dve.tensor_scalar(prob[:], prob[:], stat[:, 2:3], None, ALU.mult))
                dve.wait_ge(ten, 1)
                st.did(dve.tensor_copy(probT[:], ps_p[0:A, 0:E]))
                dve.wait_ge(ten, 2)
                st.did(dve.tensor_copy(impT[:], ps_imp[:, 0:NB * E]))
                dve.wait_ge(ten, 3)
                st.settle()
                st.chain(dve.tensor_tensor(val[:], ps_dl[:, 0:NB * E], impT[:], ALU.mult))
                pv = parts[:, 0:ZB].rearrange("p (b w) -> p b w", w=W3)
                vv = val[:].rearrange("p (b e) -> p b e", e=E)
                vv2 = val2[:].rearrange("p (b e) -> p b e", e=E)
                st.chain(dve.tensor_copy(pv[:, :, 0:E], vv))
                st.chain(dve.tensor_tensor(vv2, vv, pv[:, :, 0:E], ALU.subtract))
                st.chain(dve.tensor_copy(pv[:, :, E:2 * E], vv2))
                st.chain(dve.tensor_tensor(vv, vv2, pv[:, :, E:2 * E], ALU.subtract))
                st.chain(dve.tensor_copy(pv[:, :, 2 * E:3 * E], vv))
                dve.sem_inc(eq_used, 2)
                with dve.Fori(0, NB // 2) as pair:
                    for u in range(2):
                        dve.wait_ge(eq_used, pair * 2 + u + 1)
                        dve.tensor_scalar(eq[u][:], row_f[:], col_f[:, bass.ds(pair * 2 + u, 1)], None, ALU.is_equal)
                        dve.scalar_tensor_tensor(out=eqd[u][:], in0=row_f[:, bass.ds((pair * 2 + u) * P, P)],
                                                 scalar=col_f[:, bass.ds(pair * 2 + u, 1)], in1=before[:],
                                                 op0=ALU.is_equal, op1=ALU.mult).then_inc(eq_ready, 1)
                st.did(dve.tensor_scalar(place_i[:], idx_col[:], D - 1, 9, ALU.bitwise_and, ALU.logical_shift_left))
                st.chain(dve.tensor_scalar(place_j[:], idx_col[:], 9, None, ALU.logical_shift_right))
                st.chain(dve.tensor_tensor(place_i[:], place_i[:], place_j[:], ALU.bitwise_or))
                st.chain(dve.tensor_copy(place_f[:], place_i[:]))
                dve.wait_ge(poo, 1)
                st.chain(dve.tensor_tensor(place_f[:], place_f[:], spare_f[:], ALU.subtract))
                dve.wait_ge(ten, 4)
                for n in range(NB // PB):
                    st.did(dve.tensor_copy(acc[:, n * PB:(n + 1) * PB, :], ps_eq[n][:]))
                st.did(dve.tensor_copy(earlier[:], ps_dg[:, 0:NB]))
                st.settle()
                st.did(dve.tensor_tensor(earlier[:].unsqueeze(2), earlier[:].unsqueeze(2), acc[:, :, W3:W3 + 1], ALU.add))
                st.chain(dve.tensor_tensor(total[:], acc[:, :, 0:E], acc[:, :, E:2 * E], ALU.add))
                st.did(dve.tensor_tensor(total[:], total[:], acc[:, :, 2 * E:3 * E], ALU.add))
                st.chain(dve.scalar_tensor_tensor(out=place_f[:], in0=earlier[:], scalar=0.5, in1=place_f[:],
                                                  op0=ALU.is_lt, op1=ALU.mult))
                st.chain(dve.tensor_tensor(place_f[:], place_f[:], spare_f[:], ALU.add))
                dve.tensor_copy(place_i[:], place_f[:])

            @block.tensor
            def _(pe):
                pe.wait_ge(vec, 11)
                pe.transpose(ps_p[0:A, 0:E], prob[:], cst["ident"][0:E, 0:E]).then_inc(ten, 1)
                pe.wait_ge(act_s, 2)
                for b in range(NB):
                    t = pe.transpose(ps_imp[:, b * E:(b + 1) * E], imp[:, b * P:(b + 1) * P], cst["ident"][0:E, 0:E])
                t.then_inc(ten, 1)
                pe.wait_ge(vec, 12)
                for b in range(NB):
                    m = pe.matmul(ps_dl[:, b * E:(b + 1) * E], atoms_sb[:, b * P:(b + 1) * P], probT[:],
                                  start=True, stop=True)
                m.then_inc(ten, 1)
                for n in range(NB // PB):
                    pe.matmul(ps_eq[n][:], zb16[:, 0:P], zb16[:, 0:PB * 2 * W3], start=True, stop=False,
                              skip_group_check=True)
                with pe.Fori(0, NB // 2) as pair:
                    for u in range(2):
                        pe.wait_ge(eq_ready, pair * 2 + u + 1)
                        for b in range(NB):
                            dist = ZB + (NB - 1 - b) * W3
                            rhs = parts[:, bass.ds((pair * 2 + u) * W3, 2 * dist)].rearrange("p (two d) -> p two d", two=2)
                            pe.matmul(ps_eq[b // PB][:, b % PB, :], eq[u][:, b * P:(b + 1) * P], rhs[:, :, 0:W3],
                                      start=False, stop=False, skip_group_check=True)
                        pe.matmul(ps_dg[:, bass.ds(pair * 2 + u, 1)], eqd[u][:], ones16[:, 0:1],
                                  start=True, stop=True).then_inc(eq_used, 1)
                for n in range(NB // PB):
                    m = pe.matmul(ps_eq[n][:], zb16[:, 0:P], zb16[:, 0:PB * 2 * W3], start=False, stop=True,
                                  skip_group_check=True)
                m.then_inc(ten, 1)


def router(nc, cst, name, x, gate_w, gate, row_of, tile_tab, dispatched, M=None, m_store=None, spread=None):
    GT = 8
    HT = GT // 2
    NG = NT // GT
    NX = 3
    with Phase(nc, name) as ph:
        sb, sem = ph.sb, ph.sem
        xn = [sb(f"xn{v}", [P, GT, D]) for v in range(NX)]
        xT = [sb(f"xT{u}", [P, KC, 2 * P]) for u in range(2)]
        lT = sb("lT", [E, 2 * P])
        gw = sb("gw", [E, D])
        gwT = sb("gwT", [P, KC, E])
        bn = sb("bn", [P, HT, 6])
        mv = [sb(f"mv{h}", [P, HT, 2]) for h in range(2)]
        rstd = [sb(f"rstd{h}", [P, HT]) for h in range(2)]
        near = sb("near", [P, HT])
        eps = sb("eps", [P, 1])
        lg = sb("lg", [P, GT, E])
        rev = sb("rev", [P, GT, E])
        cand = sb("cand", [P, GT, E])
        best = sb("best", [P, GT])
        both = sb("both", [P, GT, E])
        chosen = sb("chosen", [P, 2, NT, E])
        top = sb("top", [P, 2, NT])
        keep = sb("keep", [P, E, GT + 1])
        counts = sb("counts", [P, E, GT + 1])
        upto = sb("upto", [P, E, GT + 1])
        prod = sb("prod", [P, 2, GT, E])
        sent_f = sb("sent_f", [P, 2, NT])
        sent = [sb(f"sent{u}", [P, 2, GT], I32) for u in range(2)]
        shift = sb("shift", [P, 2, NT])
        far = sb("far", [P, NT])
        w0 = sb("w0", [P, NT])
        region, pad_off, offset = sb("region", [P, E]), sb("pad_off", [P, E]), sb("offset", [P, E])
        count_i = sb("count_i", [P, E], I32)
        blocks, blocks_to, before_e, one_e = (sb(n, [P, E]) for n in ("blocks", "blocks_to", "before_e", "one_e"))
        pad = sb("pad", [P, E])
        pad_i = sb("pad_i", [P, E], I32)
        zrow = sb("zrow", [P, D])
        blk = sb("blk", [P, BLOCKS])
        over = sb("over", [P, E - 1, BLOCKS])
        te = sb("te", [P, BLOCKS])
        tb = sb("tb", [P, BLOCKS])
        ps_T = [ph.ps(f"ps_T{r}", [P, KC, P]) for r in range(4)]
        ps_lT = ph.ps("ps_lT", [E, 2 * P])
        ps_l = [ph.ps(f"ps_l{u}", [P, GT, E]) for u in range(2)]
        ps_c = ph.ps("ps_c", [P, 2, GT, E])
        loaded = [[sem(f"loaded{g}{h}") for h in range(2)] for g in range(NG)]
        gone = [[sem(f"gone{g}{h}") for h in range(2)] for g in range(NG)]
        made, bn_done, stats, logged, rsqrt, normed = (sem(n) for n in ("made", "bn", "stats", "logged", "rsqrt", "normed"))
        turned, copied, multiplied, taken, scored, pads, side = (
            sem(n) for n in ("turned", "copied", "multiplied", "taken", "scored", "pads", "side"))
        gw_in, gw_T, chose, counted, placed, vec, end, far_s = (sem(n) for n in (
            "gw_in", "gw_T", "chose", "counted", "placed", "vec", "end", "far"))
        m_in = sem("m_in")
        with nc.Block() as block:
            @block.sync
            def _(sp):
                src = x.rearrange("(g j p) d -> g p j d", g=2 * NG, p=P)

                def load(g):
                    for h in range(2):
                        if g >= NX:
                            sp.wait_ge(gone[g - NX][h], 32 * HT)
                        sp.dma_start(xn[g % NX][:, h * HT:(h + 1) * HT, :], src[2 * g + h]).then_inc(loaded[g][h], 16)

                def fetch(kc):
                    if M is not None:
                        sp.dma_start(M[:, kc].bitcast(F32), m_store[:, kc]).then_inc(m_in, 16)

                load(0)
                sp.dma_start(gw[:], gate_w).then_inc(gw_in, 16)
                load(1)
                load(2)
                fetch(0)
                fetch(1)
                load(3)
                fetch(2)
                fetch(3)
                if M is not None:
                    sp.wait_ge(m_in, 16 * KC)

            @block.gpsimd
            def _(pool):
                pool.memset(eps[:], LN_EPS).then_inc(made, 1)
                pool.iota(rev[:], pattern=[[0, GT], [-1, E]], base=E, channel_multiplier=0,
                          allow_small_or_imprecise_dtypes=True).then_inc(made, 1)
                pool.iota(region[:], pattern=[[REGION, E]], base=0, channel_multiplier=0,
                          allow_small_or_imprecise_dtypes=True).then_inc(made, 1)
                pool.iota(pad_off[:], pattern=[[0, E]], base=0, channel_multiplier=1,
                          allow_small_or_imprecise_dtypes=True).then_inc(made, 1)
                pool.iota(blk[:], pattern=[[1, BLOCKS]], base=0, channel_multiplier=0,
                          allow_small_or_imprecise_dtypes=True).then_inc(made, 1)
                pool.memset(zrow[:], 0.0).then_inc(made, 1)
                if spread is not None:
                    table, place_i, total = spread
                    for b in range(NB):
                        pool.indirect_dma_start(table, bass.IndirectOffsetOnAxis(ap=place_i[:, b:b + 1], axis=0),
                                                total[:, b, :], None).then_inc(side, 16)
                for g in range(NG):
                    u = g % 2
                    pool.wait_ge(placed, g + 1)
                    for j in range(GT):
                        for k in range(2):
                            pool.indirect_dma_start(dispatched, bass.IndirectOffsetOnAxis(ap=sent[u][:, k, j:j + 1], axis=0),
                                                    xn[g % NX][:, j, :], None).then_inc(gone[g][j // HT], 16)
                pool.wait_ge(placed, NG + 1)
                pool.wait_ge(made, 6)
                for e in range(E):
                    pool.indirect_dma_start(dispatched, bass.IndirectOffsetOnAxis(ap=pad_i[:, e:e + 1], axis=0),
                                            zrow[:], None).then_inc(pads, 16)
                pool.wait_ge(pads, 16 * E)
                for g in range(NG):
                    for h in range(2):
                        pool.wait_ge(gone[g][h], 32 * HT)
                if spread is not None:
                    pool.wait_ge(side, 16 * NB)

            @block.vector
            def _(dve):
                def take_stats(g):
                    for h in range(2):
                        n = (2 * g + h) * HT
                        dve.wait_ge(loaded[g][h], 16)
                        wait(dve, stats, n)
                        for j in range(HT):
                            dve.bn_stats(bn[:, j, :], xn[g % NX][:, h * HT + j, :]).then_inc(bn_done, 1)
                        wait(dve, normed, n - HT)
                        for j in range(HT):
                            if j == 0:
                                dve.wait_ge(bn_done, n + HT)
                            dve.bn_aggr(mv[h][:, j, :], bn[:, j, :]).then_inc(stats, 1)

                st = Steps(dve, vec)

                def norm(g):
                    for h in range(2):
                        dve.wait_ge(rsqrt, 2 * g + h + 1)
                        st.chain(dve.tensor_tensor(near[:], rstd[h][:], rstd[h][:], ALU.mult))
                        st.chain(dve.scalar_tensor_tensor(out=near[:], in0=mv[h][:, :, 1], scalar=LN_EPS, in1=near[:],
                                                          op0=ALU.add, op1=ALU.mult))
                        st.chain(dve.tensor_scalar(near[:], near[:], -0.5, 1.5, ALU.mult, ALU.add))
                        st.chain(dve.tensor_tensor(rstd[h][:], rstd[h][:], near[:], ALU.mult))
                        for j in range(HT):
                            t = xn[g % NX][:, h * HT + j, :]
                            dve.tensor_scalar(t, t, mv[h][:, j, 0:1], rstd[h][:, j:j + 1],
                                              ALU.subtract, ALU.mult).then_inc(normed, 1)

                def rank(g):
                    u, tiles = g % 2, slice(g * GT, (g + 1) * GT)
                    dve.wait_ge(scored, (g + 1) * GT // 2)
                    st.chain(dve.tensor_scalar(lg[:], ps_l[u][:], 50.0, -50.0, ALU.min, ALU.max))
                    for k in range(2):
                        oh, hi = chosen[:, k, tiles, :], top[:, k, tiles]
                        st.chain(dve.tensor_reduce(hi, lg[:], AX.X, ALU.max))
                        st.chain(dve.tensor_tensor(cand[:], lg[:], bc(hi, 2, E), ALU.is_equal))
                        st.chain(dve.tensor_tensor(cand[:], cand[:], rev[:], ALU.mult))
                        st.chain(dve.tensor_reduce(best[:], cand[:], AX.X, ALU.max))
                        st.chain(dve.tensor_tensor(oh, cand[:], bc(best[:], 2, E), ALU.is_equal))
                        if k == 0:
                            st.chain(dve.scalar_tensor_tensor(out=lg[:], in0=oh, scalar=-1000.0, in1=lg[:],
                                                              op0=ALU.mult, op1=ALU.add))
                    wait(dve, counted, g)
                    dve.tensor_tensor(both[:], chosen[:, 0, tiles, :], chosen[:, 1, tiles, :], ALU.add).then_inc(chose, 1)
                    dve.wait_ge(counted, g + 1)
                    st.chain(dve.tensor_copy(counts[:, :, 1:].rearrange("p e j -> p j e"), ps_c[:, 1]))
                    flat = lambda t: t[:].rearrange("p e j -> p (e j)")
                    st.chain(dve.tensor_tensor_scan(flat(upto), flat(keep), flat(counts), 0.0, ALU.mult, ALU.add))
                    st.chain(dve.tensor_copy(counts[:, :, 0], upto[:, :, GT]))
                    place = upto[:, :, 0:GT]
                    st.chain(dve.tensor_tensor(place, ps_c[:, 0].rearrange("p j e -> p e j"), place, ALU.add))
                    st.chain(dve.tensor_tensor(prod[:], chosen[:, :, tiles, :], bc(place.rearrange("p e j -> p j e"), 1, 2),
                                               ALU.mult))
                    st.chain(dve.tensor_reduce(sent_f[:, :, tiles], prod[:], AX.X, ALU.add))
                    if g >= 2:
                        for h in range(2):
                            dve.wait_ge(gone[g - 2][h], 32 * HT)
                    dve.tensor_copy(sent[u][:], sent_f[:, :, tiles]).then_inc(placed, 1)

                take_stats(0)
                norm(0)
                take_stats(1)
                dve.wait_ge(made, 5)
                st.did(dve.memset(keep[:], 1.0))
                st.did(dve.memset(one_e[:], 1.0))
                st.did(dve.tensor_copy(counts[:, :, 0], region[:]))
                st.settle()
                st.chain(dve.memset(keep[:, :, 0:1], 0.0))
                norm(1)
                for g in range(NG):
                    rank(g)
                    if g + 2 < NG:
                        take_stats(g + 2)
                        norm(g + 2)
                last = counts[:, :, 0]
                st.did(dve.tensor_tensor(pad[:], last, pad_off[:], ALU.add))
                st.chain(dve.tensor_tensor(blocks[:], last, region[:], ALU.subtract))
                dve.tensor_copy(pad_i[:], pad[:]).then_inc(placed, 1)
                st.chain(dve.tensor_scalar(count_i[:], blocks[:], float(P - 1), None, ALU.add))
                st.chain(dve.tensor_scalar(count_i[:], count_i[:], 7, None, ALU.logical_shift_right))
                st.chain(dve.tensor_copy(blocks[:], count_i[:]))
                st.chain(dve.tensor_tensor_scan(blocks_to[:], one_e[:], blocks[:], 0.0, ALU.mult, ALU.add))
                st.chain(dve.tensor_tensor(before_e[:], blocks_to[:], blocks[:], ALU.subtract))
                dve.tensor_tensor(far[:], top[:, 1, :], top[:, 0, :], ALU.subtract).then_inc(far_s, 1)
                st.chain(dve.scalar_tensor_tensor(out=offset[:], in0=before_e[:], scalar=float(P), in1=region[:],
                                                  op0=ALU.mult, op1=ALU.subtract))
                for g in range(NG):
                    tiles = slice(g * GT, (g + 1) * GT)
                    st.chain(dve.tensor_tensor(prod[:], chosen[:, :, tiles, :],
                                               offset[:].unsqueeze(1).unsqueeze(1).broadcast_to([P, 2, GT, E]), ALU.mult))
                    st.chain(dve.tensor_reduce(shift[:, :, tiles], prod[:], AX.X, ALU.add))
                st.chain(dve.tensor_tensor(row_of[:], sent_f[:], shift[:], ALU.add))
                bb = bc(blk[:], 1, E - 1)
                st.chain(dve.tensor_tensor(over[:], bb, bc(blocks_to[:, 0:E - 1], 2, BLOCKS), ALU.is_ge))
                st.chain(dve.tensor_reduce(te[:], over[:].rearrange("p e j -> p j e"), AX.X, ALU.add))
                st.chain(dve.tensor_tensor(over[:], over[:], bc(blocks[:, 0:E - 1], 2, BLOCKS), ALU.mult))
                st.chain(dve.tensor_reduce(tb[:], over[:].rearrange("p e j -> p j e"), AX.X, ALU.add))
                st.did(dve.tensor_copy(tile_tab[:, 0, :], te[0:1, :]))
                st.chain(dve.tensor_tensor(tb[:], blk[:], tb[:], ALU.subtract))
                st.chain(dve.scalar_tensor_tensor(out=tb[:], in0=blk[:], scalar=blocks_to[:, E - 1:E], in1=tb[:],
                                                  op0=ALU.is_lt, op1=ALU.mult))
                st.did(dve.tensor_scalar(te[:], te[:], float(REGION), None, ALU.mult))
                st.chain(dve.tensor_scalar(tb[:], tb[:], float(P), None, ALU.mult))
                st.chain(dve.tensor_tensor(tb[:], tb[:], te[:], ALU.add))
                st.chain(dve.tensor_copy(tile_tab[:, 1, :], tb[0:1, :]))
                dve.wait_ge(end, 1)
                st.chain(dve.tensor_scalar(w0[:], far[:], 1.0, None, ALU.add))
                st.chain(dve.reciprocal(w0[:], w0[:]))
                st.did(dve.tensor_scalar(gate[:, 0, :], w0[:], 0.5, None, ALU.mult))
                st.chain(dve.tensor_tensor(far[:], w0[:], far[:], ALU.mult))
                st.chain(dve.tensor_scalar(gate[:, 1, :], far[:], 0.5, None, ALU.mult))

            @block.tensor
            def _(pe):
                pe.wait_ge(gw_in, 16)
                for kc in range(KC):
                    m = pe.transpose(ps_T[1][:, kc, 0:E], gw[:, kc * P:(kc + 1) * P], cst["ident"][0:E, 0:E])
                m.then_inc(gw_T, 1)
                pe.wait_ge(gw_T, 2)

                def turn(n):
                    pe.wait_ge(normed, n + 1)
                    wait(pe, copied, n - 3)
                    for kc in range(KC):
                        m = pe.transpose(ps_T[n % 4][:, kc, :], xn[n // GT % NX][:, n % GT, kc * P:(kc + 1) * P],
                                         cst["ident"][:])
                    m.then_inc(turned, 1)

                def multiply(q):
                    pe.wait_ge(copied, 2 * q + 2)
                    wait(pe, taken, q)
                    for kc in range(KC):
                        m = pe.matmul(ps_lT[:], gwT[:, kc, :], xT[q % 2][:, kc, :], start=(kc == 0), stop=(kc == KC - 1))
                    m.then_inc(multiplied, 1)

                def turn_back(q):
                    pe.wait_ge(taken, q + 1)
                    for t in range(2):
                        n = 2 * q + t
                        m = pe.transpose(ps_l[n // GT % 2][:, n % GT, :], lT[:, t * P:(t + 1) * P], cst["ident"][0:E, 0:E])
                    m.then_inc(scored, 1)

                def count(g):
                    u = g % 2
                    pe.wait_ge(chose, g + 1)
                    wait(pe, placed, g)
                    pe.matmul(ps_c[:, 0], cst["before"][:], both[:], start=True, stop=True)
                    pe.matmul(ps_c[:, 1], cst["ones"][:], both[:], start=True, stop=True).then_inc(counted, 1)

                turn(0)
                turn(1)
                for q in range(NT // 2):
                    if q + 1 < NT // 2:
                        turn(2 * q + 2)
                        turn(2 * q + 3)
                    if q > 0:
                        turn_back(q - 1)
                    multiply(q)
                    if q > GT // 2 and q % (GT // 2) == 1:
                        count(q // (GT // 2) - 1)
                turn_back(NT // 2 - 1)
                count(NG - 1)

            @block.scalar
            def _(act):
                act.preload_act_table_set("natural_log_exp_and_others")
                act.wait_ge(made, 1)
                act.wait_ge(gw_T, 1)
                act.copy(gwT[:], ps_T[1][:, :, 0:E]).then_inc(gw_T, 1)
                def take_rstd(g):
                    for h in range(2):
                        n = 2 * g + h
                        act.wait_ge(stats, (n + 1) * HT)
                        wait(act, normed, (n - 1) * HT)
                        act.activation(rstd[h][:], mv[h][:, :, 1], ACT.Ln, bias=eps[:]).then_inc(logged, 1)
                        act.wait_ge(logged, n + 1)
                        act.activation(rstd[h][:], rstd[h][:], ACT.Exp, scale=-0.5).then_inc(rsqrt, 1)

                def take_logits(q):
                    act.wait_ge(multiplied, q + 1)
                    wait(act, scored, q)
                    act.copy(lT[:], ps_lT[:]).then_inc(taken, 1)

                take_rstd(0)
                for q in range(NT // 2):
                    for n in (2 * q, 2 * q + 1):
                        act.wait_ge(turned, n + 1)
                        wait(act, multiplied, q - 1)
                        act.copy(xT[q % 2][:, :, n % 2 * P:(n % 2 + 1) * P], ps_T[n % 4][:]).then_inc(copied, 1)
                    if q > 0:
                        take_logits(q - 1)
                    if q % (GT // 2) == 1 and 2 * q // GT + 1 < NG:
                        take_rstd(2 * q // GT + 1)
                take_logits(NT // 2 - 1)
                act.wait_ge(far_s, 1)
                act.activation(far[:], far[:], ACT.Exp).then_inc(end, 1)


def dense_experts(nc, cst, table, W, M, m_store):
    with Phase(nc, "md") as ph:
        sb, sem = ph.sb, ph.sem
        w_sb = sb("w", [P, KC, D])
        tb = [sb(f"tb{u}", [P, D, E]) for u in range(2)]
        ps_w = [ph.ps(f"ps_w{kc}", [P, D]) for kc in range(KC)]
        w_in, turned, added, high, low, stored = (sem("w_in"), sem("turned"), sem("added"), sem("high"), sem("low"),
                                                  sem("stored"))
        tb_in = [sem(f"tb_in{u}") for u in range(2)]
        with nc.Block() as block:
            @block.sync
            def _(sp):
                sp.dma_start(w_sb[:], W.rearrange("(a p) c -> p a c", p=P)).then_inc(w_in, 16)
                for kc in range(KC):
                    if kc >= 2:
                        sp.wait_ge(low, kc - 1)
                    sp.dma_start(tb[kc % 2][:], table[kc * P * D:(kc + 1) * P * D, :]
                                 .rearrange("(p r) e -> p (r e)", p=P)).then_inc(tb_in[kc % 2], 16)
                for kc in range(KC):
                    sp.wait_ge(low, kc + 1)
                    sp.dma_start(m_store[:, kc], M[:, kc].bitcast(F32)).then_inc(stored, 16)
                sp.wait_ge(stored, 16 * KC)

            @block.tensor
            def _(pe):
                pe.wait_ge(w_in, 16)
                for kc in range(KC):
                    for rb in range(KC):
                        m = pe.transpose(ps_w[kc][:, rb * P:(rb + 1) * P], w_sb[:, rb, kc * P:(kc + 1) * P], cst["ident"][:])
                    m.then_inc(turned, 1)

            @block.vector
            def _(dve):
                for kc in range(KC):
                    t = tb[kc % 2][:].rearrange("p r e -> p e r")
                    dve.wait_ge(tb_in[kc % 2], 16 * (kc // 2 + 1))
                    dve.wait_ge(turned, kc + 1)
                    dve.tensor_tensor(t, bc(ps_w[kc][:], 1, E), t, ALU.add).then_inc(added, 1)
                    dve.wait_ge(high, kc + 1)
                    dve.tensor_tensor(M[:, kc, 1], t, M[:, kc, 0].bitcast(F32), ALU.subtract).then_inc(low, 1)

            @block.scalar
            def _(act):
                for kc in range(KC):
                    act.wait_ge(added, kc + 1)
                    act.copy(M[:, kc, 0], tb[kc % 2][:].rearrange("p r e -> p e r")).then_inc(high, 1)


def split_matmul(pe, out, lhs, rhs, first=True, last=True):
    for n, (a, b) in enumerate(((0, 0), (0, 1), (1, 0))):
        m = pe.matmul(out, lhs[a], rhs[b], start=first and n == 0, stop=last and n == 2)
    return m


def experts(nc, cst, name, M, tile_tab, dispatched, routed):
    with Phase(nc, name) as ph:
        sb, sem = ph.sb, ph.sem
        DEEP = 4
        xt = [sb(f"xt{r}", [P, D]) for r in range(DEEP)]
        xT = [[sb(f"xT{u}{h}", [P, KC, P], F32R) for h in range(2)] for u in range(2)]
        yt = [sb(f"yt{u}", [P, D]) for u in range(2)]
        ps_T = [ph.ps(f"ps_T{u}", [P, KC, P]) for u in range(2)]
        ps_y = [ph.ps(f"ps_y{u}", [P, D]) for u in range(2)]
        xt_in = [sem(f"xt_in{r}") for r in range(DEEP)]
        y_out = [sem(f"y_out{u}") for u in range(2)]
        turned, high, low, multiplied, y_ready = (sem("turned"), sem("high"), sem("low"), sem("multiplied"), sem("y_ready"))
        m_in = [sem(f"m_in{kc}") for kc in range(KC)]
        QB = BLOCKS // DEEP
        with nc.Block() as block:
            @block.sync
            def _(sp):
                for u in range(2):
                    sp.sem_inc(y_out[u], 16)

                def load(r, n):
                    row = sp.snap(sp.value_load(tile_tab[0:1, 1, bass.ds(n, 1)], min_val=0,
                                                max_val=(E - 1) * REGION + TOK))
                    sp.wait_ge(turned, n + 1)
                    sp.dma_start(xt[r][:], dispatched[bass.ds(row, P), :]).then_inc(xt_in[r], 16)

                def store(u, n):
                    row = sp.snap(n * P)
                    sp.wait_ge(y_ready, n + 3)
                    sp.dma_start(routed[bass.ds(row, P), :], yt[u][:]).then_inc(y_out[u], 16)

                for r in range(DEEP):
                    load(r, r)
                with sp.Fori(0, QB - 1) as quad:
                    for r in range(DEEP):
                        store(r % 2, quad * DEEP + r)
                        load(r, quad * DEEP + DEEP + r)
                for r in range(DEEP):
                    store(r % 2, BLOCKS - DEEP + r)
                for u in range(2):
                    sp.wait_ge(y_out[u], 16 * (BLOCKS // 2 + 1))

            def turn(pe, r, n, quad):
                pe.wait_ge(xt_in[r], (quad + 1) * 16)
                pe.wait_ge(low, n + 1)
                for kc in range(KC):
                    m = pe.transpose(ps_T[r % 2][:, kc, :], xt[r][:, kc * P:(kc + 1) * P], cst["ident"][:])
                m.then_inc(turned, 1)

            def multiply(pe, u, n):
                e = pe.value_load(tile_tab[0:1, 0, bass.ds(n, 1)] if not isinstance(n, int)
                                  else tile_tab[0:1, 0, n:n + 1], min_val=0, max_val=E - 1)
                pe.wait_ge(low, n + 3)
                pe.wait_ge(y_ready, n + 1)
                for kc in range(KC):
                    m = split_matmul(pe, ps_y[u][:].unsqueeze(1), [xT[u][h][:, kc, :] for h in range(2)],
                                     [M[:, kc, h, bass.ds(e, 1), :] for h in range(2)], kc == 0, kc == KC - 1)
                m.then_inc(multiplied, 1)

            @block.tensor
            def _(pe):
                pe.sem_inc(turned, DEEP)
                pe.sem_inc(multiplied, 2)
                turn(pe, 0, 0, 0)
                with pe.Fori(0, QB - 1) as quad:
                    for r in range(DEEP):
                        n = quad * DEEP + r
                        turn(pe, (r + 1) % DEEP, n + 1, quad + (r + 1) // DEEP)
                        multiply(pe, r % 2, n)
                for r in range(DEEP):
                    n = BLOCKS - DEEP + r
                    if r + 1 < DEEP:
                        turn(pe, r + 1, n + 1, QB - 1)
                    multiply(pe, r % 2, n)

            @block.vector
            def _(dve):
                dve.sem_inc(low, 2)
                with dve.Fori(0, BLOCKS // 2) as pair:
                    for u in range(2):
                        n = pair * 2 + u
                        dve.wait_ge(high, n + 1)
                        dve.tensor_tensor(xT[u][1][:], ps_T[u][:], xT[u][0][:].bitcast(F32), ALU.subtract).then_inc(low, 1)

            @block.scalar
            def _(act):
                def take_high(u, n):
                    act.wait_ge(turned, n + 1 + DEEP)
                    act.wait_ge(multiplied, n + 1)
                    act.copy(xT[u][0][:], ps_T[u][:]).then_inc(high, 1)

                def take_y(u, n, pair):
                    act.wait_ge(multiplied, n + 3)
                    act.wait_ge(y_out[u], pair * 16 + 16)
                    act.copy(yt[u][:], ps_y[u][:]).then_inc(y_ready, 1)

                act.sem_inc(y_ready, 2)
                take_high(0, 0)
                with act.Fori(0, BLOCKS // 2 - 1) as pair:
                    for u in range(2):
                        n = pair * 2 + u
                        take_high(1 - u, n + 1)
                        take_y(u, n, pair)
                take_high(1, BLOCKS - 1)
                for u in range(2):
                    take_y(u, BLOCKS - 2 + u, BLOCKS // 2 - 1)


def combine(nc, name, x, routed, gate, row_of, out):
    with Phase(nc, name) as ph:
        sb, sem = ph.sb, ph.sem
        xt = [sb(f"xt{u}", [P, D]) for u in range(2)]
        y = [[sb(f"y{u}{k}", [P, D]) for k in range(2)] for u in range(2)]
        s = [sb(f"s{u}", [P, D]) for u in range(2)]
        res = [sb(f"res{u}", [P, D]) for u in range(2)]
        idx = [sb(f"idx{u}", [P, 2], I32) for u in range(2)]
        x_in = [sem(f"x_in{u}") for u in range(2)]
        y_in = [sem(f"y_in{u}") for u in range(2)]
        out_s = [sem(f"out{u}") for u in range(2)]
        idx_in, used, first, ordered = sem("idx_in"), sem("used"), sem("first"), sem("ordered")
        x_v = x.rearrange("(j p) d -> j p d", p=P)
        out_v = out.rearrange("(j p) d -> j p d", p=P)
        with nc.Block() as block:
            @block.sync
            def _(sp):
                for u in range(2):
                    sp.sem_inc(out_s[u], 16)
                with sp.Fori(0, NT // 2) as pair:
                    for u in range(2):
                        j = pair * 2 + u
                        sp.wait_ge(used, j + 1)
                        sp.dma_start(xt[u][:], x_v[bass.ds(j, 1)].rearrange("a p d -> (a p) d")).then_inc(x_in[u], 16)

            @block.gpsimd
            def _(pool):
                with pool.Fori(0, NT // 2) as pair:
                    for u in range(2):
                        j = pair * 2 + u
                        pool.wait_ge(used, j + 1)
                        pool.tensor_copy(idx[u][:].unsqueeze(2), row_of[:, :, bass.ds(j, 1)]).then_inc(idx_in, 1)
                        pool.wait_ge(idx_in, j + 1)
                        pool.sem_inc(ordered, 1)
                        for k in range(2):
                            pool.indirect_dma_start(y[u][k][:], None, routed,
                                                    bass.IndirectOffsetOnAxis(ap=idx[u][:, k:k + 1], axis=0)).then_inc(y_in[u], 16)

            @block.vector
            def _(dve):
                dve.sem_inc(used, 2)
                with dve.Fori(0, NT // 2) as pair:
                    for u in range(2):
                        j = pair * 2 + u
                        dve.wait_ge(y_in[u], (pair + 1) * 32)
                        dve.wait_ge(x_in[u], (pair + 1) * 16)
                        dve.scalar_tensor_tensor(out=s[u][:].unsqueeze(1), in0=y[u][0][:].unsqueeze(1), scalar=gate[:, 0, bass.ds(j, 1)],
                                                 in1=xt[u][:].unsqueeze(1), op0=ALU.mult, op1=ALU.add).then_inc(first, 1)
                        dve.wait_ge(first, j + 1)
                        dve.wait_ge(out_s[u], (pair + 1) * 16)
                        dve.scalar_tensor_tensor(out=res[u][:], in0=y[u][1][:], scalar=gate[:, 1, bass.ds(j, 1)],
                                                 in1=s[u][:], op0=ALU.mult, op1=ALU.add).then_inc(used, 1)

            @block.scalar
            def _(act):
                with act.Fori(0, NT // 2) as pair:
                    for u in range(2):
                        j = pair * 2 + u
                        act.wait_ge(used, j + 3)
                        act.dma_start(out_v[bass.ds(j, 1)].rearrange("a p d -> (a p) d"), res[u][:]).then_inc(out_s[u], 16)
                for u in range(2):
                    act.wait_ge(out_s[u], 16 * (NT // 2 + 1))


def wait(eng, sem, n):
    if not (isinstance(n, int) and n <= 0):
        eng.wait_ge(sem, n)


def col(ap, t):
    return ap[:, t:t + 1] if isinstance(t, int) else ap[:, bass.ds(t, 1)]


def pipeline(eng, step, lead):
    first, last = 4, NT - 4
    for i in range(lead, first):
        step(i, i % 4, i // 4)
    with eng.Fori(0, (last - first) // 4) as quad:
        for s in range(4):
            step(quad * 4 + (first + s), s, quad + first // 4)
    for i in range(last, NT + 2):
        step(i, i % 4, i // 4)


def inside(t):
    return not isinstance(t, int) or 0 <= t < NT


def attention(nc, cst, x, routed, gate, row_of, w, base, h2T):
    QK, V, G, O = range(4)
    HG = 4
    with Phase(nc, "at", recycle=True) as ph:
        sb, sem = ph.sb, ph.sem
        names = ("ws_scaled w_high w_low w_done consts "
                 "s x1 bn bn_ok mv ve rstd y t1 t2 r2 h hT_t hT_hi hT_lo low low_sb gate_p z ab ez lz ls sig gs bs dec "
                 "eb enb es decay qe ke kd qk_t keT qbd0 qbd1 v v_sb u_p s1 s2 s_tmp a0 a1 am0 am1 qk o osq ss ms8 r8 on og "
                 "og_t ogT_hi ogT_lo wo x2 sq msd rh2 h2 h2_t h2_hi h2_lo base idx_in idx_ok").split()
        S = {n: sem(n) for n in names}
        x_in = [sem(f"x_in{u}") for u in range(2)]
        y_in = [sem(f"y_in{u}") for u in range(2)]
        h_out = [sem(f"h_out{u}") for u in range(2)]
        b_out = [sem(f"b_out{u}") for u in range(2)]
        w_in = [sem(f"w_in{u}") for u in range(2)]
        small_in = sem("small_in")
        wh = [[sb(f"w{n}{h}", [P, KC, D], F32R) for h in range(2)] for n in range(4)]
        w1 = sb("w1f", [P, KC, LOW])
        w1h = [sb(f"w1h{h}", [P, KC, LOW], F32R) for h in range(2)]
        w2b = sb("w2b", [LOW + 1, KEY])
        n1, n1q = sb("n1", [P, KC]), sb("n1q", [P, KC])
        gn = sb("gn", [P, 1])
        stage = [sb(f"stage{u}", [P, KC, D]) for u in range(2)]
        cum16, suf16, causal = sb("cum16", [P, P]), sb("suf16", [P, P]), sb("causal", [P, P])
        chunk16, hmask, keep = sb("chunk16", [P, 2]), sb("hmask", [P, HG, P]), sb("keep", [P, NT // 4])
        power = sb("power", [P, H])
        two = lambda n, s, dt=F32: [sb(f"{n}{u}", s, dt) for u in range(2)]
        xt, s_, h, v_sb, gs, og, x2, h2, bt = (two(n, [P, D]) for n in
                                               "xt s h v gs og x2 h2 bt".split())
        h2T_sb = two("h2T", [P, 2, KC, P], F32R)
        yk = [two(f"yk{k}_", [P, D]) for k in range(2)]
        x1 = [stage[0][:, r, :] for r in range(4)]
        y = [stage[1][:, r, :] for r in range(4)]
        idx = two("idx", [P, 2], I32)
        bn, mv, ve, t1, t2, rstd, r2 = (two(n, s) for n, s in (("bn", [P, 6]), ("mv", [P, 2]), ("ve", [P, 1]),
                                        ("t1", [P, 1]), ("t2", [P, 1]), ("rstd", [P, 1]), ("r2", [P, 1])))
        hT = [two(f"hT{hf}_", [P, KC, P], F32R) for hf in range(2)]
        ogT = [sb(f"ogT{hf}", [P, KC, P], F32R) for hf in range(2)]
        low = two("low", [LOW + 1, P])
        ab, ez, lz = sb("ab", [P, KEY + D]), sb("ez", [P, KEY + D]), sb("lz", [P, KEY + D])
        ls = two("ls", [P, KEY + D])
        sig = sb("sig", [P, D])
        eb, enb, es = sb("eb", [P, KEY]), sb("enb", [P, KEY]), sb("es", [P, KEY])
        decay = sb("decay", [P, 2, 2])
        qe, ke = sb("qe", [P, KEY]), sb("ke", [P, KEY])
        kd = two("kd", [P, KEY])
        keT, qbd = sb("keT", [P, 2, P]), sb("qbd", [P, 2, HG, P])
        am = sb("am", [P, H, P])
        state = [sb(f"state{n}", [P, 2, HV]) for n in range(4)]
        s_tmp = sb("s_tmp", [P, 2, HV])
        osq, on = sb("osq", [P, D]), sb("on", [P, D])
        ss, ms8, r8 = sb("ss", [P, H]), sb("ms8", [P, H]), sb("r8", [P, H])
        sq, sqs, msd, rh2 = sb("sq", [P, D]), sb("sqs", [P, 1]), sb("msd", [P, 1]), sb("rh2", [P, 1])
        ps_T = ph.ps("ps_T", [P, KC, P])
        ps_qk = ph.ps("ps_qk", [P, D])
        ps_v = ph.ps("ps_v", [P, D])
        ps_zg = ph.ps("ps_zg", [P, 2 * D])
        ps_bs = ph.ps("ps_bs", [P, D])
        ps_a = [ph.ps(f"ps_a{g}", [P, HG, P]) for g in range(2)]
        ps_low, ps_dec = ps_zg[0:LOW, 0:P], ps_a[1][:, 0, 0:4]
        ps_z, ps_g, zg = ps_zg[:, D - KEY:D], ps_zg[:, D:2 * D], ps_zg[:, D - KEY:2 * D]
        ps_u = ps_qk[:, 0:4 * HV].rearrange("p (c g v) -> p c g v", c=2, g=2)

        w_src = [(w["wq"], w["wk"]), (w["wv"],), (w["wg"],), (w["wo"],)]
        W_ARRIVED = (32, 16, 48, 32)

        def w_scale(n, kc):
            if n == QK:
                return (slice(0, KEY), n1q[:, kc:kc + 1]), (slice(KEY, 2 * KEY), n1[:, kc:kc + 1])
            return (slice(0, D), gn[:, 0:1] if n == O else n1[:, kc:kc + 1]),

        x_v = x.rearrange("(j p) d -> j p d", p=P)
        base_v = base.rearrange("(j p) d -> j p d", p=P)

        def tile_of(ap, t):
            return ap[t] if isinstance(t, int) else ap[bass.ds(t, 1)].rearrange("a p d -> (a p) d")

        with nc.Block() as block:
            @block.sync
            def _(sp):
                sp.dma_start(w1[:], w["w1"].rearrange("(kc p) n -> p kc n", p=P)).then_inc(small_in, 16)
                sp.dma_start(w2b[0:LOW, :], w["w2"]).then_inc(small_in, 16)
                sp.dma_start(w2b[LOW:LOW + 1, :], w["gk_b"].rearrange("(o n) -> o n", o=1)).then_inc(small_in, 16)
                sp.dma_start(n1[:], w["norm1_w"].rearrange("(kc p) -> p kc", p=P),
                             allow_slow_non_contiguous=True).then_inc(small_in, 16)
                for c in range(2):
                    sp.dma_start(gn[c * HV:(c + 1) * HV, :], w["gnorm_w"].rearrange("(v o) -> v o", o=1)).then_inc(small_in, 16)
                for n in range(4):
                    if n >= 2:
                        sp.wait_ge(S["w_low"], n - 1)
                    at = 0
                    for src in w_src[n]:
                        cols = src.shape[1]
                        sp.dma_start(stage[n % 2][:, :, at:at + cols],
                                     src.rearrange("(kc p) n -> p kc n", p=P)).then_inc(w_in[n % 2], 16)
                        at += cols

                def step(i, r, q):
                    t = i + 3
                    if inside(t):
                        row = t if isinstance(t, int) else sp.snap(t)
                        wait(sp, S["s"], t - 1)
                        sp.dma_start(xt[(r + 3) % 2][:], tile_of(x_v, row)).then_inc(x_in[(r + 3) % 2], 16)
                    t = i - 2
                    if inside(t):
                        row = t * P if isinstance(t, int) else sp.snap(t * P)
                        dst = h2T[:, :, :, row:row + P] if isinstance(t, int) else h2T[:, :, :, bass.ds(row, P)]
                        wait(sp, S["h2_lo"], t + 1)
                        sp.dma_start(dst, h2T_sb[r % 2][:].bitcast(F32)).then_inc(h_out[r % 2], 16)
                    t = i - 1
                    if inside(t):
                        row = t if isinstance(t, int) else sp.snap(t)
                        wait(sp, S["base"], t + 1)
                        sp.dma_start(tile_of(base_v, row), bt[(r + 1) % 2][:]).then_inc(b_out[(r + 1) % 2], 16)
                pipeline(sp, step, -3)
                for u in range(2):
                    sp.wait_ge(h_out[u], 16 * NT // 2)
                    sp.wait_ge(b_out[u], 16 * NT // 2)

            @block.gpsimd
            def _(pool):
                made = Steps(pool, S["consts"])

                def ms(ap, v):
                    made.chain(pool.memset(ap, v))
                for ap, v in ((cum16, 1 / 16), (suf16, 1 / 16), (causal, 1.0), (chunk16, 0.0), (hmask, 0.0),
                              (keep, 1.0), (power, -0.5), (low[0], 1.0), (low[1], 1.0), (state[0], 0.0), (kd[0], 0.0), (kd[1], 0.0)):
                    ms(ap[:], v)
                for m, sign in ((cum16, 1), (causal, 1), (suf16, -1)):
                    made.chain(pool.affine_select(out=m[:], in_=m[:], compare_op=ALU.is_ge if sign > 0 else ALU.is_gt,
                                                  fill=0.0, base=0, pattern=[[sign, P]], channel_multiplier=-sign))
                ms(cum16[0:CHUNK, CHUNK:P], 0.0)
                ms(causal[0:CHUNK, CHUNK:P], 0.0)
                ms(suf16[CHUNK:P, 0:CHUNK], 0.0)
                for c in range(2):
                    ms(chunk16[c * CHUNK:(c + 1) * CHUNK, c:c + 1], 1 / 16)
                for n in range(HG):
                    ms(hmask[n * HK:(n + 1) * HK, n, :], 1.0)
                ms(keep[:].rearrange("p (a b) -> p a b", b=TILES_B // 4)[:, :, 0:1], 0.0)

                def step(i, r, q):
                    t = i - 1
                    if inside(t):
                        wait(pool, S["ms8"], t + 1)
                        pool.tensor_tensor(r8[:], ms8[:], power[:, 0:H], ALU.pow).then_inc(S["r8"], 1)
                    t = i + 3
                    if inside(t):
                        u = (r + 3) % 2
                        wait(pool, S["x1"], t - 1)
                        src = row_of[:, :, t:t + 1] if isinstance(t, int) else row_of[:, :, bass.ds(t, 1)]
                        pool.tensor_copy(idx[u][:].unsqueeze(2), src).then_inc(S["idx_in"], 1)
                        wait(pool, S["idx_in"], t + 1)
                        pool.sem_inc(S["idx_ok"], 1)
                        for k in range(2):
                            pool.indirect_dma_start(yk[k][u][:], None, routed,
                                                    bass.IndirectOffsetOnAxis(ap=idx[u][:, k:k + 1], axis=0)).then_inc(y_in[u], 16)
                    t = i + 2
                    if inside(t):
                        u = r % 2
                        wait(pool, S["ve"], t + 1)
                        pool.tensor_tensor(rstd[u][:], ve[u][:], power[:, 0:1], ALU.pow).then_inc(S["rstd"], 1)
                        wait(pool, S["t2"], t + 1)
                        pool.tensor_tensor(r2[u][:], t2[u][:], power[:, 0:1], ALU.pow).then_inc(S["r2"], 1)
                    t = i - 1
                    if inside(t):
                        u = (r + 1) % 2
                        wait(pool, S["x2"], t + 1)
                        wait(pool, b_out[u], (t + (r + 1) % 2 * -1) * 8)
                        pool.tensor_tensor(bt[u][:], x1[(r + 3) % 4], x2[u][:], ALU.add).then_inc(S["base"], 1)
                        wait(pool, S["msd"], i)
                        pool.tensor_tensor(rh2[:], msd[:], power[:, 0:1], ALU.pow).then_inc(S["rh2"], 1)
                pipeline(pool, step, -3)

            @block.scalar
            def _(act):
                act.preload_act_table_set("natural_log_exp_and_others")
                act.wait_ge(S["ws_scaled"], 1)
                for n in range(4):
                    act.wait_ge(w_in[n % 2], W_ARRIVED[n])
                    for kc in range(KC):
                        for cols, scale in w_scale(n, kc):
                            op = act.activation(wh[n][0][:, kc, cols], stage[n % 2][:, kc, cols], ACT.Copy, scale=scale)
                    op.then_inc(S["w_high"], 1)
                for kc in range(KC):
                    op = act.activation(w1h[0][:, kc], w1[:, kc], ACT.Copy, scale=n1[:, kc:kc + 1])
                op.then_inc(S["w_high"], 1)

                def step(i, r, q):
                    u, nu = r % 2, (r + 1) % 2
                    if inside(i - 1):
                        wait(act, S["o"], i)
                        wait(act, S["ss"], i - 1)
                        act.activation(osq[:], ps_v[:], ACT.Square).then_inc(S["osq"], 1)
                    n = i + 1
                    if inside(n):
                        wait(act, S["hT_t"], n + 1)
                        wait(act, S["v"], n - 1)
                        wait(act, S["qk"], n - 1)
                        act.copy(hT[0][nu][:], ps_T[:]).then_inc(S["hT_hi"], 1)
                    if inside(i):
                        wait(act, S["bs"], i + 1)
                        wait(act, S["kd"], i)
                        act.activation(eb[:], ps_bs[:, 0:KEY], ACT.Exp).then_inc(S["eb"], 1)
                        act.activation(enb[:], ps_bs[:, 0:KEY], ACT.Exp, scale=-1.0).then_inc(S["enb"], 1)
                        act.activation(es[:], ps_bs[:, KEY:2 * KEY], ACT.Exp).then_inc(S["es"], 1)
                        wait(act, S["dec"], i + 1)
                        wait(act, S["s2"], i)
                        act.activation(decay[:].rearrange("p g c -> p (g c)"), ps_dec, ACT.Exp).then_inc(S["decay"], 1)
                    if inside(n):
                        wait(act, S["low"], n + 1)
                        wait(act, S["z"], n - 1)
                        act.copy(low[nu][0:LOW, :], ps_low).then_inc(S["low_sb"], 1)
                    t = i - 2
                    if inside(t):
                        wait(act, S["h2_t"], t + 1)
                        wait(act, h_out[u], (t - r % 2) * 8)
                        act.copy(h2T_sb[u][:, 0], ps_T[:]).then_inc(S["h2_hi"], 1)
                    if inside(n):
                        wait(act, S["z"], n + 1)
                        wait(act, S["gate_p"], n + 1)
                        wait(act, S["ez"], n)
                        act.activation(ab[:], zg, ACT.Abs).then_inc(S["ab"], 1)
                        wait(act, S["ab"], n + 1)
                        wait(act, S["lz"], n)
                        act.activation(ez[:], ab[:], ACT.Exp, scale=-1.0).then_inc(S["ez"], 1)
                        wait(act, S["ez"], n + 1)
                        wait(act, S["ls"], n)
                        act.activation(lz[:], ez[:], ACT.Ln, bias=1.0).then_inc(S["lz"], 1)
                    if inside(i):
                        wait(act, S["qk_t"], i + 1)
                        wait(act, S["a1"], i)
                        act.copy(keT[:], ps_T[:, 2:4, :]).then_inc(S["keT"], 1)
                    if inside(n):
                        wait(act, S["ls"], n + 1)
                        wait(act, S["gs"], n)
                        act.activation(sig[:], ls[nu][:, KEY:], ACT.Exp).then_inc(S["sig"], 1)
                        wait(act, S["v"], n + 1)
                        wait(act, S["o"], n - 1)
                        act.copy(v_sb[nu][:], ps_v[:]).then_inc(S["v_sb"], 1)
                    if inside(i - 1):
                        wait(act, S["og_t"], i)
                        wait(act, S["wo"], i - 1)
                        act.copy(ogT[0][:], ps_T[:]).then_inc(S["ogT_hi"], 1)
                        wait(act, S["x2"], i)
                        wait(act, S["msd"], i - 1)
                        act.activation(sq[:], x2[nu][:], ACT.Square, accum_out=sqs[:]).then_inc(S["sq"], 1)
                pipeline(act, step, -1)

            @block.vector
            def _(dve):
                dve.wait_ge(small_in, 96)
                dve.tensor_scalar(n1q[:], n1[:], float(HK) ** -0.5, None, ALU.mult).then_inc(S["ws_scaled"], 1)
                dve.wait_ge(S["ws_scaled"], 1)
                for n in range(4):
                    dve.wait_ge(w_in[n % 2], W_ARRIVED[n])
                    dve.wait_ge(S["w_high"], n + 1)
                    for kc in range(KC):
                        for cols, scale in w_scale(n, kc):
                            op = dve.scalar_tensor_tensor(out=wh[n][1][:, kc, cols], in0=stage[n % 2][:, kc, cols], scalar=scale,
                                                          in1=wh[n][0][:, kc, cols].bitcast(F32), op0=ALU.mult, op1=ALU.subtract)
                    op.then_inc(S["w_low"], 1)
                dve.wait_ge(S["w_high"], 5)
                for kc in range(KC):
                    op = dve.scalar_tensor_tensor(out=w1h[1][:, kc], in0=w1[:, kc], scalar=n1[:, kc:kc + 1],
                                                  in1=w1h[0][:, kc].bitcast(F32), op0=ALU.mult, op1=ALU.subtract)
                op.then_inc(S["w_low"], 1)
                dve.wait_ge(S["consts"], 25)

                def step(i, r, q):
                    u, nu = r % 2, (r + 1) % 2
                    n, j, m = i + 1, i - 1, i + 2
                    if inside(n):
                        wait(dve, S["hT_hi"], n + 1)
                        dve.tensor_tensor(hT[1][nu][:], ps_T[:], hT[0][nu][:].bitcast(F32), ALU.subtract).then_inc(S["hT_lo"], 1)
                    if inside(j):
                        wait(dve, S["osq"], j + 1)
                        dve.tensor_reduce(ss[:], osq[:].rearrange("p (h v) -> p h v", h=H), AX.X, ALU.add).then_inc(S["ss"], 1)
                        wait(dve, S["ss"], j + 1)
                        wait(dve, S["r8"], j)
                        dve.tensor_scalar(ms8[:], ss[:], 1.0 / HV, RMS_EPS, ALU.mult, ALU.add).then_inc(S["ms8"], 1)
                    if inside(i):
                        wait(dve, S["qk"], i + 1)
                        wait(dve, S["eb"], i + 1)
                        wait(dve, S["qk_t"], i)
                        dve.tensor_tensor(qe[:], ps_qk[:, 0:KEY], eb[:], ALU.mult).then_inc(S["qe"], 1)
                        wait(dve, S["enb"], i + 1)
                        dve.tensor_tensor(ke[:], ps_qk[:, KEY:], enb[:], ALU.mult).then_inc(S["ke"], 1)
                        wait(dve, S["es"], i + 1)
                        wait(dve, S["u_p"], i)
                        for c in range(2):
                            rows = slice(c * CHUNK, (c + 1) * CHUNK)
                            op = dve.tensor_tensor(kd[c][rows], ps_qk[rows, KEY:], es[rows], ALU.mult)
                        op.then_inc(S["kd"], 1)
                    if inside(j):
                        wait(dve, S["r8"], j + 1)
                        wait(dve, S["og"], j)
                        dve.tensor_tensor(on[:].rearrange("p (h v) -> p h v", h=H), ps_v[:].rearrange("p (h v) -> p h v", h=H),
                                          bc(r8[:], 2, HV), ALU.mult).then_inc(S["on"], 1)
                        wait(dve, S["on"], j + 1)
                        wait(dve, S["og_t"], j - 1)
                        dve.tensor_tensor(og[nu][:], on[:], gs[nu][:], ALU.mult).then_inc(S["og"], 1)
                    if inside(i - 2):
                        wait(dve, S["h2_hi"], i - 1)
                        dve.tensor_tensor(h2T_sb[u][:, 1], ps_T[:], h2T_sb[u][:, 0].bitcast(F32), ALU.subtract).then_inc(S["h2_lo"], 1)
                    if inside(n):
                        wait(dve, S["lz"], n + 1)
                        wait(dve, S["dec"], n - 1)
                        dve.scalar_tensor_tensor(out=ls[nu][:], in0=zg, scalar=0.0, in1=lz[:],
                                                 op0=ALU.min, op1=ALU.subtract).then_inc(S["ls"], 1)
                    if inside(i):
                        wait(dve, S["keT"], i + 1)
                        wait(dve, S["o"], i)
                        for g in range(2):
                            dve.tensor_tensor(qbd[:, g], bc(ps_T[:, g, :], 1, HG), hmask[:], ALU.mult).then_inc(S[f"qbd{g}"], 1)
                    if inside(n):
                        wait(dve, S["sig"], n + 1)
                        wait(dve, S["og"], n - 1)
                        dve.tensor_tensor(gs[nu][:], ps_g, sig[:], ALU.mult).then_inc(S["gs"], 1)
                    if inside(i):
                        wait(dve, S["u_p"], i + 1)
                        wait(dve, S["decay"], i + 1)
                        wait(dve, S["s2"], i)
                        for g in range(2):
                            op = dve.scalar_tensor_tensor(out=state[2 * u + 1][:, g], in0=state[2 * u][:, g],
                                                         scalar=decay[:, g, 0:1], in1=ps_u[:, 0, g],
                                                         op0=ALU.mult, op1=ALU.add)
                        op.then_inc(S["s1"], 1)
                        wait(dve, S["s1"], i + 1)
                        wait(dve, S["o"], i)
                        nxt = state[(2 * u + 2) % 4] if r != 3 else s_tmp
                        for g in range(2):
                            op = dve.scalar_tensor_tensor(out=nxt[:, g], in0=state[2 * u + 1][:, g],
                                                         scalar=decay[:, g, 1:2], in1=ps_u[:, 1, g],
                                                         op0=ALU.mult, op1=ALU.add)
                        if r == 3:
                            op.then_inc(S["s_tmp"], 1)
                            wait(dve, S["s_tmp"], q + 1)
                            if inside(i + 1):
                                op = dve.tensor_scalar(state[0][:], s_tmp[:], col(keep, q + 1), None, ALU.mult)
                        if r != 3 or inside(i + 1):
                            op.then_inc(S["s2"], 1)
                    if inside(j):
                        wait(dve, S["ogT_hi"], j + 1)
                        dve.tensor_tensor(ogT[1][:], ps_T[:], ogT[0][:].bitcast(F32), ALU.subtract).then_inc(S["ogT_lo"], 1)
                    if inside(i):
                        for g in range(2):
                            wait(dve, S[f"a{g}"], i + 1)
                            dve.tensor_tensor(am[:, g * HG:(g + 1) * HG], ps_a[g][:], bc(causal[:], 1, HG),
                                              ALU.mult).then_inc(S[f"am{g}"], 1)
                    if inside(m):
                        wait(dve, y_in[u], (m - r % 2) * 16 + 32)
                        wait(dve, x_in[u], (m - r % 2) * 8 + 16)
                        dve.scalar_tensor_tensor(out=s_[u][:], in0=yk[0][u][:], scalar=col(gate[:, 0], m), in1=xt[u][:],
                                                 op0=ALU.mult, op1=ALU.add).then_inc(S["s"], 1)
                        wait(dve, S["s"], m + 1)
                        wait(dve, S["base"], m - 3)
                        dve.scalar_tensor_tensor(out=x1[(r + 2) % 4], in0=yk[1][u][:], scalar=col(gate[:, 1], m), in1=s_[u][:],
                                                 op0=ALU.mult, op1=ALU.add).then_inc(S["x1"], 1)
                        wait(dve, S["x1"], m + 1)
                        dve.bn_stats(bn[u][:], x1[(r + 2) % 4]).then_inc(S["bn"], 1)
                        wait(dve, S["bn"], m + 1)
                        dve.sem_inc(S["bn_ok"], 1)
                        dve.bn_aggr(mv[u][:], bn[u][:]).then_inc(S["mv"], 1)
                        wait(dve, S["mv"], m + 1)
                        dve.tensor_scalar(ve[u][:], mv[u][:, 1:2], LN_EPS, None, ALU.add).then_inc(S["ve"], 1)
                        wait(dve, S["rstd"], m + 1)
                        dve.tensor_scalar(y[(r + 2) % 4], x1[(r + 2) % 4], mv[u][:, 0:1], rstd[u][:],
                                          ALU.subtract, ALU.mult).then_inc(S["y"], 1)
                        dve.tensor_scalar(t1[u][:], mv[u][:, 1:2], rstd[u][:], None, ALU.mult).then_inc(S["t1"], 1)
                        wait(dve, S["t1"], m + 1)
                        dve.tensor_scalar(t2[u][:], t1[u][:], rstd[u][:], RMS_EPS, ALU.mult, ALU.add).then_inc(S["t2"], 1)
                        wait(dve, S["r2"], m + 1)
                        wait(dve, S["hT_t"], m - 1)
                        dve.tensor_scalar(h[u][:], y[(r + 2) % 4], r2[u][:], None, ALU.mult).then_inc(S["h"], 1)
                    if inside(j):
                        wait(dve, S["wo"], j + 1)
                        wait(dve, S["h2"], j - 1)
                        wait(dve, S["base"], j - 1)
                        dve.tensor_tensor(x2[nu][:], ps_bs[:], y[(r + 3) % 4], ALU.add).then_inc(S["x2"], 1)
                        wait(dve, S["sq"], j + 1)
                        wait(dve, S["rh2"], j)
                        dve.tensor_scalar(msd[:], sqs[:], 1.0 / D, RMS_EPS, ALU.mult, ALU.add).then_inc(S["msd"], 1)
                        wait(dve, S["rh2"], j + 1)
                        wait(dve, S["h2_t"], j - 1)
                        dve.tensor_scalar(h2[nu][:], x2[nu][:], rh2[:], None, ALU.mult).then_inc(S["h2"], 1)
                pipeline(dve, step, -2)

            @block.tensor
            def _(pe):
                pe.wait_ge(S["w_low"], 5)
                pe.wait_ge(S["consts"], 25)

                def turn(src, blocks, at=0):
                    for kc in range(blocks):
                        op = pe.transpose(ps_T[:, at + kc, :], src[:, kc * P:(kc + 1) * P], cst["ident"][:])
                    return op

                def project(out, u, wt):
                    for kc in range(KC):
                        op = split_matmul(pe, out, [hT[hf][u][:, kc, :] for hf in range(2)],
                                         [wt[hf][:, kc, :] for hf in range(2)], kc == 0, kc == KC - 1)
                    return op

                def step(i, r, q):
                    u, nu = r % 2, (r + 1) % 2
                    n, j, t = i + 1, i - 1, i - 2
                    if inside(n):
                        wait(pe, S["h"], n + 1)
                        wait(pe, S["ogT_lo"], n - 2)
                        turn(h[nu], KC).then_inc(S["hT_t"], 1)
                    if inside(i):
                        wait(pe, S["ls"], i + 1)
                        wait(pe, S["x2"], i - 1)
                        pe.matmul(ps_bs[:, 0:KEY], cum16[:], ls[u][:, 0:KEY], start=True, stop=True)
                        pe.matmul(ps_bs[:, KEY:], suf16[:], ls[u][:, 0:KEY], start=True, stop=True).then_inc(S["bs"], 1)
                        wait(pe, S["am1"], i)
                        for g in range(2):
                            op = pe.matmul(ps_dec[:, 2 * g:2 * g + 2], ls[u][:, g * P:(g + 1) * P], chunk16[:],
                                          start=True, stop=True)
                        op.then_inc(S["dec"], 1)
                    if inside(n):
                        wait(pe, S["hT_lo"], n + 1)
                        wait(pe, S["low_sb"], n)
                        for kc in range(KC):
                            op = split_matmul(pe, ps_low, [w1h[hf][:, kc, :] for hf in range(2)],
                                             [hT[hf][nu][:, kc, :] for hf in range(2)], kc == 0, kc == KC - 1)
                        op.then_inc(S["low"], 1)
                        wait(pe, S["gs"], n)
                        project(ps_g, nu, wh[G]).then_inc(S["gate_p"], 1)
                    if inside(t):
                        wait(pe, S["h2"], t + 1)
                        turn(h2[u], KC).then_inc(S["h2_t"], 1)
                    if inside(n):
                        wait(pe, S["low_sb"], n + 1)
                        pe.matmul(ps_z, low[nu][:], w2b[:], start=True, stop=True).then_inc(S["z"], 1)
                    if inside(i):
                        wait(pe, S["ke"], i + 1)
                        wait(pe, S["h2_lo"], i - 1)
                        turn(qe, 2)
                        turn(ke, 2, 2).then_inc(S["qk_t"], 1)
                    if inside(n):
                        wait(pe, S["on"], n - 1)
                        project(ps_v[:], nu, wh[V]).then_inc(S["v"], 1)
                    if inside(i):
                        wait(pe, S["kd"], i + 1)
                        wait(pe, S["v_sb"], i + 1)
                        for c in range(2):
                            for hd in range(H):
                                g, hh = divmod(hd, HG)
                                op = pe.matmul(ps_u[hh * HK:(hh + 1) * HK, c, g], kd[c][:, hd * HK:(hd + 1) * HK],
                                               v_sb[u][:, hd * HV:(hd + 1) * HV], start=True, stop=True)
                        op.then_inc(S["u_p"], 1)
                    if inside(j):
                        wait(pe, S["og"], j + 1)
                        wait(pe, S["keT"], min(j + 2, NT) if isinstance(j, int) else j + 2)
                        wait(pe, S["qbd1"], min(j + 2, NT) if isinstance(j, int) else j + 2)
                        if isinstance(j, int) and j == NT - 1:
                            wait(pe, S["h2_lo"], NT - 1)
                        turn(og[nu], KC).then_inc(S["og_t"], 1)
                    if inside(i):
                        wait(pe, S["keT"], i + 1)
                        for g in range(2):
                            wait(pe, S[f"qbd{g}"], i + 1)
                            wait(pe, S["decay"], i + 1)
                            pe.matmul(ps_a[g][:], keT[:, g], qbd[:, g], start=True, stop=True).then_inc(S[f"a{g}"], 1)
                    if inside(n):
                        wait(pe, S["s2"], n)
                        project(ps_qk[:], nu, wh[QK]).then_inc(S["qk"], 1)
                    if inside(j):
                        wait(pe, S["ogT_lo"], j + 1)
                        wait(pe, S["es"], min(j + 2, NT) if isinstance(j, int) else j + 2)
                        for kc in range(KC):
                            op = split_matmul(pe, ps_bs[:], [ogT[hf][:, kc, :] for hf in range(2)],
                                             [wh[O][hf][:, kc, :] for hf in range(2)], kc == 0, kc == KC - 1)
                        op.then_inc(S["wo"], 1)
                    if inside(i):
                        wait(pe, S["v_sb"], min(i + 2, NT) if isinstance(i, int) else i + 2)
                        wait(pe, S["s1"], i + 1)
                        for g in range(2):
                            wait(pe, S[f"am{g}"], i + 1)
                            for hh in range(HG):
                                hd = g * HG + hh
                                pe.matmul(ps_v[:, hd * HV:(hd + 1) * HV], am[:, hd], v_sb[u][:, hd * HV:(hd + 1) * HV],
                                          start=(hd == 0), stop=False, skip_group_check=True)
                                for c in range(2):
                                    op = pe.matmul(ps_v[c * CHUNK:(c + 1) * CHUNK, hd * HV:(hd + 1) * HV],
                                                  qbd[:, g, hh, c * CHUNK:(c + 1) * CHUNK], state[2 * u + c][:, g],
                                                  start=False, stop=(hd == H - 1), skip_group_check=True)
                        op.then_inc(S["o"], 1)
                pipeline(pe, step, -1)


def swiglu(nc, h2T, norm_w, w_gate, w_up, w_down, base, out):
    SPAN = 512
    NSP = TOK // SPAN
    TS = SPAN // P
    with Phase(nc, "ff") as ph:
        sb, sem = ph.sb, ph.sem
        wgu = [[sb(f"w{m}{hf}", [P, NF, KC, P], F32R) for hf in range(2)] for m in range(2)]
        wd = [sb(f"wd{hf}", [P, NF, D], F32R) for hf in range(2)]
        nw = sb("nw", [P, KC])
        hh = [sb(f"hh{u}", [P, 2, KC, SPAN], F32R) for u in range(2)]
        bt = [sb(f"bt{u}", [P, TS, D]) for u in range(2)]
        sg = [sb(f"sg{u}", [P, SPAN]) for u in range(2)]
        act_f = [sb(f"act{u}", [P, SPAN]) for u in range(2)]
        aT = [[sb(f"aT{u}{hf}", [P, SPAN], F32R) for hf in range(2)] for u in range(2)]
        ps_g = [ph.ps(f"ps_g{u}", [P, SPAN]) for u in range(2)]
        ps_u = [ph.ps(f"ps_u{u}", [P, SPAN]) for u in range(2)]
        acc = [ph.ps(f"acc{t}", [P, D]) for t in range(TS)]
        nw_in, w_high, w_low = sem("nw_in"), sem("w_high"), sem("w_low")
        w_in = [sem(f"w_in{u}") for u in range(2)]
        h_in = [sem(f"h_in{u}") for u in range(2)]
        b_in = [sem(f"b_in{u}") for u in range(2)]
        x_out = [sem(f"x_out{u}") for u in range(2)]
        gate_s, up_s, silu_s, act_s, high, low, down_s, added = (
            sem(n) for n in ("gate", "up", "silu", "act", "high", "low", "down", "added"))
        base_v = base.rearrange("(s t p) d -> s p t d", p=P, t=TS)
        out_v = out.rearrange("(s t p) d -> s p t d", p=P, t=TS)

        def spans(eng, body):
            for s in range(2):
                body(s, s)
            with eng.Fori(0, NSP // 2 - 1) as pair:
                for s in range(2):
                    body(pair * 2 + (s + 2), s)

        def of(v, s):
            return v[s] if isinstance(s, int) else v[bass.ds(s, 1)].rearrange("a p t d -> (a p) t d")

        with nc.Block() as block:
            @block.sync
            def _(sp):
                def load_h(s, u):
                    at = s * SPAN if isinstance(s, int) else sp.snap(s * SPAN)
                    src = h2T[:, :, :, at:at + SPAN] if isinstance(s, int) else h2T[:, :, :, bass.ds(at, SPAN)]
                    wait(sp, up_s, (s - 1) * NF)
                    sp.dma_start(hh[u][:].bitcast(F32), src).then_inc(h_in[u], 16)

                sp.dma_start(nw[:], norm_w.rearrange("(kc p) -> p kc", p=P), allow_slow_non_contiguous=True).then_inc(nw_in, 16)
                load_h(0, 0)
                for f in range(NF):
                    wait(sp, w_low, f - 1)
                    st = bt[f % 2]
                    cols = slice(f * P, (f + 1) * P)
                    for m, wm in enumerate((w_gate, w_up)):
                        sp.dma_start(st[:, m].rearrange("p (kc n) -> p kc n", kc=KC),
                                     wm[:, cols].rearrange("(kc p) n -> p kc n", p=P)).then_inc(w_in[f % 2], 16)
                    sp.dma_start(st[:, 2], w_down[f * P:(f + 1) * P, :]).then_inc(w_in[f % 2], 16)
                load_h(1, 1)
                sp.wait_ge(w_low, NF)

                def body(s, u, h_next):
                    row = s if isinstance(s, int) else sp.snap(s)
                    wait(sp, x_out[u], (s - u) * 8)
                    sp.dma_start(bt[u][:], of(base_v, row)).then_inc(b_in[u], 16)
                    if isinstance(s, int) and s == 0:
                        return
                    row = s - 1 if isinstance(s, int) else sp.snap(s - 1)
                    wait(sp, added, s)
                    sp.dma_start(of(out_v, row), bt[1 - u][:]).then_inc(x_out[1 - u], 16)
                    if h_next:
                        load_h(s + 1, 1 - u)
                for s in range(NSP):
                    body(s, s % 2, s < NSP - 1)
                sp.wait_ge(added, NSP)
                sp.dma_start(out_v[NSP - 1], bt[1][:]).then_inc(x_out[1], 16)
                for u in range(2):
                    sp.wait_ge(x_out[u], 16 * NSP // 2)

            @block.scalar
            def _(act):
                def take_high(f):
                    b = f % 2
                    act.wait_ge(w_in[b], 48 * (f // 2 + 1))
                    for m in range(2):
                        for kc in range(KC):
                            act.activation(wgu[m][0][:, f, kc], bt[b][:, m, kc * P:(kc + 1) * P], ACT.Copy,
                                           scale=nw[:, kc:kc + 1])
                    act.copy(wd[0][:, f], bt[b][:, 2]).then_inc(w_high, 1)

                act.wait_ge(nw_in, 16)
                take_high(0)

                def body(s, u):
                    for f in range(NF):
                        b = f % 2
                        g = s * NF + f
                        if isinstance(s, int) and s == 0 and f + 1 < NF:
                            take_high(f + 1)
                        wait(act, gate_s, g + 1)
                        wait(act, act_s, g if f == 0 else g - 1)
                        act.activation(sg[b][:], ps_g[b][:], ACT.Silu).then_inc(silu_s, 1)
                        wait(act, act_s, g + 1)
                        wait(act, down_s, g if f == 0 else g - 1)
                        act.copy(aT[b][0][:], act_f[b][:]).then_inc(high, 1)
                spans(act, body)

            @block.vector
            def _(dve):
                dve.wait_ge(nw_in, 16)

                def finish(s, u):
                    wait(dve, down_s, (s + 1) * NF)
                    wait(dve, b_in[u], (s - u) * 8 + 16)
                    for t in range(TS):
                        op = dve.tensor_tensor(bt[u][:, t], acc[t][:], bt[u][:, t], ALU.add)
                    op.then_inc(added, 1)

                def take_low(f):
                    b = f % 2
                    dve.wait_ge(w_in[b], 48 * (f // 2 + 1))
                    dve.wait_ge(w_high, f + 1)
                    for m in range(2):
                        for kc in range(KC):
                            dve.scalar_tensor_tensor(out=wgu[m][1][:, f, kc], in0=bt[b][:, m, kc * P:(kc + 1) * P],
                                                     scalar=nw[:, kc:kc + 1], in1=wgu[m][0][:, f, kc].bitcast(F32),
                                                     op0=ALU.mult, op1=ALU.subtract)
                    dve.tensor_tensor(wd[1][:, f], bt[b][:, 2], wd[0][:, f].bitcast(F32),
                                      ALU.subtract).then_inc(w_low, 1)

                take_low(0)

                def body(s, u):
                    for f in range(NF):
                        b = f % 2
                        g = s * NF + f
                        if isinstance(s, int) and s == 0 and f + 1 < NF:
                            take_low(f + 1)
                        wait(dve, silu_s, g + 1)
                        wait(dve, up_s, g + 1)
                        wait(dve, low, g if f == 0 else g - 1)
                        dve.tensor_tensor(act_f[b][:], ps_u[b][:], sg[b][:], ALU.mult).then_inc(act_s, 1)
                        wait(dve, high, g + 1)
                        dve.tensor_tensor(aT[b][1][:], act_f[b][:], aT[b][0][:].bitcast(F32), ALU.subtract).then_inc(low, 1)
                        if f == 0 and not (isinstance(s, int) and s == 0):
                            finish(s - 1, 1 - u)
                spans(dve, body)
                finish(NSP - 1, 1)

            @block.tensor
            def _(pe):
                def down(g, f, first, last):
                    wait(pe, low, g + 1)
                    for t in range(TS):
                        cols = slice(t * P, (t + 1) * P)
                        op = split_matmul(pe, acc[t][:], [aT[f % 2][hf][:, cols] for hf in range(2)],
                                          [wd[hf][:, f] for hf in range(2)], first, last)
                    op.then_inc(down_s, 1)

                def body(s, u):
                    wait(pe, h_in[u], (s - u) * 8 + 16)
                    for f in range(NF):
                        b = f % 2
                        g = s * NF + f
                        if isinstance(s, int) and s == 0:
                            pe.wait_ge(w_low, f + 1)
                        wait(pe, silu_s, g if f == 0 else g - 1)
                        for kc in range(KC):
                            op = split_matmul(pe, ps_g[b][:], [wgu[0][hf][:, f, kc] for hf in range(2)],
                                              [hh[u][:, hf, kc] for hf in range(2)], kc == 0, kc == KC - 1)
                        op.then_inc(gate_s, 1)
                        wait(pe, act_s, g if f == 0 else g - 1)
                        for kc in range(KC):
                            op = split_matmul(pe, ps_u[b][:], [wgu[1][hf][:, f, kc] for hf in range(2)],
                                              [hh[u][:, hf, kc] for hf in range(2)], kc == 0, kc == KC - 1)
                        op.then_inc(up_s, 1)
                        if f > 0:
                            if f == 1:
                                wait(pe, added, s)
                            down(g - 1, f - 1, f == 1, False)
                        elif not (isinstance(s, int) and s == 0):
                            down(g - 1, NF - 1, False, True)
                spans(pe, body)
                down(NSP * NF - 1, NF - 1, False, True)


def macaron(nc, x, norm1_w, wq, wk, wv, w1, w2, gk_b, wg, gnorm_w, wo, ffn_norm_w, w_gate, w_up, w_down,
            gate_w, W, atoms, eaw, importance, mask_idx, out):
    x = x.rearrange("b t d -> (b t) d")
    out = out.rearrange("b t d -> (b t) d")

    def dram(name, shape):
        return nc.dram_tensor(name, shape, F32).ap()

    table = dram("table", (PLACES + NS, E))
    m_store = dram("m_store", (P, KC, 2, E, D))
    dispatched = dram("dispatched", (E * REGION, D))
    routed = dram("routed", (BLOCKS * P, D))
    base = dram("base", (TOK, D))
    h2T = dram("h2T", (P, 2, KC, TOK))
    x3 = dram("x3", (TOK, D))
    with ExitStack() as ctx:
        def sb(name, shape, dt=F32):
            return ctx.enter_context(nc.sbuf_tensor(name, shape, dt))

        cst = constants(nc, sb)
        gate = sb("gate", [P, 2, NT])
        row_of = sb("row_of", [P, 2, NT], I32)
        tile_tab = sb("tile_tab", [1, 2, BLOCKS], I32)
        place_i = sb("place_i", [P, NB], I32)
        total = sb("total", [P, NB, E])
        sparse_places(nc, cst, atoms, eaw, importance, mask_idx, table, place_i, total)
        router(nc, cst, "r1", x, gate_w, gate, row_of, tile_tab, dispatched, spread=(table, place_i, total))
        with nc.sbuf_tensor("M1", [P, KC, 2, E, D], F32R) as M:
            dense_experts(nc, cst, table, W, M, m_store)
            experts(nc, cst, "e1", M, tile_tab, dispatched, routed)
        w = dict(norm1_w=norm1_w, wq=wq, wk=wk, wv=wv, w1=w1, w2=w2, gk_b=gk_b, wg=wg, gnorm_w=gnorm_w, wo=wo)
        attention(nc, cst, x, routed, gate, row_of, w, base, h2T)
        swiglu(nc, h2T, ffn_norm_w, w_gate, w_up, w_down, base, x3)
        with nc.sbuf_tensor("M2", [P, KC, 2, E, D], F32R) as M:
            router(nc, cst, "r2", x3, gate_w, gate, row_of, tile_tab, dispatched, M=M, m_store=m_store)
            experts(nc, cst, "e2", M, tile_tab, dispatched, routed)
        combine(nc, "c2", x3, routed, gate, row_of, out)


_INS = ['L0_attn_x', 'L0_attn_norm1_w', 'L0_attn_wq', 'L0_attn_wk', 'L0_attn_wv', 'L0_attn_gk_w1', 'L0_attn_gk_w2',
        'L0_attn_gk_b', 'L0_attn_wg', 'L0_attn_gnorm_w', 'L0_attn_wo', 'L0_attn_ffn_norm_w', 'L0_attn_w_gate',
        'L0_attn_w_up', 'L0_attn_w_down', 'L0_ffn_gate_w', 'L0_ffn_W', 'L0_ffn_atoms', 'L0_ffn_expert_atom_weights',
        'L0_ffn_importance', 'L0_ffn_mask_idx']


def kernel(**inputs):
    import numpy as _np
    import concourse.bacc as _bacc
    from concourse.bass_utils import run_bass_kernel_spmd as _run

    nc = _bacc.Bacc("TRN2", target_bir_lowering=False, num_devices=1)
    arrays, args = {}, []
    for name in _INS:
        a = _np.ascontiguousarray(inputs[name])
        arrays[f"in_{name}_dram"] = a
        args.append(nc.dram_tensor(f"in_{name}_dram", a.shape, mybir.dt.from_np(a.dtype), kind="ExternalInput").ap())
    args.append(nc.dram_tensor("out_0_dram", (B, T, D), F32, kind="ExternalOutput").ap())
    macaron(nc, *args)
    r = _run(nc, [arrays], core_ids=[0])
    return r.results[0]["out_0_dram"]
```

```python
from contextlib import ExitStack

import concourse.bass as bass
from concourse import mybir

F32 = mybir.dt.float32
F32R = mybir.dt.float32r
BF16 = mybir.dt.bfloat16
I32 = mybir.dt.int32
ALU = mybir.AluOpType
ACT = mybir.ActivationFunctionType
AX = mybir.AxisListType

P = 128
D = 512
KC = D // P
B, T = 4, 1024
TOK = B * T
NT = TOK // P
E = 8
A = 64
NS = 4096
NB = NS // P
GB = 4
NG_SP = NB // GB
PLACES = D * D
REGION = TOK + P
BLOCKS = (2 * TOK + E * (P - 1)) // P + 1
H, HK, HV = 8, 32, 64
KEY, VAL, LOW = H * HK, H * HV, 16
CHUNK = 64
HID = 1408
NF = HID // P
TILES_B = T // P
LN_EPS, RMS_EPS = 1e-5, 1e-6
assert BLOCKS % 4 == 0


class Phase:

    def __init__(self, nc, name, recycle=False):
        self.nc, self.name, self.recycle, self.sems = nc, name, recycle, []
        self.ctx = ExitStack()

    def __enter__(self):
        self.ctx.__enter__()
        return self

    def __exit__(self, *exc):
        self.ctx.__exit__(*exc)
        if self.recycle and exc[0] is None:
            self.nc.clear_and_free_semaphores(self.sems)
            self.nc.all_engine_barrier()

    def sb(self, name, shape, dt=F32):
        return self.ctx.enter_context(self.nc.sbuf_tensor(f"{self.name}_{name}", shape, dt))

    def ps(self, name, shape, dt=F32):
        return self.ctx.enter_context(self.nc.psum_tensor(f"{self.name}_{name}", shape, dt))

    def sem(self, name):
        self.sems.append(self.nc.alloc_semaphore(f"{self.name}_{name}"))
        return self.sems[-1]


class Steps:

    def __init__(self, eng, sem, base=0):
        self.eng, self.sem, self.base, self.n = eng, sem, base, 0

    def did(self, ins):
        ins.then_inc(self.sem, 1)
        self.n += 1

    def settle(self):
        self.eng.wait_ge(self.sem, self.base + self.n)

    def chain(self, ins):
        self.did(ins)
        self.settle()


def bc(ap, axis, n):
    a = ap.unsqueeze(axis)
    shape = list(a.shape)
    shape[axis] = n
    return a.broadcast_to(shape)


def constants(nc, sb):
    c = {}
    c["ident"] = sb("ident", [P, P])
    c["ident_r"] = sb("ident_r", [P, P], F32R)
    c["before"] = sb("before", [P, P])
    c["ones"] = sb("ones", [P, P])
    with Phase(nc, "const") as ph:
        made = ph.sem("made")
        with nc.Block() as block:
            @block.gpsimd
            def _(pool):
                pool.memset(c["ident"][:], 0.0).then_inc(made, 1)
                pool.memset(c["ones"][:], 1.0).then_inc(made, 1)
                pool.wait_ge(made, 2)
                pool.affine_select(out=c["ident"][:], in_=c["ident"][:], compare_op=ALU.not_equal, fill=1.0,
                                   base=0, pattern=[[-1, P]], channel_multiplier=1).then_inc(made, 1)
                pool.affine_select(out=c["before"][:], in_=c["ones"][:], compare_op=ALU.is_gt, fill=0.0,
                                   base=0, pattern=[[1, P]], channel_multiplier=-1)

            @block.scalar
            def _(act):
                act.wait_ge(made, 3)
                act.copy(c["ident_r"][:], c["ident"][:])
    return c


def sparse_places(nc, cst, atoms, eaw, importance, mask_idx, table, place_i, total):
    W3 = 3 * E
    GP = GB * P
    with Phase(nc, "sp") as ph:
        sb, sem = ph.sb, ph.sem
        eaw_sb = sb("eaw", [E, A])
        atoms_sb = sb("atoms", [A, NS])
        imp = sb("imp", [E, NS])
        idx_row = sb("idx_row", [P, NS], I32)
        idx_col = sb("idx_col", [P, NB], I32)
        row_f = sb("row_f", [P, NS])
        col_f = sb("col_f", [P, NB])
        zero = sb("zero", [P, 4096])
        stat = sb("stat", [E, 4])
        prob = sb("prob", [E, A])
        probT = sb("probT", [A, E])
        impT = sb("impT", [P, NB * E])
        val = sb("val", [P, NB * E])
        val2 = sb("val2", [P, NB * E])
        parts = sb("parts", [P, NB * W3], BF16)
        before = sb("before16", [P, P], BF16)
        ones16 = sb("ones16", [P, 2], BF16)
        eq = sb("eq", [P, NB, GP], BF16)
        eqd = sb("eqd", [P, NB, P], BF16)
        sumT = [sb(f"sumT{u}", [W3, GP]) for u in range(2)]
        acc = sb("acc", [P, NB, W3])
        earlier = sb("earlier", [P, NB])
        place_j = sb("place_j", [P, NB], I32)
        place_f = sb("place_f", [P, NB])
        spare_f = sb("spare_f", [P, NB])
        ps_sum = [ph.ps(f"ps_sum{u}", [W3, GP]) for u in range(2)]
        ps_back = [ph.ps(f"ps_back{u}", [P, GB, W3]) for u in range(2)]
        ps_imp = ph.ps("ps_imp", [P, 512])
        ps_dl = ph.ps("ps_dl", [P, 512])
        ps_dg = ph.ps("ps_dg", [P, 512])
        ps_p = ph.ps("ps_p", [P, 512])
        vec, act_s, ten, poo, eq_ready, zeroed = (sem(n) for n in ("vec", "act", "ten", "pool", "eq_ready", "zeroed"))
        summed, copied, turned_s, kept, ordered = (sem(n) for n in ("summed", "copied", "turned", "kept", "ordered"))
        eaw_in, imp_in, idx_in, atoms_in = (sem(n) for n in ("eaw_in", "imp_in", "idx_in", "atoms_in"))

        with nc.Block() as block:
            @block.sync
            def _(sp):
                sp.dma_start(eaw_sb[:], eaw).then_inc(eaw_in, 16)
                sp.dma_start(imp[:], importance).then_inc(imp_in, 16)
                sp.dma_start(idx_row[:], mask_idx.rearrange("(o s) -> o s", o=1).broadcast_to([P, NS])).then_inc(idx_in, 16)
                sp.dma_start(idx_col[:], mask_idx.rearrange("(b p) -> p b", p=P),
                             allow_slow_non_contiguous=True).then_inc(idx_in, 16)
                sp.dma_start(atoms_sb[:], atoms).then_inc(atoms_in, 16)
                sp.wait_ge(vec, 1)
                flat = table[0:PLACES, :].rearrange("(n p k) e -> n p (k e)", n=4, p=P)
                for n in range(4):
                    sp.dma_start(flat[n], zero[:]).then_inc(zeroed, 16)
                sp.dma_start(table[PLACES:, :].rearrange("(p k) e -> p (k e)", p=P), zero[:, 0:NB * E]).then_inc(zeroed, 16)

            @block.gpsimd
            def _(pool):
                st = Steps(pool, poo)
                st.did(pool.iota(spare_f[:], pattern=[[P, NB]], base=PLACES, channel_multiplier=1,
                                 allow_small_or_imprecise_dtypes=True))
                pool.wait_ge(zeroed, 80)

            @block.scalar
            def _(act):
                act.wait_ge(vec, 3)
                act.activation(prob[:], eaw_sb[:], ACT.Exp, bias=stat[:, 0:1], accum_out=stat[:, 1:2]).then_inc(act_s, 1)
                act.wait_ge(imp_in, 16)
                act.activation(imp[:], imp[:], ACT.Sigmoid).then_inc(act_s, 1)
                act.sem_inc(copied, 2)
                with act.Fori(0, NG_SP // 2) as pair:
                    for u in range(2):
                        act.wait_ge(summed, pair * 2 + u + 1)
                        act.wait_ge(turned_s, pair * 2 + u + 1)
                        act.copy(sumT[u][:], ps_sum[u][:]).then_inc(copied, 1)

            @block.vector
            def _(dve):
                st = Steps(dve, vec)
                st.did(dve.memset(zero[:], 0.0))
                st.did(dve.memset(ones16[:], 1.0))
                dve.wait_ge(eaw_in, 16)
                dve.tensor_reduce(stat[:, 0:1], eaw_sb[:], AX.X, ALU.max, negate=True).then_inc(vec, 1)
                st.n += 1
                st.did(dve.tensor_copy(before[:], cst["before"][:]))
                st.settle()
                dve.wait_ge(act_s, 1)
                st.chain(dve.reciprocal(stat[:, 2:3], stat[:, 1:2]))
                st.did(dve.tensor_scalar(prob[:], prob[:], stat[:, 2:3], None, ALU.mult))
                dve.wait_ge(ten, 1)
                st.did(dve.tensor_copy(probT[:], ps_p[0:A, 0:E]))
                dve.wait_ge(idx_in, 32)
                st.did(dve.tensor_copy(row_f[:], idx_row[:]))
                st.chain(dve.tensor_copy(col_f[:], idx_col[:]))
                with dve.Fori(0, NG_SP) as g:
                    for i in range(GB):
                        dve.tensor_scalar(eq[:, bass.ds(g * GB + i, 1), :], row_f[:, bass.ds(g * GP, GP)].unsqueeze(1),
                                          col_f[:, bass.ds(g * GB + i, 1)], None, ALU.is_equal)
                        op = dve.scalar_tensor_tensor(out=eqd[:, bass.ds(g * GB + i, 1), :],
                                                      in0=row_f[:, bass.ds(g * GP + i * P, P)].unsqueeze(1),
                                                      scalar=col_f[:, bass.ds(g * GB + i, 1)], in1=before[:].unsqueeze(1),
                                                      op0=ALU.is_equal, op1=ALU.mult)
                    op.then_inc(eq_ready, 1)
                dve.wait_ge(ten, 2)
                st.did(dve.tensor_copy(impT[:], ps_imp[:, 0:NB * E]))
                dve.wait_ge(ten, 3)
                st.settle()
                st.chain(dve.tensor_tensor(val[:], ps_dl[:, 0:NB * E], impT[:], ALU.mult))
                pv = parts[:].rearrange("p (b w) -> p b w", w=W3)
                vv = val[:].rearrange("p (b e) -> p b e", e=E)
                vv2 = val2[:].rearrange("p (b e) -> p b e", e=E)
                st.chain(dve.tensor_copy(pv[:, :, 0:E], vv))
                st.chain(dve.tensor_tensor(vv2, vv, pv[:, :, 0:E], ALU.subtract))
                st.chain(dve.tensor_copy(pv[:, :, E:2 * E], vv2))
                st.chain(dve.tensor_tensor(vv, vv2, pv[:, :, E:2 * E], ALU.subtract))
                st.chain(dve.tensor_copy(pv[:, :, 2 * E:3 * E], vv))
                st.did(dve.tensor_scalar(place_i[:], idx_col[:], D - 1, 9, ALU.bitwise_and, ALU.logical_shift_left))
                st.chain(dve.tensor_scalar(place_j[:], idx_col[:], 9, None, ALU.logical_shift_right))
                st.chain(dve.tensor_tensor(place_i[:], place_i[:], place_j[:], ALU.bitwise_or))
                st.chain(dve.tensor_copy(place_f[:], place_i[:]))
                dve.wait_ge(poo, 1)
                st.chain(dve.tensor_tensor(place_f[:], place_f[:], spare_f[:], ALU.subtract))
                dve.sem_inc(kept, 2)
                with dve.Fori(0, NG_SP // 2) as pair:
                    for u in range(2):
                        dve.wait_ge(turned_s, pair * 2 + u + 3)
                        dve.tensor_copy(acc[:, bass.ds((pair * 2 + u) * GB, GB), :], ps_back[u][:]).then_inc(kept, 1)
                dve.wait_ge(kept, NG_SP + 2)
                dve.wait_ge(ten, 4)
                st.did(dve.tensor_copy(earlier[:], ps_dg[:, 0:NB]))
                st.settle()
                st.chain(dve.tensor_tensor(total[:], acc[:, :, 0:E], acc[:, :, E:2 * E], ALU.add))
                st.did(dve.tensor_tensor(total[:], total[:], acc[:, :, 2 * E:3 * E], ALU.add))
                st.chain(dve.scalar_tensor_tensor(out=place_f[:], in0=earlier[:], scalar=0.5, in1=place_f[:],
                                                  op0=ALU.is_lt, op1=ALU.mult))
                st.chain(dve.tensor_tensor(place_f[:], place_f[:], spare_f[:], ALU.add))
                dve.tensor_copy(place_i[:], place_f[:])

            @block.tensor
            def _(pe):
                pe.wait_ge(vec, 6)
                pe.transpose(ps_p[0:A, 0:E], prob[:], cst["ident"][0:E, 0:E]).then_inc(ten, 1)
                pe.wait_ge(act_s, 2)
                for b in range(NB):
                    t = pe.transpose(ps_imp[:, b * E:(b + 1) * E], imp[:, b * P:(b + 1) * P], cst["ident"][0:E, 0:E])
                t.then_inc(ten, 1)
                pe.wait_ge(vec, 7)
                pe.wait_ge(atoms_in, 16)
                for b in range(NB):
                    m = pe.matmul(ps_dl[:, b * E:(b + 1) * E], atoms_sb[:, b * P:(b + 1) * P], probT[:],
                                  start=True, stop=True)
                m.then_inc(ten, 1)
                with pe.Fori(0, NG_SP) as g:
                    pe.wait_ge(eq_ready, g + 1)
                    for k in range(GB):
                        count = ps_dg[:, bass.ds(g * GB + k, 1)]
                        for i in range(k):
                            pe.matmul(count, eq[:, bass.ds(g * GB + i, 1), k * P:(k + 1) * P].squeeze(1), ones16[:, 0:1],
                                      start=(i == 0), stop=False)
                        pe.matmul(count, eqd[:, bass.ds(g * GB + k, 1), :].squeeze(1), ones16[:, 0:1], start=(k == 0), stop=True)
                pe.wait_ge(vec, 16)
                pe.sem_inc(turned_s, 2)

                def add_up(g, u):
                    pe.wait_ge(copied, g + 1)
                    for i in range(GB):
                        m = pe.matmul(ps_sum[u][:].unsqueeze(1), parts[:, bass.ds((g * GB + i) * W3, W3)] if not isinstance(g, int)
                                      else parts[:, (g * GB + i) * W3:(g * GB + i + 1) * W3],
                                      eq[:, bass.ds(g * GB + i, 1), :], start=(i == 0), stop=(i == GB - 1))
                    m.then_inc(summed, 1)

                def turn_sums(g, u):
                    pe.wait_ge(copied, g + 3)
                    pe.wait_ge(kept, g + 1)
                    pe.sem_inc(ordered, 1)
                    for k in range(GB):
                        m = pe.transpose(ps_back[u][:, k, :], sumT[u][:, k * P:(k + 1) * P],
                                         cst["ident"][0:W3, 0:W3])
                    m.then_inc(turned_s, 1)

                add_up(0, 0)
                with pe.Fori(0, NG_SP // 2 - 1) as pair:
                    add_up(pair * 2 + 1, 1)
                    turn_sums(pair * 2, 0)
                    add_up(pair * 2 + 2, 0)
                    turn_sums(pair * 2 + 1, 1)
                add_up(NG_SP - 1, 1)
                turn_sums(NG_SP - 2, 0)
                turn_sums(NG_SP - 1, 1)
                pe.wait_ge(turned_s, NG_SP + 2)
                pe.nop().then_inc(ten, 1)


def router(nc, cst, name, x, gate_w, gate, row_of, tile_tab, dispatched, M, m_store=None, sparse=None):
    GT = 8
    HT = GT // 2
    NG = NT // GT
    QG = GT // 2
    make = sparse is not None
    NX = 2 if make else 3
    PIECES = KC * KC
    TB = 3
    with Phase(nc, name, recycle=True) as ph:
        sb, sem = ph.sb, ph.sem
        xn = [sb(f"xn{v}", [P, GT, D]) for v in range(NX)]
        xT = [sb(f"xT{u}", [P, KC, 2 * P]) for u in range(2)]
        lT = sb("lT", [E, 2 * P])
        gw = sb("gw", [E, D])
        gwT = sb("gwT", [P, KC, E])
        bn = sb("bn", [P, HT, 6])
        mv = [sb(f"mv{h}", [P, HT, 2]) for h in range(2)]
        rstd = [sb(f"rstd{h}", [P, HT]) for h in range(2)]
        near = sb("near", [P, HT])
        eps = sb("eps", [P, 1])
        lg = sb("lg", [P, GT, E])
        rev = sb("rev", [P, GT, E])
        cand = sb("cand", [P, GT, E])
        best = sb("best", [P, GT])
        both = sb("both", [P, GT, E])
        chosen = sb("chosen", [P, 2, NT, E])
        top = sb("top", [P, 2, NT])
        keep = sb("keep", [P, E, GT + 1])
        counts = sb("counts", [P, E, GT + 1])
        upto = sb("upto", [P, E, GT + 1])
        prod = sb("prod", [P, 2, GT, E])
        sent_f = sb("sent_f", [P, 2, NT])
        sent = [sb(f"sent{u}", [P, 2, GT], I32) for u in range(2)]
        shift = sb("shift", [P, 2, NT])
        far = sb("far", [P, NT])
        w0 = sb("w0", [P, NT])
        region, offset = sb("region", [P, E]), sb("offset", [P, E])
        count_i = sb("count_i", [P, E], I32)
        blocks, blocks_to, before_e, one_e = (sb(n, [P, E]) for n in ("blocks", "blocks_to", "before_e", "one_e"))
        pad_i = sb("pad_i", [P, E], I32)
        zrow = sb("zrow", [P, D])
        blk = sb("blk", [P, BLOCKS])
        over = sb("over", [P, E - 1, BLOCKS])
        te = sb("te", [P, BLOCKS])
        tb = sb("tb", [P, BLOCKS])
        ps_T = [ph.ps(f"ps_T{r}", [P, KC, P]) for r in range(4)]
        ps_lT = ph.ps("ps_lT", [E, 2 * P])
        ps_l = ph.ps("ps_l", [P, GT, E])
        if make:
            W, table, place_i, total = sparse
            w_sb = sb("w", [P, KC, D])
            tab = [sb(f"tab{v}", [P, P, E]) for v in range(TB)]
            ps_w = ph.ps("ps_w", [P, D])
        w_in, w_turned, added, high, low = (sem(n) for n in ("w_in", "w_turned", "added", "high", "low"))
        tab_in = [sem(f"tab_in{v}") for v in range(TB)]
        clipped = sem("clipped")
        ps_c = ph.ps("ps_c", [P, 2, GT, E])
        loaded = [[sem(f"loaded{g}{h}") for h in range(2)] for g in range(NG)]
        gone = [[sem(f"gone{g}{h}") for h in range(2)] for g in range(NG)]
        made, bn_done, stats, logged, rsqrt, normed = (sem(n) for n in ("made", "bn", "stats", "logged", "rsqrt", "normed"))
        turned, copied, multiplied, taken, scored, pads, side = (
            sem(n) for n in ("turned", "copied", "multiplied", "taken", "scored", "pads", "side"))
        gw_in, gw_T, chose, counted, placed, vec, end, far_s = (sem(n) for n in (
            "gw_in", "gw_T", "chose", "counted", "placed", "vec", "end", "far"))
        m_in = sem("m_in")
        with nc.Block() as block:
            @block.sync
            def _(sp):
                src = x.rearrange("(g j p) d -> g p j d", g=2 * NG, p=P)

                def load(g):
                    for h in range(2):
                        if g >= NX:
                            sp.wait_ge(gone[g - NX][h], 32 * HT)
                        sp.dma_start(xn[g % NX][:, h * HT:(h + 1) * HT, :], src[2 * g + h]).then_inc(loaded[g][h], 16)

                def fetch(kc):
                    sp.dma_start(M[:, kc].bitcast(F32), m_store[:, kc]).then_inc(m_in, 16)

                def fetch_table(pieces):
                    for p in pieces:
                        wait(sp, low, p - TB + 1)
                        sp.dma_start(tab[p % TB][:], table_v[p // KC, p % KC]).then_inc(tab_in[p % TB], 16)

                def send_pads():
                    sp.wait_ge(placed, NG + 1)
                    sp.wait_ge(made, 5)
                    for e in range(E):
                        row = sp.snap(sp.value_load(pad_i[0:1, e:e + 1], min_val=0, max_val=(E - 1) * REGION + TOK))
                        sp.dma_start(dispatched[bass.ds(row, P), :], zrow[:]).then_inc(pads, 16)

                load(0)
                sp.dma_start(gw[:], gate_w).then_inc(gw_in, 16)
                if make:
                    table_v = table[0:PLACES, :].rearrange("(kc p rb r) e -> kc rb p r e", kc=KC, p=P, rb=KC)
                    sp.wait_ge(side, 16 * GB)
                    load(1)
                    sp.dma_start(w_sb[:], W.rearrange("(a p) c -> p a c", p=P)).then_inc(w_in, 16)
                    load(2)
                    sp.wait_ge(side, 16 * NB)
                    fetch_table(range(KC))
                    load(3)
                    fetch_table(range(KC, 2 * KC + TB))
                    send_pads()
                    fetch_table(range(2 * KC + TB, PIECES))
                else:
                    load(1)
                    load(2)
                    fetch(0)
                    fetch(1)
                    load(3)
                    fetch(2)
                    fetch(3)
                    send_pads()
                    sp.wait_ge(m_in, 16 * KC)
                sp.wait_ge(pads, 16 * E)

            @block.gpsimd
            def _(pool):
                pool.memset(eps[:], LN_EPS).then_inc(made, 1)
                pool.iota(rev[:], pattern=[[0, GT], [-1, E]], base=E, channel_multiplier=0,
                          allow_small_or_imprecise_dtypes=True).then_inc(made, 1)
                pool.iota(region[:], pattern=[[REGION, E]], base=0, channel_multiplier=0,
                          allow_small_or_imprecise_dtypes=True).then_inc(made, 1)
                pool.iota(blk[:], pattern=[[1, BLOCKS]], base=0, channel_multiplier=0,
                          allow_small_or_imprecise_dtypes=True).then_inc(made, 1)
                pool.memset(zrow[:], 0.0).then_inc(made, 1)

                def spread(g):
                    wait(pool, side, 16 * GB * g)
                    for b in range(g * GB, (g + 1) * GB):
                        pool.indirect_dma_start(table, bass.IndirectOffsetOnAxis(ap=place_i[:, b:b + 1], axis=0),
                                                total[:, b, :], None, compute_op=ALU.add).then_inc(side, 16)

                EARLY = 6
                if make:
                    for g in range(EARLY):
                        spread(g)
                for g in range(NG):
                    u = g % 2
                    pool.wait_ge(placed, g + 1)
                    for j in range(GT):
                        for k in range(2):
                            pool.indirect_dma_start(dispatched, bass.IndirectOffsetOnAxis(ap=sent[u][:, k, j:j + 1], axis=0),
                                                    xn[g % NX][:, j, :], None).then_inc(gone[g][j // HT], 16)
                        if make and g == 0 and j % 3 == 1 and EARLY + j // 3 < NG_SP:
                            spread(EARLY + j // 3)
                for g in range(NG):
                    for h in range(2):
                        pool.wait_ge(gone[g][h], 32 * HT)
                if make:
                    pool.wait_ge(side, 16 * NB)

            @block.vector
            def _(dve):
                def take_stats(g):
                    for h in range(2):
                        n = (2 * g + h) * HT
                        dve.wait_ge(loaded[g][h], 16)
                        wait(dve, stats, n)
                        for j in range(HT):
                            dve.bn_stats(bn[:, j, :], xn[g % NX][:, h * HT + j, :]).then_inc(bn_done, 1)
                        wait(dve, normed, n - HT)
                        for j in range(HT):
                            if j == 0:
                                dve.wait_ge(bn_done, n + HT)
                            dve.bn_aggr(mv[h][:, j, :], bn[:, j, :]).then_inc(stats, 1)

                st = Steps(dve, vec)

                def norm(g):
                    for h in range(2):
                        dve.wait_ge(rsqrt, 2 * g + h + 1)
                        st.chain(dve.tensor_tensor(near[:], rstd[h][:], rstd[h][:], ALU.mult))
                        st.chain(dve.scalar_tensor_tensor(out=near[:], in0=mv[h][:, :, 1], scalar=LN_EPS, in1=near[:],
                                                          op0=ALU.add, op1=ALU.mult))
                        st.chain(dve.tensor_scalar(near[:], near[:], -0.5, 1.5, ALU.mult, ALU.add))
                        st.chain(dve.tensor_tensor(rstd[h][:], rstd[h][:], near[:], ALU.mult))
                        for j in range(HT):
                            t = xn[g % NX][:, h * HT + j, :]
                            dve.tensor_scalar(t, t, mv[h][:, j, 0:1], rstd[h][:, j:j + 1],
                                              ALU.subtract, ALU.mult).then_inc(normed, 1)

                def rank(g):
                    u, tiles = g % 2, slice(g * GT, (g + 1) * GT)
                    dve.wait_ge(scored, (g + 1) * GT // 2)
                    dve.tensor_scalar(lg[:], ps_l[:], 50.0, -50.0, ALU.min, ALU.max).then_inc(clipped, 1)
                    dve.wait_ge(clipped, g + 1)
                    for k in range(2):
                        oh, hi = chosen[:, k, tiles, :], top[:, k, tiles]
                        st.chain(dve.tensor_reduce(hi, lg[:], AX.X, ALU.max))
                        st.chain(dve.tensor_tensor(cand[:], lg[:], bc(hi, 2, E), ALU.is_equal))
                        st.chain(dve.tensor_tensor(cand[:], cand[:], rev[:], ALU.mult))
                        st.chain(dve.tensor_reduce(best[:], cand[:], AX.X, ALU.max))
                        st.chain(dve.tensor_tensor(oh, cand[:], bc(best[:], 2, E), ALU.is_equal))
                        if k == 0:
                            st.chain(dve.scalar_tensor_tensor(out=lg[:], in0=oh, scalar=-1000.0, in1=lg[:],
                                                              op0=ALU.mult, op1=ALU.add))
                    wait(dve, counted, g)
                    dve.tensor_tensor(both[:], chosen[:, 0, tiles, :], chosen[:, 1, tiles, :], ALU.add).then_inc(chose, 1)
                    dve.wait_ge(counted, g + 1)
                    st.chain(dve.tensor_copy(counts[:, :, 1:].rearrange("p e j -> p j e"), ps_c[:, 1]))
                    flat = lambda t: t[:].rearrange("p e j -> p (e j)")
                    st.chain(dve.tensor_tensor_scan(flat(upto), flat(keep), flat(counts), 0.0, ALU.mult, ALU.add))
                    st.chain(dve.tensor_copy(counts[:, :, 0], upto[:, :, GT]))
                    place = upto[:, :, 0:GT]
                    st.chain(dve.tensor_tensor(place, ps_c[:, 0].rearrange("p j e -> p e j"), place, ALU.add))
                    st.chain(dve.tensor_tensor(prod[:], chosen[:, :, tiles, :], bc(place.rearrange("p e j -> p j e"), 1, 2),
                                               ALU.mult))
                    st.chain(dve.tensor_reduce(sent_f[:, :, tiles], prod[:], AX.X, ALU.add))
                    if g >= 2:
                        for h in range(2):
                            dve.wait_ge(gone[g - 2][h], 32 * HT)
                    dve.tensor_copy(sent[u][:], sent_f[:, :, tiles]).then_inc(placed, 1)

                take_stats(0)
                norm(0)
                take_stats(1)
                dve.wait_ge(made, 4)
                st.did(dve.memset(keep[:], 1.0))
                st.did(dve.memset(one_e[:], 1.0))
                st.did(dve.tensor_copy(counts[:, :, 0], region[:]))
                st.settle()
                st.chain(dve.memset(keep[:, :, 0:1], 0.0))
                norm(1)

                def make_pieces(kc):
                    def take_low(p):
                        dve.wait_ge(high, p + 1)
                        rows = slice(p % KC * P, (p % KC + 1) * P)
                        dve.tensor_tensor(M[:, kc, 1, :, rows], tab[p % TB][:].rearrange("p r e -> p e r"),
                                          M[:, kc, 0, :, rows].bitcast(F32), ALU.subtract).then_inc(low, 1)

                    dve.wait_ge(w_turned, kc + 1)
                    for p in range(kc * KC, (kc + 1) * KC):
                        t = tab[p % TB][:].rearrange("p r e -> p e r")
                        dve.wait_ge(tab_in[p % TB], 16 * (p // TB + 1))
                        dve.tensor_tensor(t, bc(ps_w[:, p % KC * P:(p % KC + 1) * P], 1, E), t, ALU.add).then_inc(added, 1)
                        if p % KC > 0:
                            take_low(p - 1)
                    take_low(p)

                if make:
                    rank(0)
                    rank(1)
                    take_stats(2)
                    norm(2)
                    make_pieces(0)
                    take_stats(3)
                    norm(3)
                    rank(2)
                    make_pieces(1)
                    rank(3)
                else:
                    for g in range(NG):
                        rank(g)
                        if g + 2 < NG:
                            take_stats(g + 2)
                            norm(g + 2)
                last = counts[:, :, 0]
                dve.tensor_copy(pad_i[:], last).then_inc(placed, 1)
                st.chain(dve.tensor_tensor(blocks[:], last, region[:], ALU.subtract))
                st.chain(dve.tensor_scalar(count_i[:], blocks[:], float(P - 1), None, ALU.add))
                st.chain(dve.tensor_scalar(count_i[:], count_i[:], 7, None, ALU.logical_shift_right))
                st.chain(dve.tensor_copy(blocks[:], count_i[:]))
                st.chain(dve.tensor_tensor_scan(blocks_to[:], one_e[:], blocks[:], 0.0, ALU.mult, ALU.add))
                st.chain(dve.tensor_tensor(before_e[:], blocks_to[:], blocks[:], ALU.subtract))
                dve.tensor_tensor(far[:], top[:, 1, :], top[:, 0, :], ALU.subtract).then_inc(far_s, 1)
                st.chain(dve.scalar_tensor_tensor(out=offset[:], in0=before_e[:], scalar=float(P), in1=region[:],
                                                  op0=ALU.mult, op1=ALU.subtract))
                for g in range(NG):
                    tiles = slice(g * GT, (g + 1) * GT)
                    st.chain(dve.tensor_tensor(prod[:], chosen[:, :, tiles, :],
                                               offset[:].unsqueeze(1).unsqueeze(1).broadcast_to([P, 2, GT, E]), ALU.mult))
                    st.chain(dve.tensor_reduce(shift[:, :, tiles], prod[:], AX.X, ALU.add))
                st.chain(dve.tensor_tensor(row_of[:], sent_f[:], shift[:], ALU.add))
                bb = bc(blk[:], 1, E - 1)
                st.chain(dve.tensor_tensor(over[:], bb, bc(blocks_to[:, 0:E - 1], 2, BLOCKS), ALU.is_ge))
                st.chain(dve.tensor_reduce(te[:], over[:].rearrange("p e j -> p j e"), AX.X, ALU.add))
                st.chain(dve.tensor_tensor(over[:], over[:], bc(blocks[:, 0:E - 1], 2, BLOCKS), ALU.mult))
                st.chain(dve.tensor_reduce(tb[:], over[:].rearrange("p e j -> p j e"), AX.X, ALU.add))
                st.did(dve.tensor_copy(tile_tab[:, 0, :], te[0:1, :]))
                st.chain(dve.tensor_tensor(tb[:], blk[:], tb[:], ALU.subtract))
                st.chain(dve.scalar_tensor_tensor(out=tb[:], in0=blk[:], scalar=blocks_to[:, E - 1:E], in1=tb[:],
                                                  op0=ALU.is_lt, op1=ALU.mult))
                st.did(dve.tensor_scalar(te[:], te[:], float(REGION), None, ALU.mult))
                st.chain(dve.tensor_scalar(tb[:], tb[:], float(P), None, ALU.mult))
                st.chain(dve.tensor_tensor(tb[:], tb[:], te[:], ALU.add))
                st.chain(dve.tensor_copy(tile_tab[:, 1, :], tb[0:1, :]))
                dve.wait_ge(end, 1)
                st.chain(dve.tensor_scalar(w0[:], far[:], 1.0, None, ALU.add))
                st.chain(dve.reciprocal(w0[:], w0[:]))
                st.did(dve.tensor_scalar(gate[:, 0, :], w0[:], 0.5, None, ALU.mult))
                st.chain(dve.tensor_tensor(far[:], w0[:], far[:], ALU.mult))
                st.chain(dve.tensor_scalar(gate[:, 1, :], far[:], 0.5, None, ALU.mult))
                if make:
                    make_pieces(2)
                    make_pieces(3)

            @block.tensor
            def _(pe):
                pe.wait_ge(gw_in, 16)
                for kc in range(KC):
                    m = pe.transpose(ps_T[1][:, kc, 0:E], gw[:, kc * P:(kc + 1) * P], cst["ident"][0:E, 0:E])
                m.then_inc(gw_T, 1)
                pe.wait_ge(gw_T, 2)

                def turn(n):
                    pe.wait_ge(normed, n + 1)
                    wait(pe, copied, n - 3)
                    for kc in range(KC):
                        m = pe.transpose(ps_T[n % 4][:, kc, :], xn[n // GT % NX][:, n % GT, kc * P:(kc + 1) * P],
                                         cst["ident"][:])
                    m.then_inc(turned, 1)

                def multiply(q):
                    pe.wait_ge(copied, 2 * q + 2)
                    wait(pe, taken, q)
                    for kc in range(KC):
                        m = pe.matmul(ps_lT[:], gwT[:, kc, :], xT[q % 2][:, kc, :], start=(kc == 0), stop=(kc == KC - 1))
                    m.then_inc(multiplied, 1)

                def turn_back(q):
                    pe.wait_ge(taken, q + 1)
                    wait(pe, clipped, q // QG)
                    for t in range(2):
                        n = 2 * q + t
                        m = pe.transpose(ps_l[:, n % GT, :], lT[:, t * P:(t + 1) * P], cst["ident"][0:E, 0:E])
                    m.then_inc(scored, 1)

                def count(g):
                    u = g % 2
                    pe.wait_ge(chose, g + 1)
                    wait(pe, placed, g)
                    pe.matmul(ps_c[:, 0], cst["before"][:], both[:], start=True, stop=True)
                    pe.matmul(ps_c[:, 1], cst["ones"][:], both[:], start=True, stop=True).then_inc(counted, 1)

                def turn_pair(q):
                    turn(2 * q)
                    turn(2 * q + 1)

                def turn_weights(kc):
                    wait(pe, added, kc * KC)
                    for rb in range(KC):
                        m = pe.transpose(ps_w[:, rb * P:(rb + 1) * P], w_sb[:, rb, kc * P:(kc + 1) * P], cst["ident"][:])
                    m.then_inc(w_turned, 1)

                if make:
                    for g in range(NG):
                        if g == 2:
                            pe.wait_ge(w_in, 16)
                        if g >= 2:
                            turn_weights(g - 2)
                        turn_pair(g * QG)
                        for q in range(g * QG, (g + 1) * QG):
                            if q % QG + 1 < QG:
                                turn_pair(q + 1)
                            if q % QG > 0:
                                turn_back(q - 1)
                            multiply(q)
                            if g == 1 and q % QG == 1:
                                count(0)
                        turn_back(q)
                        if g == NG - 1:
                            turn_weights(2)
                        if g > 0:
                            count(g)
                    turn_weights(3)
                else:
                    turn_pair(0)
                    for q in range(NT // 2):
                        if q + 1 < NT // 2:
                            turn_pair(q + 1)
                        if q > 0:
                            turn_back(q - 1)
                        multiply(q)
                        if q > QG and q % QG == 1:
                            count(q // QG - 1)
                    turn_back(NT // 2 - 1)
                    count(NG - 1)

            @block.scalar
            def _(act):
                act.preload_act_table_set("natural_log_exp_and_others")
                act.wait_ge(made, 1)
                act.wait_ge(gw_T, 1)
                act.copy(gwT[:], ps_T[1][:, :, 0:E]).then_inc(gw_T, 1)
                def take_rstd(g):
                    for h in range(2):
                        n = 2 * g + h
                        act.wait_ge(stats, (n + 1) * HT)
                        wait(act, normed, (n - 1) * HT)
                        act.activation(rstd[h][:], mv[h][:, :, 1], ACT.Ln, bias=eps[:]).then_inc(logged, 1)
                        act.wait_ge(logged, n + 1)
                        act.activation(rstd[h][:], rstd[h][:], ACT.Exp, scale=-0.5).then_inc(rsqrt, 1)

                def take_logits(q):
                    act.wait_ge(multiplied, q + 1)
                    wait(act, scored, q)
                    act.copy(lT[:], ps_lT[:]).then_inc(taken, 1)

                def take_pair(q):
                    for n in (2 * q, 2 * q + 1):
                        act.wait_ge(turned, n + 1)
                        wait(act, multiplied, q - 1)
                        act.copy(xT[q % 2][:, :, n % 2 * P:(n % 2 + 1) * P], ps_T[n % 4][:]).then_inc(copied, 1)

                def take_high(p):
                    act.wait_ge(added, p + 1)
                    act.copy(M[:, p // KC, 0, :, p % KC * P:(p % KC + 1) * P],
                             tab[p % TB][:].rearrange("p r e -> p e r")).then_inc(high, 1)

                take_rstd(0)
                if make:
                    for g in range(NG):
                        if g >= 2:
                            take_rstd(g)
                        for q in range(g * QG, (g + 1) * QG):
                            take_pair(q)
                            if q % QG > 0:
                                take_logits(q - 1)
                            if q == 1:
                                take_rstd(1)
                            if g >= 2:
                                take_high((g - 2) * KC + q % QG)
                        take_logits(q)
                else:
                    for q in range(NT // 2):
                        take_pair(q)
                        if q > 0:
                            take_logits(q - 1)
                        if q % QG == 1 and q // QG + 1 < NG:
                            take_rstd(q // QG + 1)
                    take_logits(NT // 2 - 1)
                act.wait_ge(far_s, 1)
                act.activation(far[:], far[:], ACT.Exp).then_inc(end, 1)
                if make:
                    for p in range(2 * KC, PIECES):
                        take_high(p)


def split_matmul(pe, out, lhs, rhs, first=True, last=True):
    for n, (a, b) in enumerate(((0, 0), (0, 1), (1, 0))):
        m = pe.matmul(out, lhs[a], rhs[b], start=first and n == 0, stop=last and n == 2)
    return m


def experts(nc, cst, name, M, tile_tab, dispatched, routed, m_store=None, ahead=None):
    with Phase(nc, name, recycle=True) as ph:
        sb, sem = ph.sb, ph.sem
        DEEP = 4
        xt = [sb(f"xt{r}", [P, D], F32R) for r in range(DEEP)]
        xT = [[sb(f"xT{u}{h}", [P, KC, P], F32R) for h in range(2)] for u in range(2)]
        yt = [sb(f"yt{u}", [P, D]) for u in range(2)]
        ps_T = [ph.ps(f"ps_T{u}", [P, KC, P]) for u in range(2)]
        ps_y = [ph.ps(f"ps_y{u}", [P, D]) for u in range(2)]
        xt_in = [sem(f"xt_in{r}") for r in range(DEEP)]
        y_out = [sem(f"y_out{u}") for u in range(2)]
        kept = sem("kept")
        turned, high, low, multiplied, y_ready = (sem("turned"), sem("high"), sem("low"), sem("multiplied"), sem("y_ready"))
        QB = BLOCKS // DEEP
        with nc.Block() as block:
            @block.sync
            def _(sp):
                for u in range(2):
                    sp.sem_inc(y_out[u], 16)

                def load(r, n):
                    row = sp.snap(sp.value_load(tile_tab[0:1, 1, bass.ds(n, 1)], min_val=0,
                                                max_val=(E - 1) * REGION + TOK))
                    sp.wait_ge(turned, n + 1)
                    sp.dma_start(xt[r][:].bitcast(F32), dispatched[bass.ds(row, P), :]).then_inc(xt_in[r], 16)

                def store(u, n):
                    row = sp.snap(n * P)
                    sp.wait_ge(y_ready, n + 3)
                    sp.dma_start(routed[bass.ds(row, P), :], yt[u][:]).then_inc(y_out[u], 16)

                for r in range(DEEP):
                    load(r, r)
                with sp.Fori(0, QB - 1) as quad:
                    for r in range(DEEP):
                        store(r % 2, quad * DEEP + r)
                        load(r, quad * DEEP + DEEP + r)
                for r in range(DEEP):
                    store(r % 2, BLOCKS - DEEP + r)
                for u in range(2):
                    sp.wait_ge(y_out[u], 16 * (BLOCKS // 2 + 1))

            def turn(pe, r, n, quad):
                pe.wait_ge(xt_in[r], (quad + 1) * 16)
                pe.wait_ge(low, n + 1)
                for kc in range(KC):
                    m = pe.transpose(ps_T[r % 2][:, kc, :].bitcast(F32R), xt[r][:, kc * P:(kc + 1) * P], cst["ident_r"][:])
                m.then_inc(turned, 1)

            def multiply(pe, u, n):
                e = pe.value_load(tile_tab[0:1, 0, bass.ds(n, 1)] if not isinstance(n, int)
                                  else tile_tab[0:1, 0, n:n + 1], min_val=0, max_val=E - 1)
                pe.wait_ge(low, n + 3)
                pe.wait_ge(y_ready, n + 1)
                for kc in range(KC):
                    m = split_matmul(pe, ps_y[u][:].unsqueeze(1), [xT[u][h][:, kc, :] for h in range(2)],
                                     [M[:, kc, h, bass.ds(e, 1), :] for h in range(2)], kc == 0, kc == KC - 1)
                m.then_inc(multiplied, 1)

            @block.tensor
            def _(pe):
                pe.sem_inc(turned, DEEP)
                pe.sem_inc(multiplied, 2)
                turn(pe, 0, 0, 0)
                with pe.Fori(0, QB - 1) as quad:
                    for r in range(DEEP):
                        n = quad * DEEP + r
                        turn(pe, (r + 1) % DEEP, n + 1, quad + (r + 1) // DEEP)
                        multiply(pe, r % 2, n)
                for r in range(DEEP):
                    n = BLOCKS - DEEP + r
                    if r + 1 < DEEP:
                        turn(pe, r + 1, n + 1, QB - 1)
                    multiply(pe, r % 2, n)

            @block.vector
            def _(dve):
                dve.sem_inc(low, 2)
                with dve.Fori(0, BLOCKS // 2) as pair:
                    for u in range(2):
                        n = pair * 2 + u
                        dve.wait_ge(high, n + 1)
                        dve.tensor_tensor(xT[u][1][:], ps_T[u][:], xT[u][0][:].bitcast(F32), ALU.subtract).then_inc(low, 1)

            @block.scalar
            def _(act):
                def take_high(u, n):
                    act.wait_ge(turned, n + 1 + DEEP)
                    act.wait_ge(multiplied, n + 1)
                    act.copy(xT[u][0][:], ps_T[u][:]).then_inc(high, 1)

                def take_y(u, n, pair):
                    act.wait_ge(multiplied, n + 3)
                    act.wait_ge(y_out[u], pair * 16 + 16)
                    act.copy(yt[u][:], ps_y[u][:]).then_inc(y_ready, 1)

                act.sem_inc(y_ready, 2)
                take_high(0, 0)
                with act.Fori(0, BLOCKS // 2 - 1) as pair:
                    for u in range(2):
                        n = pair * 2 + u
                        take_high(1 - u, n + 1)
                        take_y(u, n, pair)
                take_high(1, BLOCKS - 1)
                for u in range(2):
                    take_y(u, BLOCKS - 2 + u, BLOCKS // 2 - 1)

            @block.gpsimd
            def _(pool):
                if m_store is not None:
                    kept_v = M[:].rearrange("p kc hf e r -> p (kc hf e) r").bitcast(F32)
                    store_v = m_store.rearrange("p kc hf e r -> p (kc hf e) r")
                    with pool.Fori(0, KC * 2 * E) as n:
                        pool.wait_ge(multiplied, n + 3)
                        pool.dma_start(store_v[:, bass.ds(n, 1), :], kept_v[:, bass.ds(n, 1), :]).then_inc(kept, 16)
                    pool.wait_ge(kept, 16 * KC * 2 * E)
                if ahead is not None:
                    x, held = ahead
                    x_v = x.rearrange("(j p) d -> p j d", p=P)
                    with pool.Fori(0, held.shape[1]) as j:
                        pool.wait_ge(multiplied, j * 2 + 3)
                        pool.dma_start(held[:, bass.ds(j, 1), :], x_v[:, bass.ds(j, 1), :]).then_inc(kept, 16)
                    pool.wait_ge(kept, 16 * held.shape[1])


def combine(nc, name, x, held, space, routed, gate, row_of, out):
    NK = held.shape[1]
    DEEP = 4
    with Phase(nc, name, recycle=True) as ph:
        sb, sem = ph.sb, ph.sem
        rest = space[:, 1, 0, 0:NT - NK].bitcast(F32)
        y = [[space[:, 0, k, r].bitcast(F32) for k in range(2)] for r in range(DEEP)]
        s = [sb(f"s{r}", [P, D]) for r in range(DEEP)]
        res = [sb(f"res{r}", [P, D]) for r in range(DEEP)]
        idx = [sb(f"idx{r}", [P, 2], I32) for r in range(DEEP)]
        rest_in = sem("rest_in")
        y_in = [sem(f"y_in{r}") for r in range(DEEP)]
        out_s = [sem(f"out{r}") for r in range(DEEP)]
        idx_in, used, first, ordered = sem("idx_in"), sem("used"), sem("first"), sem("ordered")
        out_v = out.rearrange("(j p) d -> j p d", p=P)

        def held_tiles(eng, body):
            with eng.Fori(0, NK // DEEP) as quad:
                for r in range(DEEP):
                    body(quad * DEEP + r, r, quad, held, quad * DEEP + r)

        def rest_tiles(eng, body):
            with eng.Fori(0, (NT - NK) // DEEP) as quad:
                for r in range(DEEP):
                    body(quad * DEEP + (NK + r), r, quad + NK // DEEP, rest, quad * DEEP + r)

        with nc.Block() as block:
            @block.sync
            def _(sp):
                for r in range(DEEP):
                    sp.sem_inc(out_s[r], 16)
                sp.dma_start(rest, x[NK * P:, :].rearrange("(j p) d -> p j d", p=P)).then_inc(rest_in, 16)

                def store(j, r, quad, *_):
                    row = sp.snap(j)
                    sp.wait_ge(used, j + 1 + DEEP)
                    sp.dma_start(out_v[bass.ds(row, 1)].rearrange("a p d -> (a p) d"), res[r][:]).then_inc(out_s[r], 16)
                held_tiles(sp, store)
                rest_tiles(sp, store)
                for r in range(DEEP):
                    sp.wait_ge(out_s[r], 16 * (NT // DEEP + 1))

            @block.gpsimd
            def _(pool):
                def gather(j, r, *_):
                    pool.wait_ge(used, j + 1)
                    pool.tensor_copy(idx[r][:].unsqueeze(2), row_of[:, :, bass.ds(j, 1)]).then_inc(idx_in, 1)
                    pool.wait_ge(idx_in, j + 1)
                    pool.sem_inc(ordered, 1)
                    for k in range(2):
                        pool.indirect_dma_start(y[r][k], None, routed,
                                                bass.IndirectOffsetOnAxis(ap=idx[r][:, k:k + 1], axis=0)).then_inc(y_in[r], 16)
                held_tiles(pool, gather)
                rest_tiles(pool, gather)

            @block.vector
            def _(dve):
                dve.sem_inc(used, DEEP)

                def add(j, r, quad, rows, at):
                    dve.wait_ge(y_in[r], (quad + 1) * 32)
                    dve.scalar_tensor_tensor(out=s[r][:].unsqueeze(1), in0=y[r][0].unsqueeze(1), scalar=gate[:, 0, bass.ds(j, 1)],
                                             in1=rows[:, bass.ds(at, 1), :], op0=ALU.mult, op1=ALU.add).then_inc(first, 1)
                    dve.wait_ge(first, j + 1)
                    dve.wait_ge(out_s[r], (quad + 1) * 16)
                    dve.scalar_tensor_tensor(out=res[r][:], in0=y[r][1], scalar=gate[:, 1, bass.ds(j, 1)],
                                             in1=s[r][:], op0=ALU.mult, op1=ALU.add).then_inc(used, 1)
                held_tiles(dve, add)
                dve.wait_ge(rest_in, 16)
                rest_tiles(dve, add)


def wait(eng, sem, n):
    if not (isinstance(n, int) and n <= 0):
        eng.wait_ge(sem, n)


def col(ap, t):
    return ap[:, t:t + 1] if isinstance(t, int) else ap[:, bass.ds(t, 1)]


def pipeline(eng, step, lead):
    first, last = 4, NT - 4
    for i in range(lead, first):
        step(i, i % 4, i // 4)
    with eng.Fori(0, (last - first) // 4) as quad:
        for s in range(4):
            step(quad * 4 + (first + s), s, quad + first // 4)
    for i in range(last, NT + 2):
        step(i, i % 4, i // 4)


def inside(t):
    return not isinstance(t, int) or 0 <= t < NT


def attention(nc, cst, x, routed, gate, row_of, w, base, h2T):
    QK, V, G, O = range(4)
    HG = 4
    with Phase(nc, "at", recycle=True) as ph:
        sb, sem = ph.sb, ph.sem
        names = ("ws_scaled w_high w_low w_done consts "
                 "s x1 bn bn_ok mv ve rstd y t1 t2 r2 h hT_t hT_hi hT_lo low low_sb gate_p z ab ez lz ls sig gs bs dec "
                 "eb enb es decay qe ke kd qk_t keT qbd0 qbd1 v v_sb u_p s1 s2 s_tmp a0 a1 am0 am1 qk o osq ss ms8 r8 on og "
                 "og_t ogT_hi ogT_lo wo x2 sq msd rh2 h2 h2_t h2_hi h2_lo base idx_in idx_ok").split()
        S = {n: sem(n) for n in names}
        x_in = [sem(f"x_in{u}") for u in range(2)]
        y_in = [sem(f"y_in{u}") for u in range(2)]
        h_out = [sem(f"h_out{u}") for u in range(2)]
        b_out = [sem(f"b_out{u}") for u in range(2)]
        w_in = [sem(f"w_in{n}") for n in range(4)]
        small_in = sem("small_in")
        wh = [[sb(f"w{n}{h}", [P, KC, D], F32R) for h in range(2)] for n in range(4)]
        w1 = sb("w1f", [P, KC, LOW])
        w1h = [sb(f"w1h{h}", [P, KC, LOW], F32R) for h in range(2)]
        w2b = sb("w2b", [LOW + 1, KEY])
        n1, n1q = sb("n1", [P, KC]), sb("n1q", [P, KC])
        gn = sb("gn", [P, 1])
        cum16, suf16, causal = sb("cum16", [P, P]), sb("suf16", [P, P]), sb("causal", [P, P])
        chunk16, hmask, keep = sb("chunk16", [P, 2]), sb("hmask", [P, HG, P]), sb("keep", [P, NT // 4])
        power = sb("power", [P, H])
        two = lambda n, s, dt=F32: [sb(f"{n}{u}", s, dt) for u in range(2)]
        xt, s_, h, v_sb, gs, og, x2, h2, bt = (two(n, [P, D]) for n in
                                               "xt s h v gs og x2 h2 bt".split())
        h2T_sb = two("h2T", [P, 2, KC, P], F32R)
        yk = [two(f"yk{k}_", [P, D]) for k in range(2)]
        x1, y = ([sb(f"{n}{r}", [P, D]) for r in range(4)] for n in ("x1_", "y_"))
        idx = two("idx", [P, 2], I32)
        bn, mv, ve, t1, t2, rstd, r2 = (two(n, s) for n, s in (("bn", [P, 6]), ("mv", [P, 2]), ("ve", [P, 1]),
                                        ("t1", [P, 1]), ("t2", [P, 1]), ("rstd", [P, 1]), ("r2", [P, 1])))
        hT = [two(f"hT{hf}_", [P, KC, P], F32R) for hf in range(2)]
        ogT = [sb(f"ogT{hf}", [P, KC, P], F32R) for hf in range(2)]
        low = two("low", [LOW + 1, P])
        stage = [sb(f"stage{n}", [P, KC, D]) for n in range(3)] + [sb("stage3", [P, 3 * (KEY + D)])]
        flat = [t[:].rearrange("p a b -> p (a b)") for t in stage[0:2]] + [None, stage[3][:]]
        ab, ez, lz = (flat[3][:, n * (KEY + D):(n + 1) * (KEY + D)] for n in range(3))
        ls = [flat[1][:, n * (KEY + D):(n + 1) * (KEY + D)] for n in range(2)]
        sig = flat[1][:, 2 * (KEY + D):2 * (KEY + D) + D]
        qbd = flat[0][:, 0:2 * D].rearrange("p (g n t) -> p g n t", g=2, n=HG)
        am = flat[0][:, 2 * D:4 * D].rearrange("p (n t) -> p n t", n=H)
        staged = [t[:] for t in stage[0:3]] + [flat[3][:, 0:KC * D].rearrange("p (kc n) -> p kc n", kc=KC)]
        eb, enb, es = sb("eb", [P, KEY]), sb("enb", [P, KEY]), sb("es", [P, KEY])
        decay = sb("decay", [P, 2, 2])
        qe, ke = sb("qe", [P, KEY]), sb("ke", [P, KEY])
        kd = two("kd", [P, KEY])
        keT = sb("keT", [P, 2, P])
        state = [sb(f"state{n}", [P, 2, HV]) for n in range(4)]
        s_tmp = sb("s_tmp", [P, 2, HV])
        osq, on = sb("osq", [P, D]), sb("on", [P, D])
        ss, ms8, r8 = sb("ss", [P, H]), sb("ms8", [P, H]), sb("r8", [P, H])
        sq, sqs, msd, rh2 = sb("sq", [P, D]), sb("sqs", [P, 1]), sb("msd", [P, 1]), sb("rh2", [P, 1])
        ps_T = ph.ps("ps_T", [P, KC, P])
        ps_qk = ph.ps("ps_qk", [P, D])
        ps_v = ph.ps("ps_v", [P, D])
        ps_zg = ph.ps("ps_zg", [P, 2 * D])
        ps_bs = ph.ps("ps_bs", [P, D])
        ps_a = [ph.ps(f"ps_a{g}", [P, HG, P]) for g in range(2)]
        ps_low, ps_dec = ps_zg[0:LOW, 0:P], ps_a[1][:, 0, 0:4]
        ps_z, ps_g, zg = ps_zg[:, D - KEY:D], ps_zg[:, D:2 * D], ps_zg[:, D - KEY:2 * D]
        ps_u = ps_qk[:, 0:4 * HV].rearrange("p (c g v) -> p c g v", c=2, g=2)

        W_ORDER = (G, V, QK, O)
        stage_of = {V: staged[0], QK: staged[1], O: staged[2], G: staged[3]}
        w_src = [(w["wq"], w["wk"]), (w["wv"],), (w["wg"],), (w["wo"],)]
        def w_scale(n, kc):
            if n == QK:
                return (slice(0, KEY), n1q[:, kc:kc + 1]), (slice(KEY, 2 * KEY), n1[:, kc:kc + 1])
            return (slice(0, D), gn[:, 0:1] if n == O else n1[:, kc:kc + 1]),

        x_v = x.rearrange("(j p) d -> j p d", p=P)
        base_v = base.rearrange("(j p) d -> j p d", p=P)

        def tile_of(ap, t):
            return ap[t] if isinstance(t, int) else ap[bass.ds(t, 1)].rearrange("a p d -> (a p) d")

        with nc.Block() as block:
            @block.sync
            def _(sp):
                sp.dma_start(w1[:], w["w1"].rearrange("(kc p) n -> p kc n", p=P)).then_inc(small_in, 16)
                sp.dma_start(w2b[0:LOW, :], w["w2"]).then_inc(small_in, 16)
                sp.dma_start(w2b[LOW:LOW + 1, :], w["gk_b"].rearrange("(o n) -> o n", o=1)).then_inc(small_in, 16)
                sp.dma_start(n1[:], w["norm1_w"].rearrange("(kc p) -> p kc", p=P),
                             allow_slow_non_contiguous=True).then_inc(small_in, 16)
                for c in range(2):
                    sp.dma_start(gn[c * HV:(c + 1) * HV, :], w["gnorm_w"].rearrange("(v o) -> v o", o=1)).then_inc(small_in, 16)
                def step(i, r, q):
                    t = i + 3
                    if inside(t):
                        row = t if isinstance(t, int) else sp.snap(t)
                        wait(sp, S["s"], t - 1)
                        sp.dma_start(xt[(r + 3) % 2][:], tile_of(x_v, row)).then_inc(x_in[(r + 3) % 2], 16)
                    t = i - 2
                    if inside(t):
                        row = t * P if isinstance(t, int) else sp.snap(t * P)
                        dst = h2T[:, :, :, row:row + P] if isinstance(t, int) else h2T[:, :, :, bass.ds(row, P)]
                        wait(sp, S["h2_lo"], t + 1)
                        sp.dma_start(dst, h2T_sb[r % 2][:].bitcast(F32)).then_inc(h_out[r % 2], 16)
                    t = i - 1
                    if inside(t):
                        row = t if isinstance(t, int) else sp.snap(t)
                        wait(sp, S["base"], t + 1)
                        sp.dma_start(tile_of(base_v, row), bt[(r + 1) % 2][:]).then_inc(b_out[(r + 1) % 2], 16)
                step(-3, 1, -1)
                for n in W_ORDER:
                    if n == QK:
                        sp.wait_ge(y_in[0], 32)
                    at = 0
                    for src in w_src[n]:
                        cols = src.shape[1]
                        sp.dma_start(stage_of[n][:, :, at:at + cols],
                                     src.rearrange("(kc p) n -> p kc n", p=P)).then_inc(w_in[n], 16)
                        at += cols
                pipeline(sp, step, -2)
                for u in range(2):
                    sp.wait_ge(h_out[u], 16 * NT // 2)
                    sp.wait_ge(b_out[u], 16 * NT // 2)

            @block.gpsimd
            def _(pool):
                made = Steps(pool, S["consts"])

                def ms(ap, v):
                    made.chain(pool.memset(ap, v))
                for ap, v in ((cum16, 1 / 16), (suf16, 1 / 16), (causal, 1.0), (chunk16, 0.0), (hmask, 0.0),
                              (keep, 1.0), (power, -0.5), (low[0], 1.0), (low[1], 1.0), (state[0], 0.0), (kd[0], 0.0), (kd[1], 0.0)):
                    ms(ap[:], v)
                for m, sign in ((cum16, 1), (causal, 1), (suf16, -1)):
                    made.chain(pool.affine_select(out=m[:], in_=m[:], compare_op=ALU.is_ge if sign > 0 else ALU.is_gt,
                                                  fill=0.0, base=0, pattern=[[sign, P]], channel_multiplier=-sign))
                ms(cum16[0:CHUNK, CHUNK:P], 0.0)
                ms(causal[0:CHUNK, CHUNK:P], 0.0)
                ms(suf16[CHUNK:P, 0:CHUNK], 0.0)
                for c in range(2):
                    ms(chunk16[c * CHUNK:(c + 1) * CHUNK, c:c + 1], 1 / 16)
                for n in range(HG):
                    ms(hmask[n * HK:(n + 1) * HK, n, :], 1.0)
                ms(keep[:].rearrange("p (a b) -> p a b", b=TILES_B // 4)[:, :, 0:1], 0.0)

                def step(i, r, q):
                    t = i - 1
                    if inside(t):
                        wait(pool, S["ms8"], t + 1)
                        pool.tensor_tensor(r8[:], ms8[:], power[:, 0:H], ALU.pow).then_inc(S["r8"], 1)
                    t = i + 3
                    if inside(t):
                        u = (r + 3) % 2
                        wait(pool, S["x1"], t - 1)
                        src = row_of[:, :, t:t + 1] if isinstance(t, int) else row_of[:, :, bass.ds(t, 1)]
                        pool.tensor_copy(idx[u][:].unsqueeze(2), src).then_inc(S["idx_in"], 1)
                        wait(pool, S["idx_in"], t + 1)
                        pool.sem_inc(S["idx_ok"], 1)
                        for k in range(2):
                            pool.indirect_dma_start(yk[k][u][:], None, routed,
                                                    bass.IndirectOffsetOnAxis(ap=idx[u][:, k:k + 1], axis=0)).then_inc(y_in[u], 16)
                    t = i + 2
                    if inside(t):
                        u = r % 2
                        wait(pool, S["ve"], t + 1)
                        pool.tensor_tensor(rstd[u][:], ve[u][:], power[:, 0:1], ALU.pow).then_inc(S["rstd"], 1)
                        wait(pool, S["t2"], t + 1)
                        pool.tensor_tensor(r2[u][:], t2[u][:], power[:, 0:1], ALU.pow).then_inc(S["r2"], 1)
                    t = i - 1
                    if inside(t):
                        u = (r + 1) % 2
                        wait(pool, S["x2"], t + 1)
                        wait(pool, b_out[u], (t + (r + 1) % 2 * -1) * 8)
                        pool.tensor_tensor(bt[u][:], x1[(r + 3) % 4][:], x2[u][:], ALU.add).then_inc(S["base"], 1)
                        wait(pool, S["msd"], i)
                        pool.tensor_tensor(rh2[:], msd[:], power[:, 0:1], ALU.pow).then_inc(S["rh2"], 1)
                pipeline(pool, step, -3)

            @block.scalar
            def _(act):
                act.preload_act_table_set("natural_log_exp_and_others")
                act.wait_ge(S["ws_scaled"], 1)
                for kc in range(KC):
                    op = act.activation(w1h[0][:, kc], w1[:, kc], ACT.Copy, scale=n1[:, kc:kc + 1])
                op.then_inc(S["w_high"], 1)
                for n in W_ORDER:
                    act.wait_ge(w_in[n], 16 * len(w_src[n]))
                    for kc in range(KC):
                        for cols, scale in w_scale(n, kc):
                            op = act.activation(wh[n][0][:, kc, cols], stage_of[n][:, kc, cols], ACT.Copy, scale=scale)
                    op.then_inc(S["w_high"], 1)

                def step(i, r, q):
                    u, nu = r % 2, (r + 1) % 2
                    if inside(i - 1):
                        wait(act, S["o"], i)
                        wait(act, S["ss"], i - 1)
                        act.activation(osq[:], ps_v[:], ACT.Square).then_inc(S["osq"], 1)
                    n, m = i + 1, i + 2
                    if inside(i):
                        wait(act, S["bs"], i + 1)
                        wait(act, S["kd"], i)
                        act.activation(eb[:], ps_bs[:, 0:KEY], ACT.Exp).then_inc(S["eb"], 1)
                        act.activation(enb[:], ps_bs[:, 0:KEY], ACT.Exp, scale=-1.0).then_inc(S["enb"], 1)
                        act.activation(es[:], ps_bs[:, KEY:2 * KEY], ACT.Exp).then_inc(S["es"], 1)
                        wait(act, S["dec"], i + 1)
                        wait(act, S["s2"], i)
                        act.activation(decay[:].rearrange("p g c -> p (g c)"), ps_dec, ACT.Exp).then_inc(S["decay"], 1)
                    if inside(n):
                        wait(act, S["low"], n + 1)
                        wait(act, S["z"], n - 1)
                        act.copy(low[nu][0:LOW, :], ps_low).then_inc(S["low_sb"], 1)
                    t = i - 2
                    if inside(t):
                        wait(act, S["h2_t"], t + 1)
                        wait(act, h_out[u], (t - r % 2) * 8)
                        act.copy(h2T_sb[u][:, 0], ps_T[:]).then_inc(S["h2_hi"], 1)
                    if inside(n):
                        wait(act, S["z"], n + 1)
                        wait(act, S["gate_p"], n + 1)
                        wait(act, S["ez"], n)
                        act.activation(ab, zg, ACT.Abs).then_inc(S["ab"], 1)
                        wait(act, S["ab"], n + 1)
                        wait(act, S["lz"], n)
                        act.activation(ez, ab, ACT.Exp, scale=-1.0).then_inc(S["ez"], 1)
                    if inside(i):
                        wait(act, S["qk_t"], i + 1)
                        wait(act, S["a1"], i)
                        act.copy(keT[:], ps_T[:, 2:4, :]).then_inc(S["keT"], 1)
                    if inside(n):
                        wait(act, S["ez"], n + 1)
                        wait(act, S["ls"], n)
                        act.activation(lz, ez, ACT.Ln, bias=1.0).then_inc(S["lz"], 1)
                        wait(act, S["ls"], n + 1)
                        wait(act, S["gs"], n)
                        act.activation(sig, ls[nu][:, KEY:], ACT.Exp).then_inc(S["sig"], 1)
                        wait(act, S["v"], n + 1)
                        wait(act, S["o"], n - 1)
                        act.copy(v_sb[nu][:], ps_v[:]).then_inc(S["v_sb"], 1)
                    if inside(i - 1):
                        wait(act, S["og_t"], i)
                        wait(act, S["wo"], i - 1)
                        act.copy(ogT[0][:], ps_T[:]).then_inc(S["ogT_hi"], 1)
                    if inside(m):
                        wait(act, S["hT_t"], m + 1)
                        wait(act, S["v"], m - 1)
                        wait(act, S["qk"], m - 1)
                        act.copy(hT[0][u][:], ps_T[:]).then_inc(S["hT_hi"], 1)
                    if inside(i - 1):
                        wait(act, S["x2"], i)
                        wait(act, S["msd"], i - 1)
                        act.activation(sq[:], x2[nu][:], ACT.Square, accum_out=sqs[:]).then_inc(S["sq"], 1)
                pipeline(act, step, -2)

            @block.vector
            def _(dve):
                dve.wait_ge(small_in, 96)
                dve.tensor_scalar(n1q[:], n1[:], float(HK) ** -0.5, None, ALU.mult).then_inc(S["ws_scaled"], 1)
                dve.wait_ge(S["ws_scaled"], 1)
                dve.wait_ge(S["w_high"], 1)
                for kc in range(KC):
                    op = dve.scalar_tensor_tensor(out=w1h[1][:, kc], in0=w1[:, kc], scalar=n1[:, kc:kc + 1],
                                                  in1=w1h[0][:, kc].bitcast(F32), op0=ALU.mult, op1=ALU.subtract)
                op.then_inc(S["w_low"], 1)

                def take_low(n):
                    dve.wait_ge(w_in[n], 16 * len(w_src[n]))
                    dve.wait_ge(S["w_high"], 2 + W_ORDER.index(n))
                    for kc in range(KC):
                        for cols, scale in w_scale(n, kc):
                            op = dve.scalar_tensor_tensor(out=wh[n][1][:, kc, cols], in0=stage_of[n][:, kc, cols], scalar=scale,
                                                          in1=wh[n][0][:, kc, cols].bitcast(F32), op0=ALU.mult, op1=ALU.subtract)
                    op.then_inc(S["w_low"], 1)

                dve.wait_ge(S["consts"], 25)

                def step(i, r, q):
                    u, nu = r % 2, (r + 1) % 2
                    n, j, m = i + 1, i - 1, i + 2
                    if inside(j):
                        wait(dve, S["osq"], j + 1)
                        dve.tensor_reduce(ss[:], osq[:].rearrange("p (h v) -> p h v", h=H), AX.X, ALU.add).then_inc(S["ss"], 1)
                        wait(dve, S["ss"], j + 1)
                        wait(dve, S["r8"], j)
                        dve.tensor_scalar(ms8[:], ss[:], 1.0 / HV, RMS_EPS, ALU.mult, ALU.add).then_inc(S["ms8"], 1)
                    if inside(i):
                        wait(dve, S["qk"], i + 1)
                        wait(dve, S["eb"], i + 1)
                        wait(dve, S["qk_t"], i)
                        dve.tensor_tensor(qe[:], ps_qk[:, 0:KEY], eb[:], ALU.mult).then_inc(S["qe"], 1)
                        wait(dve, S["enb"], i + 1)
                        dve.tensor_tensor(ke[:], ps_qk[:, KEY:], enb[:], ALU.mult).then_inc(S["ke"], 1)
                        wait(dve, S["es"], i + 1)
                        wait(dve, S["u_p"], i)
                        for c in range(2):
                            rows = slice(c * CHUNK, (c + 1) * CHUNK)
                            op = dve.tensor_tensor(kd[c][rows], ps_qk[rows, KEY:], es[rows], ALU.mult)
                        op.then_inc(S["kd"], 1)
                    if inside(i - 2):
                        wait(dve, S["h2_hi"], i - 1)
                        dve.tensor_tensor(h2T_sb[u][:, 1], ps_T[:], h2T_sb[u][:, 0].bitcast(F32), ALU.subtract).then_inc(S["h2_lo"], 1)
                    if inside(j):
                        wait(dve, S["r8"], j + 1)
                        wait(dve, S["og"], j)
                        dve.tensor_tensor(on[:].rearrange("p (h v) -> p h v", h=H), ps_v[:].rearrange("p (h v) -> p h v", h=H),
                                          bc(r8[:], 2, HV), ALU.mult).then_inc(S["on"], 1)
                        wait(dve, S["on"], j + 1)
                        wait(dve, S["og_t"], j - 1)
                        dve.tensor_tensor(og[nu][:], on[:], gs[nu][:], ALU.mult).then_inc(S["og"], 1)
                    if inside(m):
                        wait(dve, y_in[u], (m - r % 2) * 16 + 32)
                        wait(dve, x_in[u], (m - r % 2) * 8 + 16)
                        dve.scalar_tensor_tensor(out=s_[u][:], in0=yk[0][u][:], scalar=col(gate[:, 0], m), in1=xt[u][:],
                                                 op0=ALU.mult, op1=ALU.add).then_inc(S["s"], 1)
                        wait(dve, S["s"], m + 1)
                        wait(dve, S["base"], m - 3)
                        dve.scalar_tensor_tensor(out=x1[(r + 2) % 4][:], in0=yk[1][u][:], scalar=col(gate[:, 1], m), in1=s_[u][:],
                                                 op0=ALU.mult, op1=ALU.add).then_inc(S["x1"], 1)
                    if inside(i):
                        wait(dve, S["keT"], i + 1)
                        wait(dve, S["o"], i)
                        for g in range(2):
                            dve.tensor_tensor(qbd[:, g], bc(ps_T[:, g, :], 1, HG), hmask[:], ALU.mult).then_inc(S[f"qbd{g}"], 1)
                    if inside(n):
                        wait(dve, S["lz"], n + 1)
                        wait(dve, S["dec"], n - 1)
                        dve.scalar_tensor_tensor(out=ls[nu], in0=zg, scalar=0.0, in1=lz,
                                                 op0=ALU.min, op1=ALU.subtract).then_inc(S["ls"], 1)
                    if inside(i):
                        wait(dve, S["u_p"], i + 1)
                        wait(dve, S["decay"], i + 1)
                        wait(dve, S["s2"], i)
                        for g in range(2):
                            op = dve.scalar_tensor_tensor(out=state[2 * u + 1][:, g], in0=state[2 * u][:, g],
                                                         scalar=decay[:, g, 0:1], in1=ps_u[:, 0, g],
                                                         op0=ALU.mult, op1=ALU.add)
                        op.then_inc(S["s1"], 1)
                        wait(dve, S["s1"], i + 1)
                        wait(dve, S["o"], i)
                        nxt = state[(2 * u + 2) % 4] if r != 3 else s_tmp
                        for g in range(2):
                            op = dve.scalar_tensor_tensor(out=nxt[:, g], in0=state[2 * u + 1][:, g],
                                                         scalar=decay[:, g, 1:2], in1=ps_u[:, 1, g],
                                                         op0=ALU.mult, op1=ALU.add)
                        if r == 3:
                            op.then_inc(S["s_tmp"], 1)
                            wait(dve, S["s_tmp"], q + 1)
                            if inside(i + 1):
                                op = dve.tensor_scalar(state[0][:], s_tmp[:], col(keep, q + 1), None, ALU.mult)
                        if r != 3 or inside(i + 1):
                            op.then_inc(S["s2"], 1)
                    if inside(n):
                        wait(dve, S["sig"], n + 1)
                        wait(dve, S["og"], n - 1)
                        dve.tensor_tensor(gs[nu][:], ps_g, sig, ALU.mult).then_inc(S["gs"], 1)
                    if inside(j):
                        wait(dve, S["ogT_hi"], j + 1)
                        dve.tensor_tensor(ogT[1][:], ps_T[:], ogT[0][:].bitcast(F32), ALU.subtract).then_inc(S["ogT_lo"], 1)
                    if inside(m):
                        wait(dve, S["x1"], m + 1)
                        dve.bn_stats(bn[u][:], x1[(r + 2) % 4][:]).then_inc(S["bn"], 1)
                        wait(dve, S["bn"], m + 1)
                        dve.sem_inc(S["bn_ok"], 1)
                        dve.bn_aggr(mv[u][:], bn[u][:]).then_inc(S["mv"], 1)
                        wait(dve, S["mv"], m + 1)
                        dve.tensor_scalar(ve[u][:], mv[u][:, 1:2], LN_EPS, None, ALU.add).then_inc(S["ve"], 1)
                    if inside(i):
                        for g in range(2):
                            wait(dve, S[f"a{g}"], i + 1)
                            dve.tensor_tensor(am[:, g * HG:(g + 1) * HG], ps_a[g][:], bc(causal[:], 1, HG),
                                              ALU.mult).then_inc(S[f"am{g}"], 1)
                    if inside(m):
                        wait(dve, S["rstd"], m + 1)
                        dve.tensor_scalar(y[(r + 2) % 4][:], x1[(r + 2) % 4][:], mv[u][:, 0:1], rstd[u][:],
                                          ALU.subtract, ALU.mult).then_inc(S["y"], 1)
                        dve.tensor_scalar(t1[u][:], mv[u][:, 1:2], rstd[u][:], None, ALU.mult).then_inc(S["t1"], 1)
                        wait(dve, S["t1"], m + 1)
                        dve.tensor_scalar(t2[u][:], t1[u][:], rstd[u][:], RMS_EPS, ALU.mult, ALU.add).then_inc(S["t2"], 1)
                        wait(dve, S["r2"], m + 1)
                        wait(dve, S["hT_t"], m - 1)
                        dve.tensor_scalar(h[u][:], y[(r + 2) % 4][:], r2[u][:], None, ALU.mult).then_inc(S["h"], 1)
                    if inside(j):
                        wait(dve, S["wo"], j + 1)
                        wait(dve, S["h2"], j - 1)
                        wait(dve, S["base"], j - 1)
                        dve.tensor_tensor(x2[nu][:], ps_bs[:], y[(r + 3) % 4][:], ALU.add).then_inc(S["x2"], 1)
                    if inside(m):
                        wait(dve, S["hT_hi"], m + 1)
                        dve.tensor_tensor(hT[1][u][:], ps_T[:], hT[0][u][:].bitcast(F32), ALU.subtract).then_inc(S["hT_lo"], 1)
                    if inside(j):
                        wait(dve, S["sq"], j + 1)
                        wait(dve, S["rh2"], j)
                        dve.tensor_scalar(msd[:], sqs[:], 1.0 / D, RMS_EPS, ALU.mult, ALU.add).then_inc(S["msd"], 1)
                        wait(dve, S["rh2"], j + 1)
                        wait(dve, S["h2_t"], j - 1)
                        dve.tensor_scalar(h2[nu][:], x2[nu][:], rh2[:], None, ALU.mult).then_inc(S["h2"], 1)
                take_low(G)
                take_low(V)
                step(-2, 2, -1)
                take_low(QK)
                take_low(O)
                dve.wait_ge(S["w_low"], 5)
                pipeline(dve, step, -1)

            @block.tensor
            def _(pe):
                pe.wait_ge(S["consts"], 25)

                def turn(src, blocks, at=0):
                    for kc in range(blocks):
                        op = pe.transpose(ps_T[:, at + kc, :], src[:, kc * P:(kc + 1) * P], cst["ident"][:])
                    return op

                def project(out, u, wt):
                    for kc in range(KC):
                        op = split_matmul(pe, out, [hT[hf][u][:, kc, :] for hf in range(2)],
                                         [wt[hf][:, kc, :] for hf in range(2)], kc == 0, kc == KC - 1)
                    return op

                def step(i, r, q):
                    def weights(n):
                        if isinstance(i, int) and i == (1 if n == O else -1):
                            pe.wait_ge(S["w_low"], 2 + W_ORDER.index(n))

                    u, nu = r % 2, (r + 1) % 2
                    n, j, t, m = i + 1, i - 1, i - 2, i + 2
                    if inside(i):
                        wait(pe, S["ls"], i + 1)
                        wait(pe, S["x2"], i - 1)
                        pe.matmul(ps_bs[:, 0:KEY], cum16[:], ls[u][:, 0:KEY], start=True, stop=True)
                        pe.matmul(ps_bs[:, KEY:], suf16[:], ls[u][:, 0:KEY], start=True, stop=True).then_inc(S["bs"], 1)
                        wait(pe, S["am1"], i)
                        for g in range(2):
                            op = pe.matmul(ps_dec[:, 2 * g:2 * g + 2], ls[u][:, g * P:(g + 1) * P], chunk16[:],
                                          start=True, stop=True)
                        op.then_inc(S["dec"], 1)
                    if inside(n):
                        if isinstance(i, int) and i == -1:
                            pe.wait_ge(S["w_low"], 1)
                        wait(pe, S["hT_lo"], n + 1)
                        wait(pe, S["low_sb"], n)
                        for kc in range(KC):
                            op = split_matmul(pe, ps_low, [w1h[hf][:, kc, :] for hf in range(2)],
                                             [hT[hf][nu][:, kc, :] for hf in range(2)], kc == 0, kc == KC - 1)
                        op.then_inc(S["low"], 1)
                    if inside(t):
                        wait(pe, S["h2"], t + 1)
                        turn(h2[u], KC).then_inc(S["h2_t"], 1)
                    if inside(n):
                        wait(pe, S["gs"], n)
                        weights(G)
                        project(ps_g, nu, wh[G]).then_inc(S["gate_p"], 1)
                        wait(pe, S["low_sb"], n + 1)
                        pe.matmul(ps_z, low[nu][:], w2b[:], start=True, stop=True).then_inc(S["z"], 1)
                    if inside(i):
                        wait(pe, S["ke"], i + 1)
                        wait(pe, S["h2_lo"], i - 1)
                        turn(qe, 2)
                        turn(ke, 2, 2).then_inc(S["qk_t"], 1)
                    if inside(n):
                        wait(pe, S["on"], n - 1)
                        weights(V)
                        project(ps_v[:], nu, wh[V]).then_inc(S["v"], 1)
                    if inside(i):
                        wait(pe, S["kd"], i + 1)
                        wait(pe, S["v_sb"], i + 1)
                        for c in range(2):
                            for hd in range(H):
                                g, hh = divmod(hd, HG)
                                op = pe.matmul(ps_u[hh * HK:(hh + 1) * HK, c, g], kd[c][:, hd * HK:(hd + 1) * HK],
                                               v_sb[u][:, hd * HV:(hd + 1) * HV], start=True, stop=True)
                        op.then_inc(S["u_p"], 1)
                    if inside(j):
                        wait(pe, S["og"], j + 1)
                        wait(pe, S["keT"], min(j + 2, NT) if isinstance(j, int) else j + 2)
                        wait(pe, S["qbd1"], min(j + 2, NT) if isinstance(j, int) else j + 2)
                        if isinstance(j, int) and j == NT - 1:
                            wait(pe, S["h2_lo"], NT - 1)
                        turn(og[nu], KC).then_inc(S["og_t"], 1)
                    if inside(i):
                        wait(pe, S["keT"], i + 1)
                        for g in range(2):
                            wait(pe, S[f"qbd{g}"], i + 1)
                            wait(pe, S["decay"], i + 1)
                            pe.matmul(ps_a[g][:], keT[:, g], qbd[:, g], start=True, stop=True).then_inc(S[f"a{g}"], 1)
                    if inside(n):
                        wait(pe, S["s2"], n)
                        weights(QK)
                        project(ps_qk[:], nu, wh[QK]).then_inc(S["qk"], 1)
                    weights(O)
                    if inside(j):
                        wait(pe, S["ogT_lo"], j + 1)
                        wait(pe, S["es"], min(j + 2, NT) if isinstance(j, int) else j + 2)
                        for kc in range(KC):
                            op = split_matmul(pe, ps_bs[:], [ogT[hf][:, kc, :] for hf in range(2)],
                                             [wh[O][hf][:, kc, :] for hf in range(2)], kc == 0, kc == KC - 1)
                        op.then_inc(S["wo"], 1)
                    if inside(m):
                        wait(pe, S["h"], m + 1)
                        turn(h[u], KC).then_inc(S["hT_t"], 1)
                    if inside(i):
                        wait(pe, S["v_sb"], min(i + 2, NT) if isinstance(i, int) else i + 2)
                        wait(pe, S["s1"], i + 1)
                        for g in range(2):
                            wait(pe, S[f"am{g}"], i + 1)
                            for hh in range(HG):
                                hd = g * HG + hh
                                pe.matmul(ps_v[:, hd * HV:(hd + 1) * HV], am[:, hd], v_sb[u][:, hd * HV:(hd + 1) * HV],
                                          start=(hd == 0), stop=False, skip_group_check=True)
                                for c in range(2):
                                    op = pe.matmul(ps_v[c * CHUNK:(c + 1) * CHUNK, hd * HV:(hd + 1) * HV],
                                                  qbd[:, g, hh, c * CHUNK:(c + 1) * CHUNK], state[2 * u + c][:, g],
                                                  start=False, stop=(hd == H - 1), skip_group_check=True)
                        op.then_inc(S["o"], 1)
                pipeline(pe, step, -2)


def swiglu(nc, h2T, norm_w, w_gate, w_up, w_down, base, out):
    SPAN = 512
    NSP = TOK // SPAN
    TS = SPAN // P
    with Phase(nc, "ff") as ph:
        sb, sem = ph.sb, ph.sem
        wgu = [[sb(f"w{m}{hf}", [P, NF, KC, P], F32R) for hf in range(2)] for m in range(2)]
        wd = [sb(f"wd{hf}", [P, NF, D], F32R) for hf in range(2)]
        nw = sb("nw", [P, KC])
        hh = [sb(f"hh{u}", [P, 2, KC, SPAN], F32R) for u in range(2)]
        bt = [sb(f"bt{u}", [P, TS, D]) for u in range(2)]
        sg = [sb(f"sg{u}", [P, SPAN]) for u in range(2)]
        act_f = [sb(f"act{u}", [P, SPAN]) for u in range(2)]
        aT = [[sb(f"aT{u}{hf}", [P, SPAN], F32R) for hf in range(2)] for u in range(2)]
        ps_g = [ph.ps(f"ps_g{u}", [P, SPAN]) for u in range(2)]
        ps_u = [ph.ps(f"ps_u{u}", [P, SPAN]) for u in range(2)]
        acc = [ph.ps(f"acc{t}", [P, D]) for t in range(TS)]
        nw_in, w_high, w_low = sem("nw_in"), sem("w_high"), sem("w_low")
        w_in = [sem(f"w_in{u}") for u in range(2)]
        h_in = [sem(f"h_in{u}") for u in range(2)]
        b_in = [sem(f"b_in{u}") for u in range(2)]
        x_out = [sem(f"x_out{u}") for u in range(2)]
        gate_s, up_s, silu_s, act_s, high, low, down_s, added = (
            sem(n) for n in ("gate", "up", "silu", "act", "high", "low", "down", "added"))
        base_v = base.rearrange("(s t p) d -> s p t d", p=P, t=TS)
        out_v = out.rearrange("(s t p) d -> s p t d", p=P, t=TS)

        def spans(eng, body):
            for s in range(2):
                body(s, s)
            with eng.Fori(0, NSP // 2 - 1) as pair:
                for s in range(2):
                    body(pair * 2 + (s + 2), s)

        def of(v, s):
            return v[s] if isinstance(s, int) else v[bass.ds(s, 1)].rearrange("a p t d -> (a p) t d")

        with nc.Block() as block:
            @block.sync
            def _(sp):
                def load_h(s, u):
                    at = s * SPAN if isinstance(s, int) else sp.snap(s * SPAN)
                    src = h2T[:, :, :, at:at + SPAN] if isinstance(s, int) else h2T[:, :, :, bass.ds(at, SPAN)]
                    wait(sp, up_s, (s - 1) * NF)
                    sp.dma_start(hh[u][:].bitcast(F32), src).then_inc(h_in[u], 16)

                sp.dma_start(nw[:], norm_w.rearrange("(kc p) -> p kc", p=P), allow_slow_non_contiguous=True).then_inc(nw_in, 16)
                for f in range(NF):
                    if f == 1:
                        load_h(0, 0)
                    wait(sp, w_low, f - 1)
                    st = bt[f % 2]
                    cols = slice(f * P, (f + 1) * P)
                    for m, wm in enumerate((w_gate, w_up)):
                        sp.dma_start(st[:, m].rearrange("p (kc n) -> p kc n", kc=KC),
                                     wm[:, cols].rearrange("(kc p) n -> p kc n", p=P)).then_inc(w_in[f % 2], 16)
                    sp.dma_start(st[:, 2], w_down[f * P:(f + 1) * P, :]).then_inc(w_in[f % 2], 16)
                load_h(1, 1)
                sp.wait_ge(w_low, NF)

                def body(s, u, h_next):
                    row = s if isinstance(s, int) else sp.snap(s)
                    wait(sp, x_out[u], (s - u) * 8)
                    sp.dma_start(bt[u][:], of(base_v, row)).then_inc(b_in[u], 16)
                    if isinstance(s, int) and s == 0:
                        return
                    row = s - 1 if isinstance(s, int) else sp.snap(s - 1)
                    wait(sp, added, s)
                    sp.dma_start(of(out_v, row), bt[1 - u][:]).then_inc(x_out[1 - u], 16)
                    if h_next:
                        load_h(s + 1, 1 - u)
                for s in range(NSP):
                    body(s, s % 2, s < NSP - 1)
                sp.wait_ge(added, NSP)
                sp.dma_start(out_v[NSP - 1], bt[1][:]).then_inc(x_out[1], 16)
                for u in range(2):
                    sp.wait_ge(x_out[u], 16 * NSP // 2)

            @block.scalar
            def _(act):
                def take_high(f):
                    b = f % 2
                    act.wait_ge(w_in[b], 48 * (f // 2 + 1))
                    for m in range(2):
                        for kc in range(KC):
                            act.activation(wgu[m][0][:, f, kc], bt[b][:, m, kc * P:(kc + 1) * P], ACT.Copy,
                                           scale=nw[:, kc:kc + 1])
                    act.copy(wd[0][:, f], bt[b][:, 2]).then_inc(w_high, 1)

                act.preload_act_table_set("silu_and_others")
                act.wait_ge(nw_in, 16)
                take_high(0)

                def body(s, u):
                    for f in range(NF):
                        b = f % 2
                        g = s * NF + f
                        if isinstance(s, int) and s == 0 and f + 1 < NF:
                            take_high(f + 1)
                        wait(act, gate_s, g + 1)
                        wait(act, act_s, g if f == 0 else g - 1)
                        act.activation(sg[b][:], ps_g[b][:], ACT.Silu).then_inc(silu_s, 1)
                        wait(act, act_s, g + 1)
                        wait(act, down_s, g if f == 0 else g - 1)
                        act.copy(aT[b][0][:], act_f[b][:]).then_inc(high, 1)
                spans(act, body)

            @block.vector
            def _(dve):
                dve.wait_ge(nw_in, 16)

                def finish(s, u):
                    wait(dve, down_s, (s + 1) * NF)
                    wait(dve, b_in[u], (s - u) * 8 + 16)
                    for t in range(TS):
                        op = dve.tensor_tensor(bt[u][:, t], acc[t][:], bt[u][:, t], ALU.add)
                    op.then_inc(added, 1)

                def take_low(f):
                    b = f % 2
                    dve.wait_ge(w_in[b], 48 * (f // 2 + 1))
                    dve.wait_ge(w_high, f + 1)
                    for m in range(2):
                        for kc in range(KC):
                            dve.scalar_tensor_tensor(out=wgu[m][1][:, f, kc], in0=bt[b][:, m, kc * P:(kc + 1) * P],
                                                     scalar=nw[:, kc:kc + 1], in1=wgu[m][0][:, f, kc].bitcast(F32),
                                                     op0=ALU.mult, op1=ALU.subtract)
                    dve.tensor_tensor(wd[1][:, f], bt[b][:, 2], wd[0][:, f].bitcast(F32),
                                      ALU.subtract).then_inc(w_low, 1)

                take_low(0)

                def body(s, u):
                    for f in range(NF):
                        b = f % 2
                        g = s * NF + f
                        if isinstance(s, int) and s == 0 and f + 1 < NF:
                            take_low(f + 1)
                        wait(dve, silu_s, g + 1)
                        wait(dve, up_s, g + 1)
                        wait(dve, low, g if f == 0 else g - 1)
                        dve.tensor_tensor(act_f[b][:], ps_u[b][:], sg[b][:], ALU.mult).then_inc(act_s, 1)
                        wait(dve, high, g + 1)
                        dve.tensor_tensor(aT[b][1][:], act_f[b][:], aT[b][0][:].bitcast(F32), ALU.subtract).then_inc(low, 1)
                        if f == 0 and not (isinstance(s, int) and s == 0):
                            finish(s - 1, 1 - u)
                spans(dve, body)
                finish(NSP - 1, 1)

            @block.tensor
            def _(pe):
                def down(g, f, first, last):
                    wait(pe, low, g + 1)
                    for t in range(TS):
                        cols = slice(t * P, (t + 1) * P)
                        op = split_matmul(pe, acc[t][:], [aT[f % 2][hf][:, cols] for hf in range(2)],
                                          [wd[hf][:, f] for hf in range(2)], first, last)
                    op.then_inc(down_s, 1)

                def body(s, u):
                    wait(pe, h_in[u], (s - u) * 8 + 16)
                    for f in range(NF):
                        b = f % 2
                        g = s * NF + f
                        if isinstance(s, int) and s == 0:
                            pe.wait_ge(w_low, f + 1)
                        wait(pe, silu_s, g if f == 0 else g - 1)
                        for kc in range(KC):
                            op = split_matmul(pe, ps_g[b][:], [wgu[0][hf][:, f, kc] for hf in range(2)],
                                              [hh[u][:, hf, kc] for hf in range(2)], kc == 0, kc == KC - 1)
                        op.then_inc(gate_s, 1)
                        wait(pe, act_s, g if f == 0 else g - 1)
                        for kc in range(KC):
                            op = split_matmul(pe, ps_u[b][:], [wgu[1][hf][:, f, kc] for hf in range(2)],
                                              [hh[u][:, hf, kc] for hf in range(2)], kc == 0, kc == KC - 1)
                        op.then_inc(up_s, 1)
                        if f > 0:
                            if f == 1:
                                wait(pe, added, s)
                            down(g - 1, f - 1, f == 1, False)
                        elif not (isinstance(s, int) and s == 0):
                            down(g - 1, NF - 1, False, True)
                spans(pe, body)
                down(NSP * NF - 1, NF - 1, False, True)


def macaron(nc, x, norm1_w, wq, wk, wv, w1, w2, gk_b, wg, gnorm_w, wo, ffn_norm_w, w_gate, w_up, w_down,
            gate_w, W, atoms, eaw, importance, mask_idx, out):
    x = x.rearrange("b t d -> (b t) d")
    out = out.rearrange("b t d -> (b t) d")

    def dram(name, shape):
        return nc.dram_tensor(name, shape, F32).ap()

    table = dram("table", (PLACES + NS, E))
    m_store = dram("m_store", (P, KC, 2, E, D))
    dispatched = dram("dispatched", (E * REGION, D))
    routed = dram("routed", (BLOCKS * P, D))
    base = dram("base", (TOK, D))
    h2T = dram("h2T", (P, 2, KC, TOK))
    x3 = dram("x3", (TOK, D))
    with ExitStack() as ctx:
        def sb(name, shape, dt=F32):
            return ctx.enter_context(nc.sbuf_tensor(name, shape, dt))

        cst = constants(nc, sb)
        gate = sb("gate", [P, 2, NT])
        row_of = sb("row_of", [P, 2, NT], I32)
        tile_tab = sb("tile_tab", [1, 2, BLOCKS], I32)
        place_i = sb("place_i", [P, NB], I32)
        total = sb("total", [P, NB, E])
        sparse_places(nc, cst, atoms, eaw, importance, mask_idx, table, place_i, total)
        with nc.sbuf_tensor("M1", [P, KC, 2, E, D], F32R) as M:
            router(nc, cst, "r1", x, gate_w, gate, row_of, tile_tab, dispatched, M, sparse=(W, table, place_i, total))
            experts(nc, cst, "e1", M, tile_tab, dispatched, routed, m_store)
        w = dict(norm1_w=norm1_w, wq=wq, wk=wk, wv=wv, w1=w1, w2=w2, gk_b=gk_b, wg=wg, gnorm_w=gnorm_w, wo=wo)
        attention(nc, cst, x, routed, gate, row_of, w, base, h2T)
        swiglu(nc, h2T, ffn_norm_w, w_gate, w_up, w_down, base, x3)
        HELD = NT - E
        with nc.sbuf_tensor("M2", [P, KC, 2, E, D], F32R) as M:
            router(nc, cst, "r2", x3, gate_w, gate, row_of, tile_tab, dispatched, M, m_store=m_store)
            with nc.sbuf_tensor("held", [P, HELD, D], F32) as held:
                experts(nc, cst, "e2", M, tile_tab, dispatched, routed, ahead=(x3, held))
                combine(nc, "c2", x3, held, M, routed, gate, row_of, out)


_INS = ['L0_attn_x', 'L0_attn_norm1_w', 'L0_attn_wq', 'L0_attn_wk', 'L0_attn_wv', 'L0_attn_gk_w1', 'L0_attn_gk_w2',
        'L0_attn_gk_b', 'L0_attn_wg', 'L0_attn_gnorm_w', 'L0_attn_wo', 'L0_attn_ffn_norm_w', 'L0_attn_w_gate',
        'L0_attn_w_up', 'L0_attn_w_down', 'L0_ffn_gate_w', 'L0_ffn_W', 'L0_ffn_atoms', 'L0_ffn_expert_atom_weights',
        'L0_ffn_importance', 'L0_ffn_mask_idx']


def kernel(**inputs):
    import numpy as _np
    import concourse.bacc as _bacc
    from concourse.bass_utils import run_bass_kernel_spmd as _run

    nc = _bacc.Bacc("TRN2", target_bir_lowering=False, num_devices=1)
    arrays, args = {}, []
    for name in _INS:
        a = _np.ascontiguousarray(inputs[name])
        arrays[f"in_{name}_dram"] = a
        args.append(nc.dram_tensor(f"in_{name}_dram", a.shape, mybir.dt.from_np(a.dtype), kind="ExternalInput").ap())
    args.append(nc.dram_tensor("out_0_dram", (B, T, D), F32, kind="ExternalOutput").ap())
    macaron(nc, *args)
    r = _run(nc, [arrays], core_ids=[0])
    return r.results[0]["out_0_dram"]
```
